# Optimizing a Trainium2 kernel written in Bass

```python
import numpy as np
import jax
import jax.numpy as jnp

def _softmax(x, axis=-1):
    return jax.nn.softmax(x, axis=axis)

def _gelu(x):
    return jax.nn.gelu(x, approximate=True)

def _silu(x):
    return jax.nn.silu(x)

def _sigmoid(x):
    return jax.nn.sigmoid(x)

def _layernorm(x, axis=-1, eps=1e-05):
    m = jnp.mean(x, axis=axis, keepdims=True)
    v = jnp.var(x, axis=axis, keepdims=True)
    return (x - m) / jnp.sqrt(v + eps)

def _scatter_add(tgt, idx, src, axis=0):
    return tgt.at[idx].add(src)

def _segment_sum(src, seg, n):
    return jax.ops.segment_sum(src, seg, n)
kernel_name = 'mk_flamingo_gated_d2_seqx_r8_6de8d7'

def setup_inputs(seed: int=0):
    np.random.seed(seed)
    _w = jnp.asarray

    def _rec_inputs():
        import jax
        import jax.numpy as jnp
        _rk = jax.random.key(seed)
        x = 0.000341 + 1 * jax.random.normal(jax.random.fold_in(_rk, 1), (16, 128, 256), jnp.float32)
        _lenS = 128 - jax.random.randint(jax.random.fold_in(_rk, 7), (16,), 0, max(1, 128 // 4) + 1, jnp.int32)
        _lenS2 = 128 - jax.random.randint(jax.random.fold_in(_rk, 8), (16,), 0, max(1, 128 // 4) + 1, jnp.int32)
        _ctx_2048P = jax.random.normal(jax.random.fold_in(_rk, 11), (16, 16, 256), jnp.float32)
        _ctx_2048c = jax.random.dirichlet(jax.random.fold_in(_rk, 511), 0.3 * jnp.ones((16,), jnp.float32), (16, 128))
        _ctx_2048t = jnp.einsum('bsk,bkd->bsd', _ctx_2048c, _ctx_2048P)
        _ctx_2048t = _ctx_2048t * jax.lax.rsqrt(jnp.mean(jnp.square(_ctx_2048t)) + 1e-12) * 0.953939
        ctx_2048 = -1.47943e-05 + 1.00017 * (_ctx_2048t + 0.3 * jax.random.normal(jax.random.fold_in(_rk, 611), (16, 128, 256), jnp.float32))
        _validS = jnp.arange(128)[None, :] < _lenS[:, None]
        _validS2 = jnp.arange(128)[None, :] < _lenS2[:, None]
        _causal = jnp.tril(jnp.ones((128, 128), dtype=bool))
        mask_Bx1x2048_fk1 = jnp.where(jnp.ones((16, 1, 256), dtype=bool), 1.0, 0.0).astype(jnp.float32)
        _g = jax.random.normal(jax.random.fold_in(_rk, 9001), (2, 2), jnp.float32)
        _g = jnp.sign(_g) * jnp.maximum(jnp.abs(_g), 1.0) + (_g == 0) * 1.0
        g_xattn = _g[0]
        g_ffn = _g[1]
        return (x, ctx_2048, mask_Bx1x2048_fk1, g_xattn, g_ffn)
    x, ctx_2048, mask_Bx1x2048_fk1, g_xattn, g_ffn = _rec_inputs()

    def _L0_xattn_setup():
        import jax, jax.numpy as jnp
        import numpy as np

        def _wkv(time_decay, time_first, k, v):
            w = -jnp.exp(time_decay)
            u = time_first
            B, T, C = k.shape
            aa = jnp.zeros((B, C), dtype=k.dtype)
            bb = jnp.zeros((B, C), dtype=k.dtype)
            pp = jnp.full((B, C), -1e+38, dtype=k.dtype)

            def step(carry, kv_t):
                aa, bb, pp = carry
                kt, vt = kv_t
                ww = u + kt
                q = jnp.maximum(pp, ww)
                e1 = jnp.exp(pp - q)
                e2 = jnp.exp(ww - q)
                y_t = (e1 * aa + e2 * vt) / (e1 * bb + e2)
                ww2 = pp + w
                q2 = jnp.maximum(ww2, kt)
                e1b = jnp.exp(ww2 - q2)
                e2b = jnp.exp(kt - q2)
                new_carry = (e1b * aa + e2b * vt, e1b * bb + e2b, q2)
                return (new_carry, y_t)
            ks = jnp.transpose(k, (1, 0, 2))
            vs = jnp.transpose(v, (1, 0, 2))
            _, ys = jax.lax.scan(step, (aa, bb, pp), (ks, vs))
            return jnp.transpose(ys, (1, 0, 2))
        key = jax.random.key(seed)
        k1, k2, k3, k4 = jax.random.split(key, 4)
        B, T, C = (8, 128, 256)
        return {'batch_size': B, 'seq_len': T, 'embedding_dim': C, 'time_decay': jax.random.normal(k1, (C,), dtype=jnp.float32), 'time_first': jax.random.normal(k2, (C,), dtype=jnp.float32), 'k': jax.random.normal(k3, (B, T, C), dtype=jnp.float32), 'v': jax.random.normal(k4, (B, T, C), dtype=jnp.float32)}
    _L0_xattn_all = _L0_xattn_setup()
    _L0_xattn_in = {k: v for k, v in _L0_xattn_all.items() if k in ('time_decay', 'time_first')}
    del _L0_xattn_all

    def _L0_ffn_setup():
        import jax, jax.numpy as jnp
        import numpy as np
        HIDDEN = 256
        INTER = 704
        B, S = (2, 256)

        def _ternary(key, shape):
            return jax.random.randint(key, shape, -1, 2).astype(jnp.float32)
        key = jax.random.key(seed)
        ks = jax.random.split(key, 7)
        x = jax.random.normal(ks[0], (B, S, HIDDEN), dtype=jnp.float32)
        gate_w = _ternary(ks[1], (INTER, HIDDEN))
        up_w = _ternary(ks[2], (INTER, HIDDEN))
        down_w = _ternary(ks[3], (HIDDEN, INTER))
        gate_s = jax.random.uniform(ks[4], (INTER,), minval=0.01, maxval=0.1, dtype=jnp.float32)
        up_s = jax.random.uniform(ks[5], (INTER,), minval=0.01, maxval=0.1, dtype=jnp.float32)
        down_s = jax.random.uniform(ks[6], (HIDDEN,), minval=0.01, maxval=0.1, dtype=jnp.float32)
        return {'x': x, 'gate_w': gate_w, 'up_w': up_w, 'down_w': down_w, 'gate_s': gate_s, 'up_s': up_s, 'down_s': down_s}
    _L0_ffn_all = _L0_ffn_setup()
    _L0_ffn_in = {k: v for k, v in _L0_ffn_all.items() if k in ('gate_w', 'up_w', 'down_w', 'gate_s', 'up_s', 'down_s')}
    del _L0_ffn_all

    def _L1_xattn_setup():
        import math
        import jax, jax.numpy as jnp
        import numpy as np
        SIZE = 128
        HEADS = 16
        HEAD_DIM = SIZE // HEADS
        B, T, S = (2, 256, 256)
        NEG = 1000000.0
        key = jax.random.key(seed)
        ks = jax.random.split(key, 10)
        target = jax.random.normal(ks[0], (B, SIZE, T), dtype=jnp.float32)
        source = jax.random.normal(ks[1], (B, SIZE, S), dtype=jnp.float32)
        target_mask = (jax.random.uniform(ks[2], (B, 1, T)) > 0.1).astype(jnp.float32)
        source_mask = (jax.random.uniform(ks[3], (B, 1, S)) > 0.1).astype(jnp.float32)
        scale = 1.0 / math.sqrt(SIZE)
        Wq = jax.random.normal(ks[4], (SIZE, SIZE), dtype=jnp.float32) * scale
        Wk = jax.random.normal(ks[5], (SIZE, SIZE), dtype=jnp.float32) * scale
        Wv = jax.random.normal(ks[6], (SIZE, SIZE), dtype=jnp.float32) * scale
        bq = jax.random.normal(ks[7], (SIZE,), dtype=jnp.float32) * 0.01
        bk = jax.random.normal(ks[8], (SIZE,), dtype=jnp.float32) * 0.01
        bv = jax.random.normal(ks[9], (SIZE,), dtype=jnp.float32) * 0.01
        return {'target': target, 'source': source, 'target_mask': target_mask, 'source_mask': source_mask, 'Wq': Wq, 'bq': bq, 'Wk': Wk, 'bk': bk, 'Wv': Wv, 'bv': bv}
    _L1_xattn_all = _L1_xattn_setup()
    _L1_xattn_in = {k: v for k, v in _L1_xattn_all.items() if k in ('Wq', 'bq', 'Wk', 'bk', 'Wv', 'bv')}
    del _L1_xattn_all

    def _L1_ffn_setup():
        import jax, jax.numpy as jnp
        import numpy as np
        B, S, D = (4, 256, 256)
        E = 8
        H = 352
        CAP_F = 1.0

        def _moe(x, Wg, W1, W3, W2, sw1, sw3, sw2):
            b, sl, d = x.shape
            T = b * sl
            C = int(CAP_F * T / E)
            xt = x.reshape(T, d)
            probs = jax.nn.softmax(xt @ Wg, axis=-1)
            eidx = jnp.argmax(probs, axis=-1)
            gate = jnp.take_along_axis(probs, eidx[:, None], 1)[:, 0]
            oh = jax.nn.one_hot(eidx, E, dtype=jnp.int32)
            pos = (jnp.cumsum(oh, axis=0) * oh).sum(-1) - 1
            keep = pos < C
            flat = jnp.where(keep, eidx * C + pos, E * C)
            xd = jnp.zeros((E * C, d), x.dtype).at[flat].set(xt, mode='drop')
            xd = xd.reshape(E, C, d)
            h = jax.nn.silu(jnp.einsum('ecd,edh->ech', xd, W1)) * jnp.einsum('ecd,edh->ech', xd, W3)
            oe = jnp.einsum('ech,ehd->ecd', h, W2).reshape(E * C, d)
            out = jnp.take(oe, jnp.minimum(flat, E * C - 1), axis=0)
            out = out * (gate * keep.astype(x.dtype))[:, None]
            shared = jax.nn.silu(xt @ sw1) * (xt @ sw3) @ sw2
            return (out + shared).reshape(b, sl, d)
        key = jax.random.key(seed)
        ks = jax.random.split(key, 8)
        s = lambda fan: 1.0 / np.sqrt(fan)
        return {'x': jax.random.normal(ks[0], (B, S, D), jnp.float32), 'Wg': jax.random.normal(ks[1], (D, E), jnp.float32) * s(D), 'W1': jax.random.normal(ks[2], (E, D, H), jnp.float32) * s(D), 'W3': jax.random.normal(ks[3], (E, D, H), jnp.float32) * s(D), 'W2': jax.random.normal(ks[4], (E, H, D), jnp.float32) * s(H), 'sw1': jax.random.normal(ks[5], (D, H), jnp.float32) * s(D), 'sw3': jax.random.normal(ks[6], (D, H), jnp.float32) * s(D), 'sw2': jax.random.normal(ks[7], (H, D), jnp.float32) * s(H)}
    _L1_ffn_all = _L1_ffn_setup()
    _L1_ffn_in = {k: v for k, v in _L1_ffn_all.items() if k in ('Wg', 'W1', 'W3', 'W2', 'sw1', 'sw3', 'sw2')}
    del _L1_ffn_all
    return {'x': x, 'ctx_2048': ctx_2048, 'mask_Bx1x2048_fk1': mask_Bx1x2048_fk1, 'g_xattn': g_xattn, 'g_ffn': g_ffn, 'L0_xattn_time_decay': _L0_xattn_in['time_decay'], 'L0_xattn_time_first': _L0_xattn_in['time_first'], 'L0_ffn_gate_w': _L0_ffn_in['gate_w'], 'L0_ffn_up_w': _L0_ffn_in['up_w'], 'L0_ffn_down_w': _L0_ffn_in['down_w'], 'L0_ffn_gate_s': _L0_ffn_in['gate_s'], 'L0_ffn_up_s': _L0_ffn_in['up_s'], 'L0_ffn_down_s': _L0_ffn_in['down_s'], 'L1_xattn_Wq': _L1_xattn_in['Wq'], 'L1_xattn_bq': _L1_xattn_in['bq'], 'L1_xattn_Wk': _L1_xattn_in['Wk'], 'L1_xattn_bk': _L1_xattn_in['bk'], 'L1_xattn_Wv': _L1_xattn_in['Wv'], 'L1_xattn_bv': _L1_xattn_in['bv'], 'L1_ffn_Wg': _L1_ffn_in['Wg'], 'L1_ffn_W1': _L1_ffn_in['W1'], 'L1_ffn_W3': _L1_ffn_in['W3'], 'L1_ffn_W2': _L1_ffn_in['W2'], 'L1_ffn_sw1': _L1_ffn_in['sw1'], 'L1_ffn_sw3': _L1_ffn_in['sw3'], 'L1_ffn_sw2': _L1_ffn_in['sw2']}

def reference(x, ctx_2048, mask_Bx1x2048_fk1, g_xattn, g_ffn, L0_xattn_time_decay, L0_xattn_time_first, L0_ffn_gate_w, L0_ffn_up_w, L0_ffn_down_w, L0_ffn_gate_s, L0_ffn_up_s, L0_ffn_down_s, L1_xattn_Wq, L1_xattn_bq, L1_xattn_Wk, L1_xattn_bk, L1_xattn_Wv, L1_xattn_bv, L1_ffn_Wg, L1_ffn_W1, L1_ffn_W3, L1_ffn_W2, L1_ffn_sw1, L1_ffn_sw3, L1_ffn_sw2):
    import jax
    import jax.numpy as jnp

    def _L0_xattn_ref(batch_size, seq_len, embedding_dim, time_decay, time_first, k, v):
        import jax, jax.numpy as jnp
        import numpy as np

        def _wkv(time_decay, time_first, k, v):
            w = -jnp.exp(time_decay)
            u = time_first
            B, T, C = k.shape
            aa = jnp.zeros((B, C), dtype=k.dtype)
            bb = jnp.zeros((B, C), dtype=k.dtype)
            pp = jnp.full((B, C), -1e+38, dtype=k.dtype)

            def step(carry, kv_t):
                aa, bb, pp = carry
                kt, vt = kv_t
                ww = u + kt
                q = jnp.maximum(pp, ww)
                e1 = jnp.exp(pp - q)
                e2 = jnp.exp(ww - q)
                y_t = (e1 * aa + e2 * vt) / (e1 * bb + e2)
                ww2 = pp + w
                q2 = jnp.maximum(ww2, kt)
                e1b = jnp.exp(ww2 - q2)
                e2b = jnp.exp(kt - q2)
                new_carry = (e1b * aa + e2b * vt, e1b * bb + e2b, q2)
                return (new_carry, y_t)
            ks = jnp.transpose(k, (1, 0, 2))
            vs = jnp.transpose(v, (1, 0, 2))
            _, ys = jax.lax.scan(step, (aa, bb, pp), (ks, vs))
            return jnp.transpose(ys, (1, 0, 2))
        assert seq_len <= 128
        return _wkv(time_decay, time_first, k, v)

    def _L0_ffn_ref(x, gate_w, up_w, down_w, gate_s, up_s, down_s):
        import jax, jax.numpy as jnp
        import numpy as np
        HIDDEN = 256
        INTER = 704
        B, S = (2, 256)

        def _ternary(key, shape):
            return jax.random.randint(key, shape, -1, 2).astype(jnp.float32)
        b, s, h = x.shape
        xf = x.reshape(b * s, h)
        g = jnp.einsum('th,ih->ti', xf, gate_w) * gate_s
        u = jnp.einsum('th,ih->ti', xf, up_w) * up_s
        hdn = jax.nn.silu(g) * u
        out = jnp.einsum('ti,hi->th', hdn, down_w) * down_s
        return out.reshape(b, s, -1)

    def _L1_xattn_ref(target, source, target_mask, source_mask, Wq, bq, Wk, bk, Wv, bv):
        import math
        import jax, jax.numpy as jnp
        import numpy as np
        SIZE = 128
        HEADS = 16
        HEAD_DIM = SIZE // HEADS
        B, T, S = (2, 256, 256)
        NEG = 1000000.0
        b, _, t = target.shape
        s = source.shape[-1]
        q = jnp.einsum('oc,bct->bot', Wq, target) + bq[None, :, None]
        k = jnp.einsum('oc,bcs->bos', Wk, source) + bk[None, :, None]
        v = jnp.einsum('oc,bcs->bos', Wv, source) + bv[None, :, None]
        q = q.reshape(b, HEADS, HEAD_DIM, t)
        k = k.reshape(b, HEADS, HEAD_DIM, s)
        v = v.reshape(b, HEADS, HEAD_DIM, s)
        dot = jnp.einsum('bhdt,bhds->bhts', q, k) / math.sqrt(HEAD_DIM)
        mask = target_mask[:, :, :, None] * source_mask[:, :, None, :]
        dot = mask * dot - (1.0 - mask) * NEG
        amap = jax.nn.softmax(dot, axis=-1) * mask
        out = jnp.einsum('bhts,bhds->bhdt', amap, v)
        return out.reshape(b, HEADS * HEAD_DIM, t)

    def _L1_ffn_ref(x, Wg, W1, W3, W2, sw1, sw3, sw2):
        import jax, jax.numpy as jnp
        import numpy as np
        B, S, D = (4, 256, 256)
        E = 8
        H = 352
        CAP_F = 1.0

        def _moe(x, Wg, W1, W3, W2, sw1, sw3, sw2):
            b, sl, d = x.shape
            T = b * sl
            C = int(CAP_F * T / E)
            xt = x.reshape(T, d)
            probs = jax.nn.softmax(xt @ Wg, axis=-1)
            eidx = jnp.argmax(probs, axis=-1)
            gate = jnp.take_along_axis(probs, eidx[:, None], 1)[:, 0]
            oh = jax.nn.one_hot(eidx, E, dtype=jnp.int32)
            pos = (jnp.cumsum(oh, axis=0) * oh).sum(-1) - 1
            keep = pos < C
            flat = jnp.where(keep, eidx * C + pos, E * C)
            xd = jnp.zeros((E * C, d), x.dtype).at[flat].set(xt, mode='drop')
            xd = xd.reshape(E, C, d)
            h = jax.nn.silu(jnp.einsum('ecd,edh->ech', xd, W1)) * jnp.einsum('ecd,edh->ech', xd, W3)
            oe = jnp.einsum('ech,ehd->ecd', h, W2).reshape(E * C, d)
            out = jnp.take(oe, jnp.minimum(flat, E * C - 1), axis=0)
            out = out * (gate * keep.astype(x.dtype))[:, None]
            shared = jax.nn.silu(xt @ sw1) * (xt @ sw3) @ sw2
            return (out + shared).reshape(b, sl, d)
        return _moe(x, Wg, W1, W3, W2, sw1, sw3, sw2)
    x = x + jnp.tanh(g_xattn[0]) * _L0_xattn_ref(16, 128, 256, L0_xattn_time_decay, L0_xattn_time_first, _layernorm(x, axis=-1), ctx_2048)
    x = x + jnp.tanh(g_ffn[0]) * _L0_ffn_ref(_layernorm(x, axis=-1), L0_ffn_gate_w, L0_ffn_up_w, L0_ffn_down_w, L0_ffn_gate_s, L0_ffn_up_s, L0_ffn_down_s)
    x = x + jnp.tanh(g_xattn[1]) * _L1_xattn_ref(_layernorm(x, axis=-1), ctx_2048, mask_Bx1x2048_fk1, mask_Bx1x2048_fk1, L1_xattn_Wq, L1_xattn_bq, L1_xattn_Wk, L1_xattn_bk, L1_xattn_Wv, L1_xattn_bv)
    x = x + jnp.tanh(g_ffn[1]) * _L1_ffn_ref(_layernorm(x, axis=-1), L1_ffn_Wg, L1_ffn_W1, L1_ffn_W3, L1_ffn_W2, L1_ffn_sw1, L1_ffn_sw3, L1_ffn_sw2)
    return x

_drawn_inputs = setup_inputs


def setup_inputs(seed=0):
    import zlib

    import numpy as np

    out = dict(_drawn_inputs(seed))
    spreads = {'g_ffn': (-1.0, 0.2)}
    factors = {'L1_xattn_bq': 22.482, 'L1_xattn_bk': 64.0, 'L1_xattn_bv': 7.33}
    for name, (base, spread) in spreads.items():
        noise = np.random.default_rng([zlib.crc32(name.encode()), seed]).standard_normal(out[name].shape)
        drawn = base * np.exp(spread * noise) if base else spread * noise
        out[name] = jnp.asarray(drawn.astype(out[name].dtype))
    for name, factor in factors.items():
        out[name] = (out[name] * factor).astype(out[name].dtype)
    return out
```

```python
from contextlib import ExitStack

import concourse.bass as bass
from concourse import mybir

fp32 = mybir.dt.float32
bf16 = mybir.dt.bfloat16
u32 = mybir.dt.uint32
ALU = mybir.AluOpType
ACT = mybir.ActivationFunctionType
AX = mybir.AxisListType

P = 128
B, C = 16, 256
NG, GB = 4, 4
GT = GB * P
INTER = 704
NI = -(-INTER // P)
HEADS, HD = 16, 8
T = 256
NE, EH = 8, 352
NH = -(-EH // P)
CAP = B * P // NE
SLOTS = NE * CAP
NEG = 1000000.0
EPS = 1e-5
MASK_Q, MASK_K, ONES = 48, 48, 54
STACK = 60
Q_PART = (0, 0, 0, 1, 1, 2)
K_PART = (0, 1, 2, 0, 1, 0)


def width(i, n):
    return min(P, n - i * P)


class Chain:

    def __init__(self, eng, sem, start=0):
        self.eng, self.sem, self.start, self.n = eng, sem, start, 0

    def do(self, ins):
        ins.then_inc(self.sem, 1)
        self.n += 1
        return self.n

    def wait(self, n=None):
        self.eng.wait_ge(self.sem, self.start + (self.n if n is None else n))


def flamingo_kernel(nc, x, ctx, mask, g_xattn, g_ffn, time_decay, time_first, gate_wT, up_wT, down_wT,
                    gate_s, up_s, down_s, wqT, bq, wkT, bk, wvT, bv, Wg, W1, W3, W2, sw1, sw3, sw2, out,
                    stop_after=9):
    stack_scr = nc.dram_tensor("stack_scr", [2, 3, P, 2 * T], bf16).ap()
    max_scr = nc.dram_tensor("max_scr", [2, 3, 2 * HEADS, P], bf16).ap()
    qrow_scr = nc.dram_tensor("qrow_scr", [B, 12, T], bf16).ap()
    krow_scr = nc.dram_tensor("krow_scr", [B, 12, T], bf16).ap()
    dispatched = nc.dram_tensor("dispatched", [SLOTS + B * P, C], fp32).ap()
    expert_out = nc.dram_tensor("expert_out", [SLOTS, C], fp32).ap()
    xt = x.rearrange("b p c -> p b c")
    ct = ctx.rearrange("b p c -> p b c")
    ot = out.rearrange("b p c -> p b c")

    with ExitStack() as keep:
        def sb(name, shape, dt=fp32, where=keep):
            return where.enter_context(nc.sbuf_tensor(name, shape, dt))

        def sem(name, where=keep):
            return where.enter_context(nc.semaphore(name))

        psum = keep.enter_context(nc.psum_tensor("psum", [P, 8 * 512], fp32))
        bank = [psum[:, i * 512:(i + 1) * 512] for i in range(8)]
        X = sb("X", [P, B, C])
        ident = sb("ident", [P, P])
        tg = sb("tg", [P, 4])
        neghalf = sb("neghalf", [P, GB])
        stats = sb("stats", [P, GB, 6])
        mv = sb("mv", [P, GB, 2])
        veps = sb("veps", [P, GB])
        rstd = sb("rstd", [P, GB])
        wsh1 = sb("wsh1", [P, 2, EH])
        wsh3 = sb("wsh3", [P, 2, EH])
        wsh2 = sb("wsh2", [P, NH, C])
        wgt = sb("wgt", [P, 2, NE])
        wq = sb("wq", [P, P])
        wk = sb("wk", [P, P])
        wv = sb("wv", [P, P])
        bqk = sb("bqk", [P, 2])
        bvb = sb("bvb", [P, P])
        maskT = sb("maskT", [P, 2, B])
        zeros = sb("zeros", [P, 2 * C])
        s_late = sem("s_late")
        s_alone = {e: sem(f"s_alone_{e}") for e in ("sp", "dve", "pe")}

        def alone(eng):
            eng.sem_inc(s_alone[{nc.sync: "sp", nc.vector: "dve", nc.tensor: "pe"}[eng]], 1)

        def layer_norm_steps(ch, src, dst, n, s_var, s_rstd, nth):
            for i in range(n):
                last = ch.do(ch.eng.bn_stats(stats[:, i, :], src(i)))
            ch.wait(last)
            alone(ch.eng)
            for i in range(n):
                last = ch.eng.bn_aggr(mv[:, i, :], stats[:, i, :])
                if i < n - 1:
                    ch.do(last)
            ch.do(last)
            ch.wait()
            ch.eng.tensor_scalar(veps[:, 0:n], mv[:, 0:n, 1], EPS, None, ALU.add).then_inc(s_var, 1)
            ch.eng.wait_ge(s_rstd, nth)
            for i in range(n):
                last = ch.eng.tensor_scalar(dst(i), src(i), mv[:, i, 0:1], rstd[:, i:i + 1],
                                            ALU.subtract, ALU.mult)
                if i < n - 1:
                    ch.do(last)
            return last

        LN_STEPS = lambda n: n + n + n - 1

        def power_step(eng, n, s_var, s_rstd, nth):
            eng.wait_ge(s_var, nth)
            eng.tensor_tensor(rstd[:, 0:n], veps[:, 0:n], neghalf[:, 0:n], ALU.pow).then_inc(s_rstd, 1)

        with ExitStack() as part:
            def sbp(name, shape, dt=fp32):
                return sb(name, shape, dt, part)

            def semp(name):
                return sem(name, part)

            at_one = []

            def primed(name):
                at_one.append(semp(name))
                return at_one[-1]

            CV = sbp("CV", [P, GB, C])
            gw = sbp("gw", [P, 2, INTER])
            uw = sbp("uw", [P, 2, INTER])
            dw = sbp("dw", [P, NI, C])
            dsb = sbp("dsb", [P, C])
            gs = sbp("gs", [P, NI])
            us = sbp("us", [P, NI])
            hgs = sbp("hgs", [P, NI])
            hgu = sbp("hgu", [P, NI])
            gates = sbp("gates", [P, 4])
            td = sbp("td", [P, 2])
            tf = sbp("tf", [P, 2])
            tdx = sbp("tdx", [P, 2])
            decay = sbp("decay", [P, 2])
            upos = sbp("upos", [P, 2])
            uneg = sbp("uneg", [P, 2])
            steps01 = sbp("steps01", [P, GB, P])
            DEC = sbp("DEC", [P, 2, GT])
            mrow = sbp("mrow", [B, T])
            mtmp = sbp("mtmp", [B, 3, T])
            mq = sbp("mq", [B, 12, T], bf16)
            mk = sbp("mk", [B, 12, T], bf16)
            mparts = sbp("mparts", [B, 3, 3, T], bf16)
            Z1 = sbp("Z1", [P, GB, C])
            Z2 = sbp("Z2", [P, GB, C])
            EA = sbp("EA", [P, 2, GB, P])
            EB = sbp("EB", [P, 2, GB, P])
            PA = sbp("PA", [P, 2, GB, P])
            PB = sbp("PB", [P, 2, GB, P])
            SA = sbp("SA", [P, 2, GT])
            SB = sbp("SB", [P, 2, GT])
            NUM = sbp("NUM", [P, 2, GT])
            DEN = sbp("DEN", [P, 2, GT])
            Y = sbp("Y", [P, 2, GT])
            ZT = sbp("ZT", [P, 2, GT])
            TH = sbp("TH", [P, 2, GT])
            H1 = sbp("H1", [P, 2, GT])
            H = sbp("H", [P, NI, GT])

            s_ld = semp("s_ld")
            s_wts = semp("s_wts")
            s_x = semp("s_x")
            s_pool0 = semp("s_pool0")
            s_id = semp("s_id")
            s_act0 = semp("s_act0")
            s_dv0 = semp("s_dv0")
            s_mT = semp("s_mT")
            s_mT2 = semp("s_mT2")
            s_mrows = semp("s_mrows")
            s_mst = semp("s_mst")
            s_dvech = semp("s_dvech")
            s_var1 = semp("s_var1")
            s_rstd1 = semp("s_rstd1")
            s_z1 = semp("s_z1")
            s_kT = semp("s_kT")
            s_vT = primed("s_vT")
            s_exp = semp("s_exp")
            s_pab = semp("s_pab")
            s_scan = semp("s_scan")
            s_den = semp("s_den")
            s_num = semp("s_num")
            s_rec = semp("s_rec")
            s_y = semp("s_y")
            s_yT = semp("s_yT")
            s_x1 = semp("s_x1")
            s_z2 = semp("s_z2")
            s_z2T = semp("s_z2T")
            s_zt = semp("s_zt")
            s_gu = semp("s_gu")
            s_th = semp("s_th")
            s_h = primed("s_h")
            s_dn = primed("s_dn")
            s_x2 = primed("s_x2")

            WB = [bank[4], bank[5]]
            DB = [bank[6], bank[7]]

            def pe_wkv_in(pe, g, h):
                n = 2 * g + h
                if h == 0:
                    pe.wait_ge(s_z1, g + 1)
                    pe.wait_ge(s_x, 32 * (g + 1))
                    pe.wait_ge(s_x1, 2 * g)
                pe.wait_ge(s_exp, 2 * n)
                for b in range(GB):
                    last = pe.transpose(WB[0][:, b * P:(b + 1) * P], Z1[:, b, h * P:(h + 1) * P], ident[:])
                last.then_inc(s_kT, 1)
                pe.wait_ge(s_pab, 2 * n)
                for b in range(GB):
                    last = pe.transpose(WB[1][:, b * P:(b + 1) * P], CV[:, b, h * P:(h + 1) * P], ident[:])
                last.then_inc(s_vT, 1)

            def act_exps(act, g, h):
                act.wait_ge(s_kT, 2 * g + h + 1)
                act.wait_ge(s_y, 2 * g)
                kT = WB[0][:, :].rearrange("p (b t) -> p b t", b=GB)
                act.activation(EB[:, h, :, 1:P], kT[:, :, 1:P], ACT.Exp, bias=uneg[:, h:h + 1]).then_inc(s_exp, 1)
                act.activation(EA[:, h, :, 1:P], kT[:, :, 0:P - 1], ACT.Exp, bias=upos[:, h:h + 1]).then_inc(s_exp, 1)

            def dve_products(dve, g, h):
                n = 2 * g + h
                vT = WB[1][:, :].rearrange("p (b t) -> p b t", b=GB)
                dve.wait_ge(s_vT, 1 + n + 1)
                dve.wait_ge(s_exp, 2 * n + 2)
                dve.wait_ge(s_y, 2 * g)
                dve.tensor_tensor(PA[:, h, :, 1:P], EA[:, h, :, 1:P], vT[:, :, 0:P - 1], ALU.mult).then_inc(s_pab, 1)
                dve.tensor_tensor(PB[:, h, :, :], EB[:, h, :, :], vT, ALU.mult).then_inc(s_pab, 1)

            def dve_scans(dve, g, h):
                n = 2 * g + h
                flat = lambda t: t[:, h, :, :].rearrange("p b t -> p (b t)")
                dve.tensor_tensor_scan(out=SB[:, h, :], data0=DEC[:, h, :], data1=flat(EA), initial=0.0,
                                       op0=ALU.mult, op1=ALU.add).then_inc(s_scan, 1)
                dve.wait_ge(s_pab, 2 * n + 1)
                dve.tensor_tensor_scan(out=SA[:, h, :], data0=DEC[:, h, :], data1=flat(PA), initial=0.0,
                                       op0=ALU.mult, op1=ALU.add).then_inc(s_scan, 1)

            def pool_sums(pool, g, h):
                n = 2 * g + h
                flat = lambda t: t[:, h, :, :].rearrange("p b t -> p (b t)")
                pool.wait_ge(s_scan, 2 * n + 1)
                pool.tensor_tensor(DEN[:, h, :], SB[:, h, :], flat(EB), ALU.add).then_inc(s_den, 1)
                pool.wait_ge(s_scan, 2 * n + 2)
                pool.tensor_tensor(NUM[:, h, :], SA[:, h, :], flat(PB), ALU.add).then_inc(s_num, 1)

            def dve_recip(dve, g, h):
                dve.wait_ge(s_den, 2 * g + h + 1)
                dve.reciprocal(DEN[:, h, :], DEN[:, h, :]).then_inc(s_rec, 1)

            def pool_quot(pool, g, h):
                n = 2 * g + h
                pool.wait_ge(s_rec, n + 1)
                pool.wait_ge(s_num, n + 1)
                pool.wait_ge(s_yT, 2 * g)
                pool.tensor_tensor(Y[:, h, :], NUM[:, h, :], DEN[:, h, :], ALU.mult).then_inc(s_y, 1)

            def pe_wkv_out(pe, g):
                pe.wait_ge(s_y, 2 * g + 2)
                for k in range(2):
                    for b in range(2):
                        for h in range(2):
                            i = 2 * k + b
                            last = pe.transpose(WB[k][:, b * C + h * P:b * C + (h + 1) * P],
                                                Y[:, h, i * P:(i + 1) * P], ident[:])
                    last.then_inc(s_yT, 1)

            def dve_x1(dve, g):
                for k in range(2):
                    dve.wait_ge(s_yT, 2 * g + k + 1)
                    xs = X[:, bass.ds(GB * g + 2 * k, 2), :].rearrange("p b c -> p (b c)")
                    dve.scalar_tensor_tensor(out=xs, in0=WB[k][:, :], scalar=tg[:, 0:1], in1=xs,
                                             op0=ALU.mult, op1=ALU.add).then_inc(s_x1, 1)

            CH1 = 2 * LN_STEPS(GB) + NI
            xt_tile = lambda g: (lambda i: X[:, bass.ds(GB * g + i, 1), :].rearrange("p b c -> p (b c)"))

            def dve_ln1(dve, ch, g):
                dve.wait_ge(s_x, 32 * (g + 1))
                dve.wait_ge(s_kT, 2 * g)
                layer_norm_steps(ch, xt_tile(g), lambda i: Z1[:, i, :], GB, s_var1, s_rstd1, 2 * g + 1)\
                    .then_inc(s_z1, 1)

            def dve_ln2(dve, ch, g):
                dve.wait_ge(s_x1, 2 * g + 2)
                dve.wait_ge(s_z2T, 2 * g)
                alone(dve)
                layer_norm_steps(ch, xt_tile(g), lambda i: Z2[:, i, :], GB, s_var1, s_rstd1, 2 * g + 2)\
                    .then_inc(s_z2, 1)

            def pe_z2T(pe, g):
                pe.wait_ge(s_z2, g + 1)
                pe.wait_ge(s_h, 1 + NI * g)
                for h in range(2):
                    for b in range(GB):
                        last = pe.transpose(bank[h][:, b * P:(b + 1) * P], Z2[:, b, h * P:(h + 1) * P], ident[:])
                    last.then_inc(s_z2T, 1)

            def act_zt(act, g):
                for h in range(2):
                    act.wait_ge(s_z2T, 2 * g + h + 1)
                    act.activation(ZT[:, h, :], bank[h][:, :], ACT.Copy).then_inc(s_zt, 1)

            def pe_gu(pe, g, i):
                m = width(i, INTER)
                if i == 0:
                    pe.wait_ge(s_zt, 2 * g + 2)
                if i >= 2:
                    pe.wait_ge(s_h, 1 + NI * g + i - 1)
                for w, bk in ((gw, bank[2 * (i % 2)]), (uw, bank[2 * (i % 2) + 1])):
                    for h in range(2):
                        last = pe.matmul(bk[0:m, :], w[:, h, i * P:i * P + m], ZT[:, h, :],
                                         start=(h == 0), stop=(h == 1))
                last.then_inc(s_gu, 1)

            def act_tanh(act, g, i):
                m = width(i, INTER)
                act.wait_ge(s_gu, NI * g + i + 1)
                act.activation(TH[0:m, i % 2, :], bank[2 * (i % 2)][0:m, :], ACT.Tanh,
                               scale=hgs[0:m, i:i + 1]).then_inc(s_th, 1)

            def dve_h1(dve, ch, g, i):
                m = width(i, INTER)
                dve.wait_ge(s_th, NI * g + i + 1)
                ch.do(dve.scalar_tensor_tensor(out=H1[0:m, i % 2, :], in0=TH[0:m, i % 2, :], scalar=1.0,
                                               in1=bank[2 * (i % 2)][0:m, :], op0=ALU.add, op1=ALU.mult))

            def dve_h(dve, ch, g, i):
                m = width(i, INTER)
                if i == 0:
                    dve.wait_ge(s_dn, 1 + 2 * g)
                ch.wait()
                dve.scalar_tensor_tensor(out=H[0:m, i, :], in0=H1[0:m, i % 2, :], scalar=hgu[0:m, i:i + 1],
                                         in1=bank[2 * (i % 2) + 1][0:m, :], op0=ALU.mult,
                                         op1=ALU.mult).then_inc(s_h, 1)

            def pe_down(pe, g):
                pe.wait_ge(s_h, 1 + NI * g + NI)
                pe.wait_ge(s_x2, 1 + 2 * g)
                for k in range(2):
                    for b in range(2):
                        for i in range(NI):
                            m = width(i, INTER)
                            t = 2 * k + b
                            last = pe.matmul(DB[k][:, b * C:(b + 1) * C], H[0:m, i, t * P:(t + 1) * P],
                                             dw[0:m, i, :], start=(i == 0), stop=(i == NI - 1))
                    last.then_inc(s_dn, 1)

            def dve_x2(dve, g):
                for k in range(2):
                    dve.wait_ge(s_dn, 1 + 2 * g + k + 1)
                    xs = X[:, bass.ds(GB * g + 2 * k, 2), :].rearrange("p b c -> p (b c)")
                    dve.scalar_tensor_tensor(out=xs, in0=DB[k][:, :], scalar=tg[:, 2:3], in1=xs,
                                             op0=ALU.mult, op1=ALU.add).then_inc(s_x2, 1)

            N_SMALL = 14
            with nc.Block() as block:
                @block.sync
                def _(sp):
                    for primed_sem in at_one:
                        sp.sem_inc(primed_sem, 1)
                    small = [(gates[:, 0:2], g_xattn.partition_broadcast(P)), (gates[:, 2:4], g_ffn.partition_broadcast(P)),
                             (td[:], time_decay), (tf[:], time_first),
                             (dsb[:], down_s.partition_broadcast(P)), (bvb[:], bv.partition_broadcast(P)),
                             (bqk[:, 0:1], bq), (bqk[:, 1:2], bk), (mrow[:], mask),
                             (gs[:, 0:NI - 1], gate_s[0:(NI - 1) * P].rearrange("(i p) -> p i", p=P)),
                             (us[:, 0:NI - 1], up_s[0:(NI - 1) * P].rearrange("(i p) -> p i", p=P)),
                             (gs[0:width(NI - 1, INTER), NI - 1:NI],
                              gate_s[(NI - 1) * P:INTER].rearrange("(p a) -> p a", a=1)),
                             (us[0:width(NI - 1, INTER), NI - 1:NI],
                              up_s[(NI - 1) * P:INTER].rearrange("(p a) -> p a", a=1)),
                             (wq[:], wqT)]
                    assert len(small) == N_SMALL
                    with nc.allow_non_contiguous_dma(reason="small vectors"):
                        for dst, src in small:
                            sp.dma_start(dst, src).then_inc(s_ld, 16)
                    with sp.Fori(0, NG) as g:
                        sp.wait_ge(s_vT, 1 + 2 * g)
                        sp.dma_start(X[:, bass.ds(GB * g, GB), :], xt[:, bass.ds(GB * g, GB), :]).then_inc(s_x, 16)
                        sp.dma_start(CV[:, :, :], ct[:, bass.ds(GB * g, GB), :]).then_inc(s_x, 16)

                @block.scalar
                def _(act):
                    act.dma_start(gw[:, :, :], gate_wT.rearrange("(h p) i -> p h i", p=P)).then_inc(s_wts, 16)
                    act.dma_start(uw[:, :, :], up_wT.rearrange("(h p) i -> p h i", p=P)).then_inc(s_wts, 16)
                    n5 = (NI - 1) * P
                    act.dma_start(dw[:, 0:NI - 1, :], down_wT[0:n5, :].rearrange("(i p) c -> p i c", p=P)).then_inc(s_wts, 16)
                    act.dma_start(dw[0:INTER - n5, NI - 1, :], down_wT[n5:INTER, :]).then_inc(s_wts, 16)
                    for dst, src in ((wk[:], wkT), (wv[:], wvT),
                                     (wgt[:, :, :], Wg.rearrange("(h p) e -> p h e", p=P)),
                                     (wsh1[:, :, :], sw1.rearrange("(h p) e -> p h e", p=P)),
                                     (wsh3[:, :, :], sw3.rearrange("(h p) e -> p h e", p=P)),
                                     (wsh2[:, 0:2, :], sw2[0:2 * P, :].rearrange("(i p) c -> p i c", p=P)),
                                     (wsh2[0:EH - 2 * P, 2, :], sw2[2 * P:EH, :])):
                        act.dma_start(dst, src).then_inc(s_late, 16)
                    act.wait_ge(s_ld, 16 * N_SMALL)
                    act.activation(tg[:], gates[:], ACT.Tanh).then_inc(s_act0, 1)
                    act.activation(tdx[:], td[:], ACT.Exp).then_inc(s_act0, 1)
                    act.wait_ge(s_act0, 2)
                    act.activation(decay[:], tdx[:], ACT.Exp, scale=-1.0).then_inc(s_act0, 1)
                    act.wait_ge(s_dv0, 2)
                    act.wait_ge(s_pool0, 5)
                    act_exps(act, 0, 0)
                    act_exps(act, 0, 1)
                    act.wait_ge(s_dv0, 4)
                    with act.Fori(0, NG - 1) as g:
                        act_zt(act, g)
                        for i in range(NI):
                            act_tanh(act, g, i)
                            if i in (0, 2):
                                act_exps(act, g + 1, i // 2)
                    act_zt(act, NG - 1)
                    for i in range(NI):
                        act_tanh(act, NG - 1, i)

                @block.gpsimd
                def _(pool):
                    pool.memset(neghalf[:], -0.5).then_inc(s_pool0, 1)
                    pool.memset(ident[:], 0.0).then_inc(s_pool0, 1)
                    pool.memset(EA[:, :, :, 0:1], 0.0).then_inc(s_pool0, 1)
                    pool.memset(EB[:, :, :, 0:1], 1.0).then_inc(s_pool0, 1)
                    pool.memset(PA[:, :, :, 0:1], 0.0).then_inc(s_pool0, 1)
                    pool.memset(steps01[:, :, 0:1], 0.0).then_inc(s_pool0, 1)
                    pool.memset(steps01[:, :, 1:P], 1.0).then_inc(s_pool0, 1)
                    pool.memset(zeros[:], 0.0).then_inc(s_pool0, 1)
                    pool.wait_ge(s_pool0, 8)
                    pool.affine_select(out=ident[:], in_=ident[:], compare_op=ALU.not_equal, fill=1.0, base=0,
                                       pattern=[[-1, P]], channel_multiplier=1).then_inc(s_id, 1)
                    power_step(pool, GB, s_var1, s_rstd1, 1)
                    for h in range(2):
                        pool_sums(pool, 0, h)
                        pool_quot(pool, 0, h)
                    power_step(pool, GB, s_var1, s_rstd1, 2)
                    with pool.Fori(0, NG - 1) as g:
                        power_step(pool, GB, s_var1, s_rstd1, 2 * g + 3)
                        for h in range(2):
                            pool_sums(pool, g + 1, h)
                            pool_quot(pool, g + 1, h)
                        power_step(pool, GB, s_var1, s_rstd1, 2 * g + 4)

                @block.tensor
                def _(pe):
                    pe.wait_ge(s_id, 1)
                    pe.wait_ge(s_ld, 16 * N_SMALL)
                    for h in range(2):
                        last = pe.transpose(bank[7][:, h * B:(h + 1) * B], mrow[:, h * P:(h + 1) * P], ident[0:B, 0:B])
                    last.then_inc(s_mT, 1)
                    for h in range(2):
                        pe_wkv_in(pe, 0, h)
                    pe_wkv_out(pe, 0)
                    pe.wait_ge(s_wts, 64)
                    pe.wait_ge(s_dv0, 6)
                    pe.wait_ge(s_mT2, 1)
                    with pe.Fori(0, NG - 1) as g:
                        pe_z2T(pe, g)
                        for i in range(NI):
                            pe_gu(pe, g, i)
                            if i in (0, 2):
                                pe_wkv_in(pe, g + 1, i // 2)
                        pe_down(pe, g)
                        pe_wkv_out(pe, g + 1)
                    pe_z2T(pe, NG - 1)
                    for i in range(NI):
                        pe_gu(pe, NG - 1, i)
                    pe_down(pe, NG - 1)

                @block.vector
                def _(dve):
                    dve.wait_ge(s_ld, 16 * N_SMALL)
                    dve.tensor_scalar(upos[:], tf[:], 0.0, -1.0, ALU.max, ALU.mult).then_inc(s_dv0, 1)
                    dve.tensor_scalar(uneg[:], tf[:], 0.0, None, ALU.min).then_inc(s_dv0, 1)
                    m = width(NI - 1, INTER)
                    for lo, hi, q in ((0, NI - 1, P), (NI - 1, NI, m)):
                        dve.tensor_scalar(hgs[0:q, lo:hi], gs[0:q, lo:hi], 0.5, None, ALU.mult).then_inc(s_dv0, 1)
                    dve.wait_ge(s_dv0, 4)
                    for lo, hi, q in ((0, NI - 1, P), (NI - 1, NI, m)):
                        dve.tensor_tensor(hgu[0:q, lo:hi], hgs[0:q, lo:hi], us[0:q, lo:hi], ALU.mult).then_inc(s_dvech, 1)
                    dve.wait_ge(s_act0, 3)
                    dve.wait_ge(s_pool0, 8)
                    for h in range(2):
                        dve.tensor_scalar(DEC[:, h, :], steps01[:, :, :].rearrange("p b t -> p (b t)"),
                                          decay[:, h:h + 1], None, ALU.mult).then_inc(s_dvech, 1)
                    ch = Chain(dve, s_dvech, 4)
                    dve_ln1(dve, ch, 0)
                    dve.wait_ge(s_dvech, 4)
                    for h in range(2):
                        dve_products(dve, 0, h)
                        dve_scans(dve, 0, h)
                    for h in range(2):
                        dve_recip(dve, 0, h)
                    mch = ch
                    for j, (mul, add) in enumerate(((-NEG, 0.0), (NEG, -NEG), (-1.0, 1.0))):
                        mch.do(dve.tensor_scalar(mtmp[:, j, :], mrow[:], mul, add, ALU.mult, ALU.add))
                    for r in range(3):
                        mch.wait()
                        mch.do(dve.tensor_copy(mparts[:, :, r, :], mtmp[:, :, :]))
                        if r < 2:
                            mch.wait()
                            mch.do(dve.tensor_tensor(mtmp[:, :, :], mtmp[:, :, :], mparts[:, :, r, :], ALU.subtract))
                    mch.wait()
                    for r in range(6):
                        mch.do(dve.tensor_copy(mq[:, r, :], mparts[:, 0, Q_PART[r], :]))
                        mch.do(dve.tensor_copy(mk[:, r, :], mparts[:, 2, K_PART[r], :]))
                    mch.do(dve.tensor_copy(mq[:, 6:9, :], mparts[:, 1, :, :]))
                    mch.do(dve.memset(mq[:, 9:12, :], 0.0))
                    mch.do(dve.memset(mk[:, 6:12, :], 1.0))
                    mch.wait()
                    dve.wait_ge(s_mT, 1)
                    dve.tensor_copy(maskT[:, :, :].rearrange("p h b -> p (h b)"), bank[7][:, 0:2 * B]).then_inc(s_mT2, 1)
                    dve.wait_ge(s_wts, 64)
                    dve.tensor_tensor(dw[:, 0:NI - 1, :], dw[:, 0:NI - 1, :],
                                      dsb[:, :].unsqueeze(1).broadcast_to([P, NI - 1, C]), ALU.mult).then_inc(s_dv0, 1)
                    dve.tensor_tensor(dw[0:m, NI - 1, :], dw[0:m, NI - 1, :], dsb[0:m, :], ALU.mult).then_inc(s_dv0, 1)
                    dve.wait_ge(s_ld, 16 * N_SMALL)
                    mch.do(dve.tensor_scalar(wq[:], wq[:], HD ** -0.5, None, ALU.mult))
                    mch.do(dve.tensor_scalar(bqk[:, 0:1], bqk[:, 0:1], HD ** -0.5, None, ALU.mult))
                    dve_x1(dve, 0)
                    dve_ln2(dve, ch, 0)
                    before = 4 + ch.n
                    with dve.Fori(0, NG - 1) as g:
                        ch = Chain(dve, s_dvech, before + CH1 * g)
                        dve_ln1(dve, ch, g + 1)
                        for i in range(NI):
                            dve_h1(dve, ch, g, i)
                            dve_h(dve, ch, g, i)
                            if i in (1, 3):
                                dve_products(dve, g + 1, i // 2)
                                dve_scans(dve, g + 1, i // 2)
                            if i in (2, 4):
                                dve_recip(dve, g + 1, i // 2 - 1)
                        dve_x2(dve, g)
                        dve_x1(dve, g + 1)
                        dve_ln2(dve, ch, g + 1)
                        assert ch.n == CH1
                    ch = Chain(dve, s_dvech, before + CH1 * (NG - 1))
                    for i in range(NI):
                        dve_h1(dve, ch, NG - 1, i)
                        dve_h(dve, ch, NG - 1, i)
                    dve_x2(dve, NG - 1)
                    dve.wait_ge(s_x2, 1 + 2 * NG)

            with nc.Block() as block:
                @block.sync
                def _(sp):
                    sp.dma_start(qrow_scr, mq[:, :, :]).then_inc(s_mst, 16)
                    sp.dma_start(krow_scr, mk[:, :, :]).then_inc(s_mst, 16)
                    dz = dispatched[0:SLOTS, :].rearrange("(p a b) c -> a p (b c)", p=P, b=2)
                    for a in range(SLOTS // P // 2):
                        sp.dma_start(dz[a], zeros[:, :]).then_inc(s_mst, 16)
                    sp.wait_ge(s_mst, 16 * (2 + SLOTS // P // 2))

                @block.scalar
                def _(act):
                    act.wait_ge(s_late, 16 * 7)

        def store_x():
            with nc.Block() as block:
                @block.sync
                def _(sp):
                    with ExitStack() as st:
                        s_o = sem("s_store", st)
                        sp.dma_start(ot, X[:, :, :]).then_inc(s_o, 16)
                        sp.wait_ge(s_o, 16)

        if stop_after == 1:
            store_x()
            return
        with ExitStack() as part:
            def sbp(name, shape, dt=fp32):
                return sb(name, shape, dt, part)

            def semp(name):
                return sem(name, part)

            at_one = []

            def primed(name):
                at_one.append(semp(name))
                return at_one[-1]

            NS = GB
            QA = sbp("QA", [P, NS, HEADS, T], bf16)
            KA = sbp("KA", [P, NS, HEADS, T], bf16)
            VP = sbp("VP", [P, NS, 2, HEADS, 32])
            CX = sbp("CX", [P, NS, T])
            MB = sbp("MB", [P, NS, T])
            Z3 = sbp("Z3", [P, T])
            QK = sbp("QK", [P, 2 * T])
            PARTS = sbp("PARTS", [P, 3, 2 * T], bf16)
            VF = sbp("VF", [P, 2, P])
            MX = sbp("MX", [P, 2, HEADS, 2])
            NM = sbp("NM", [2 * HEADS, P])
            NP = sbp("NP", [2 * HEADS, 3, P], bf16)
            PT = sbp("PT", [P, 2, 2, 4, T])
            AV = sbp("AV", [P, 2, T])
            RD = sbp("RD", [P, 2, 4, 4])
            YA = sbp("YA", [P, 2, P])

            a_init = semp("a_init")
            a_ones = semp("a_ones")
            a_cx = [semp(f"a_cx{k}") for k in range(NS)]
            a_qa = [semp(f"a_qa{k}") for k in range(NS)]
            a_mx = [semp(f"a_mx{k}") for k in range(NS)]
            a_dve = semp("a_dve")
            a_pool = semp("a_pool")
            a_var = semp("a_var")
            a_rstd = semp("a_rstd")
            a_z3 = semp("a_z3")
            a_proj = semp("a_proj")
            a_qk = semp("a_qk")
            a_split = semp("a_split")
            a_scr = semp("a_scr")
            a_mscr = semp("a_mscr")
            a_vps = semp("a_vps")
            a_vf = semp("a_vf")
            a_vp = semp("a_vp")
            a_s = semp("a_s")
            a_red = semp("a_red")
            a_mxT = semp("a_mxT")
            a_nm = semp("a_nm")
            a_np = semp("a_np")
            a_st = primed("a_st")
            a_exp = semp("a_exp")
            a_pv = primed("a_pv")
            a_av = primed("a_av")
            a_yT = primed("a_yT")
            a_ya = semp("a_ya")
            a_yo = primed("a_yo")
            a_x3 = primed("a_x3")

            SBK = [bank[0], bank[1]]
            TBK = [psum[:, 2 * 512:4 * 512], psum[:, 4 * 512:6 * 512]]
            PVB, MISC = bank[6], bank[7]
            AHEAD_S, AHEAD_Q = 2, 3

            def xb(b):
                return X[:, bass.ds(b, 1), :].rearrange("p b c -> p (b c)")

            def at(g, k, ahead):
                return g + (k + ahead) // GB, (k + ahead) % GB

            def pe_proj(pe, g, k, misc_free):
                b = GB * g + k
                misc_free()
                pe.wait_ge(a_z3, b + 1)
                pe.wait_ge(a_cx[k], 32 * (g + 1))
                pe.matmul(MISC[:, 0:T], wq[:], Z3[:], start=True, stop=True)
                pe.matmul(MISC[:, T:2 * T], wk[:], CX[:, k, :], start=True, stop=True).then_inc(a_proj, 1)

            def pe_v(pe, g, k):
                b = GB * g + k
                pe.wait_ge(a_qk, 2 * b + 2)
                for st in range(2):
                    last = pe.matmul(MISC[:, st * P:(st + 1) * P], CX[:, k, st * P:(st + 1) * P], wv[:],
                                     start=True, stop=True)
                last.then_inc(a_vps, 1)

            def pe_scores(pe, g, k, heads, first=False):
                b = GB * g + k
                for h in heads:
                    if h == 0:
                        pe.wait_ge(a_qa[k], 16 * N_FILL * (g + 1))
                    if not (first and h < 2):
                        pe.wait_ge(a_red, HEADS * b + h - 1)
                    for tt in range(2):
                        last = pe.matmul(SBK[h % 2][:, tt * T:(tt + 1) * T], QA[:, k, h, tt * P:(tt + 1) * P],
                                         KA[:, k, h, :], start=True, stop=True)
                    last.then_inc(a_s, 1)

            def pe_mxT(pe, g, k, misc_free):
                misc_free()
                pe.wait_ge(a_red, HEADS * (GB * g + k + 1))
                pe.transpose(MISC[0:2 * HEADS, 0:P], MX[:, k % 2, :, :].rearrange("p h t -> p (h t)"),
                             ident[:]).then_inc(a_mxT, 1)

            def pe_scoresT(pe, g, k, i, first=False):
                b = GB * g + k
                if i == 0:
                    pe.wait_ge(a_mx[k], 16 * (g + 1))
                for st in range(2):
                    n = 8 * b + 2 * i + st
                    if not (first and 2 * i + st < 2):
                        pe.wait_ge(a_exp, n - 1)
                    for j in range(4):
                        h = 4 * j + i
                        last = pe.matmul(TBK[st][:, j * T:(j + 1) * T],
                                         KA[:, k, h, st * P:(st + 1) * P], QA[:, k, h, :], start=True, stop=True)
                    last.then_inc(a_st, 1)

            def pe_pv(pe, g, k, i):
                b = GB * g + k
                if i == 0:
                    pe.wait_ge(a_vp, b + 1)
                    pe.wait_ge(a_av, 1 + b)
                grp = 0 if i < 3 else 1
                for st in range(2):
                    pe.wait_ge(a_exp, 8 * b + 2 * i + st + 1)
                    for j in range(4):
                        last = pe.matmul(PVB[32 * j:32 * j + 32, grp * T:(grp + 1) * T],
                                         VP[:, k, st, 4 * j + i, :], PT[:, i % 2, st, j, :],
                                         start=(i in (0, 3) and st == 0), stop=(i in (2, 3) and st == 1))
                last.then_inc(a_pv, 1)

            def pe_yT(pe, b, misc_free):
                misc_free()
                pe.wait_ge(a_av, 1 + b + 1)
                for tt in range(2):
                    for grp in range(2):
                        last = pe.transpose(MISC[:, (2 * tt + grp) * P:(2 * tt + grp + 1) * P],
                                            AV[:, grp, tt * P:(tt + 1) * P], ident[:])
                last.then_inc(a_yT, 1)

            def pe_yo(pe, b, misc_free):
                misc_free()
                pe.wait_ge(a_ya, b + 1)
                for tt in range(2):
                    last = pe.transpose(MISC[:, tt * P:(tt + 1) * P], YA[:, tt, :], ident[:])
                last.then_inc(a_yo, 1)

            def dve_ln3(dve, ch, b):
                dve.wait_ge(a_proj, b)
                layer_norm_steps(ch, lambda i: xb(b), lambda i: Z3[:], 1, a_var, a_rstd, b + 1).then_inc(a_z3, 1)

            def dve_qk(dve, g, k):
                b = GB * g + k
                dve.wait_ge(a_proj, b + 1)
                dve.wait_ge(a_split, b)
                for c in range(2):
                    dve.scalar_tensor_tensor(out=QK[:, c * T:(c + 1) * T], in0=MISC[:, c * T:(c + 1) * T],
                                             scalar=bqk[:, c:c + 1], in1=MB[:, k, :], op0=ALU.add,
                                             op1=ALU.mult).then_inc(a_qk, 1)

            def dve_vf(dve, b):
                dve.wait_ge(a_vps, b + 1)
                dve.wait_ge(a_vp, b)
                dve.tensor_tensor(VF[:, :, :], MISC[:, 0:T].rearrange("p (s c) -> p s c", s=2),
                                  bvb[:, :].unsqueeze(1).broadcast_to([P, 2, P]), ALU.add).then_inc(a_vf, 1)

            def dve_reduce(dve, g, k, heads, first=False):
                b, par = GB * g + k, k % 2
                if heads[0] == 0 and not first:
                    dve.wait_ge(a_mxT, b - 1)
                for h in heads:
                    dve.wait_ge(a_s, HEADS * b + h + 1)
                    dve.tensor_reduce(MX[:, par, h, :], SBK[h % 2][:, :].rearrange("p (a s) -> p a s", a=2),
                                      axis=AX.X, op=ALU.max).then_inc(a_red, 1)

            def dve_y(dve, ch, b):
                dve.wait_ge(a_yT, 1 + b + 1)
                yt = MISC[:, :].rearrange("p (t g c) -> p t g c", t=2, g=2)
                den_a = yt[:, :, 0, :].rearrange("p t (j r) -> p t j r", j=4)[:, :, :, 0:27]\
                    .rearrange("p t j (i r) -> p t j i r", r=9)[:, :, :, :, 8]
                den_b = yt[:, :, 1, :].rearrange("p t (j r) -> p t j r", j=4)[:, :, :, 8]
                ch.do(dve.reciprocal(RD[:, :, :, 3], den_b))
                for tt in range(2):
                    ch.do(dve.reciprocal(RD[:, tt, :, 0:3], den_a[:, tt]))
                ch.wait()
                for tt in range(2):
                    rd = RD[:, tt, :, :].rearrange("p j i -> p (j i)")
                    ch.do(dve.tensor_scalar(rd, rd, maskT[:, tt, bass.ds(b, 1)], tg[:, 1:2], ALU.mult, ALU.mult))
                ch.wait()
                dve.wait_ge(a_yo, 1 + b)
                for tt in range(2):
                    dst = YA[:, tt, :].rearrange("p (j i d) -> p j i d", j=4, i=4)
                    src = yt[:, tt, 0, :].rearrange("p (j r) -> p j r", j=4)[:, :, 0:27]\
                        .rearrange("p j (i r) -> p j i r", r=9)[:, :, :, 0:8]
                    ch.do(dve.tensor_tensor(dst[:, :, 0:3, :], src,
                                            RD[:, tt, :, 0:3].unsqueeze(3).broadcast_to([P, 4, 3, 8]), ALU.mult))
                dst = YA[:, :, :].rearrange("p t (j i d) -> p t j i d", j=4, i=4)[:, :, :, 3, :]
                src = yt[:, :, 1, :].rearrange("p t (j r) -> p t j r", j=4)[:, :, :, 0:8]
                dve.tensor_tensor(dst, src, RD[:, :, :, 3].unsqueeze(3).broadcast_to([P, 2, 4, 8]), ALU.mult)\
                    .then_inc(a_ya, 1)

            Y_STEPS = 7

            def dve_x3(dve, b):
                dve.wait_ge(a_yo, 1 + b + 1)
                dve.tensor_tensor(xb(b), xb(b), MISC[:, 0:T], ALU.add).then_inc(a_x3, 1)

            def act_nm(act, b):
                act.wait_ge(a_mxT, b + 1)
                act.wait_ge(a_np, b)
                act.activation(NM[:], MISC[0:2 * HEADS, 0:P], ACT.Copy, scale=-1.0).then_inc(a_nm, 1)

            def act_exp(act, g, k, i, first=False):
                b = GB * g + k
                for st in range(2):
                    act.wait_ge(a_st, 1 + 8 * b + 2 * i + st + 1)
                    if st == 0 and not first:
                        act.wait_ge(a_pv, 1 + 4 * b + i - 1)
                    act.activation(PT[:, i % 2, st, :, :].rearrange("p j t -> p (j t)"), TBK[st], ACT.Exp)\
                        .then_inc(a_exp, 1)

            def act_av(act, b):
                act.wait_ge(a_pv, 1 + 4 * b + 4)
                act.wait_ge(a_yT, 1 + b)
                act.activation(AV[:, :, :].rearrange("p a t -> p (a t)"), PVB[:, :], ACT.Copy).then_inc(a_av, 1)

            def split(pool, pch, src, nil, parts):
                for r in range(2):
                    if r > 0:
                        pch.wait()
                    pch.do(pool.tensor_tensor(parts(r), src, nil, ALU.add))
                    pch.wait()
                    last = pool.tensor_tensor(src if r == 0 else parts(2), src, parts(r), ALU.subtract)
                    if r == 0:
                        pch.do(last)
                return last

            SPLIT_STEPS = 3

            def pool_split(pool, pch, b):
                pool.wait_ge(a_qk, 2 * b + 2)
                pool.wait_ge(a_scr, 16 * b)
                split(pool, pch, QK[:], zeros[:], lambda r: PARTS[:, r, :]).then_inc(a_split, 1)

            def pool_vp(pool, g, k, first=False):
                b = GB * g + k
                pool.wait_ge(a_vf, b + 1)
                if not first:
                    pool.wait_ge(a_pv, 1 + 4 * (b - 3))
                for st in range(2):
                    for i in range(4):
                        lo = 9 * i if i < 3 else 0
                        dst = VP[:, k, st, :, :].rearrange("p (j i) c -> p j i c", i=4)[:, :, i, lo:lo + 8]
                        src = VF[:, st, :].rearrange("p (j i d) -> p j i d", j=4, i=4)[:, :, i, :]
                        last = pool.tensor_tensor(dst, src, maskT[:, st, bass.ds(b, 1)].unsqueeze(2)
                                                  .broadcast_to([P, 4, 8]), ALU.mult)
                last.then_inc(a_vp, 1)

            def pool_np(pool, pch, g, k):
                pool.wait_ge(a_nm, GB * g + k + 1)
                pool.wait_ge(a_mscr, 16 * (GB * g + k))
                split(pool, pch, NM[:], zeros[0:2 * HEADS, 0:P], lambda r: NP[:, r, :]).then_inc(a_np, 1)

            N_FILL = 14

            def sp_ctx(sp, g, k):
                sp.dma_start(CX[:, k, :], ctx[bass.ds(GB * g + k, 1), :, :].rearrange("b p c -> (b p) c")).then_inc(a_cx[k], 16)
                sp.dma_start(MB[:, k, :], mask[bass.ds(GB * g + k, 1), :].broadcast_to([P, T])).then_inc(a_cx[k], 16)

            def sp_fill(sp, g, k, first=False):
                b = GB * g + k
                if not first:
                    sp.wait_ge(a_st, 1 + 8 * (b - 3))
                    alone(sp)
                sp.wait_ge(a_split, b + 1)
                alone(sp)
                if not first:
                    gg, kk = at(g, k, -2)
                    sp.wait_ge(a_qa[kk], 16 * N_FILL * (gg + 1))
                scr = stack_scr[k % 2]
                sp.dma_start(scr.rearrange("r c t -> c r t"), PARTS[:, :, :]).then_inc(a_scr, 16)
                sp.wait_ge(a_scr, 16 * (b + 1))
                alone(sp)
                for dst, part, lo in ((QA, Q_PART, 0), (KA, K_PART, T)):
                    for r in range(6):
                        sp.dma_start(dst[HD * r:HD * (r + 1), k, :, :],
                                     scr[part[r], :, lo:lo + T].rearrange("(h d) t -> d h t", d=HD))\
                          .then_inc(a_qa[k], 16)
                rows = lambda scr_, n: scr_[bass.ds(b, 1), 0:n, :].rearrange("b r t -> (b r) t").unsqueeze(1)\
                    .broadcast_to([n, HEADS, T])
                sp.dma_start(QA[48:60, k, :, :], rows(qrow_scr, 12)).then_inc(a_qa[k], 16)
                sp.dma_start(KA[48:54, k, :, :], rows(krow_scr, 6)).then_inc(a_qa[k], 16)

            def sp_max(sp, g, k, first=False):
                b = GB * g + k
                sp.wait_ge(a_np, b + 1)
                alone(sp)
                if not first:
                    gg, kk = at(g, k, -2)
                    sp.wait_ge(a_mx[kk], 16 * (gg + 1))
                sp.dma_start(max_scr[k % 2].rearrange("r p c -> p r c"), NP[:, :, :]).then_inc(a_mscr, 16)
                sp.wait_ge(a_mscr, 16 * (b + 1))
                alone(sp)
                sp.dma_start(QA[57:60, k, :, :], max_scr[k % 2].rearrange("r (h t) c -> r h (t c)", t=2))\
                  .then_inc(a_mx[k], 16)

            with nc.Block() as block:
                @block.sync
                def _(sp):
                    for primed_sem in at_one:
                        sp.sem_inc(primed_sem, 1)
                    for k in range(GB):
                        sp_ctx(sp, 0, k)
                    sp.wait_ge(a_init, 3)
                    for k in range(NS):
                        sp.dma_start(KA[54:60, k, :, :], krow_scr[0, 6:12, :].unsqueeze(1).broadcast_to([6, HEADS, T]))\
                          .then_inc(a_ones, 16)
                    for b in range(AHEAD_Q):
                        sp_fill(sp, 0, b, first=True)
                    for b in range(AHEAD_S):
                        sp_max(sp, 0, b, first=True)

                    def sp_batch(g, k, last):
                        if not last:
                            sp.wait_ge(a_vps, GB * g + k + 1)
                            alone(sp)
                            sp_ctx(sp, g + 1, k)
                        if not last or k + AHEAD_Q < GB:
                            sp_fill(sp, *at(g, k, AHEAD_Q))
                        if not last or k + AHEAD_S < GB:
                            sp_max(sp, *at(g, k, AHEAD_S))

                    with sp.Fori(0, NG - 1) as g:
                        for k in range(GB):
                            sp_batch(g, k, False)
                    for k in range(GB):
                        sp_batch(NG - 1, k, True)

                @block.scalar
                def _(act):
                    for b in range(AHEAD_S):
                        act_nm(act, b)
                    act_exp(act, 0, 0, 0, first=True)

                    def act_batch(g, k, last):
                        b = GB * g + k
                        for i in range(1, 4):
                            act_exp(act, g, k, i)
                        act_av(act, b)
                        if not last or k + 1 < GB:
                            act_exp(act, *at(g, k, 1), 0)
                        if not last or k + AHEAD_S < GB:
                            act_nm(act, b + AHEAD_S)

                    with act.Fori(0, NG - 1) as g:
                        for k in range(GB):
                            act_batch(g, k, False)
                    for k in range(GB):
                        act_batch(NG - 1, k, True)

                @block.gpsimd
                def _(pool):
                    pch = Chain(pool, a_pool)
                    pool.memset(QA[:, :, :, :].rearrange("p s h t -> p (s h t)").bitcast(fp32), 0.0).then_inc(a_init, 1)
                    pch.do(pool.memset(VP[:, :, :, :, :], 0.0))
                    pch.wait()
                    for i in range(4):
                        c = 9 * i + 8 if i < 3 else 8
                        pch.do(pool.memset(VP[:, :, :, :, :].rearrange("p s a (j i) c -> p (s a) j i c", i=4)[:, :, :, i, c], 1.0))
                    pch.wait()
                    for b in range(AHEAD_Q):
                        power_step(pool, 1, a_var, a_rstd, b + 1)
                        pool_split(pool, pch, b)
                        pool_vp(pool, 0, b, first=True)
                    for b in range(AHEAD_S):
                        pool_np(pool, pch, 0, b)
                    before = pch.n

                    def pool_batch(g, k, last):
                        if not last or k + AHEAD_Q < GB:
                            power_step(pool, 1, a_var, a_rstd, GB * g + k + AHEAD_Q + 1)
                            pool_split(pool, pch, GB * g + k + AHEAD_Q)
                            pool_vp(pool, *at(g, k, AHEAD_Q))
                        if not last or k + AHEAD_S < GB:
                            pool_np(pool, pch, *at(g, k, AHEAD_S))

                    with pool.Fori(0, NG - 1) as g:
                        pch = Chain(pool, a_pool, before + 2 * SPLIT_STEPS * GB * g)
                        for k in range(GB):
                            pool_batch(g, k, False)
                        assert pch.n == 2 * SPLIT_STEPS * GB
                    pch = Chain(pool, a_pool, before + 2 * SPLIT_STEPS * GB * (NG - 1))
                    for k in range(GB):
                        pool_batch(NG - 1, k, True)

                @block.tensor
                def _(pe):
                    for b in range(AHEAD_Q):
                        pe_proj(pe, 0, b, lambda: pe.wait_ge(a_vf, b))
                        pe_v(pe, 0, b)
                    pe.wait_ge(a_init, 3)
                    pe.wait_ge(a_ones, 16 * NS)
                    for b in range(AHEAD_S):
                        pe_scores(pe, 0, b, range(HEADS), first=(b == 0))
                        pe_mxT(pe, 0, b, lambda: pe.wait_ge(*((a_vf, AHEAD_Q) if b == 0 else (a_nm, b))))
                    pe_scoresT(pe, 0, 0, 0, first=True)

                    def pe_batch(g, k, last):
                        b = GB * g + k
                        more_q = not last or k + AHEAD_Q < GB
                        more_s = not last or k + AHEAD_S < GB
                        if more_q:
                            def free():
                                pe.wait_ge(a_nm, b + AHEAD_S)
                                pe.wait_ge(a_x3, 1 + b)
                            pe_proj(pe, *at(g, k, AHEAD_Q), free)
                        for i in range(1, 5):
                            if more_s:
                                pe_scores(pe, *at(g, k, AHEAD_S), range(4 * i - 4, 4 * i))
                            if i < 4:
                                pe_scoresT(pe, g, k, i)
                            elif not last or k + 1 < GB:
                                pe_pv(pe, g, k, 3)
                                pe_scoresT(pe, *at(g, k, 1), 0)
                            else:
                                pe_pv(pe, g, k, 3)
                            if i < 4:
                                pe_pv(pe, g, k, i - 1)
                            if i == 2 and more_q:
                                pe_v(pe, *at(g, k, AHEAD_Q))
                        if more_q:
                            pe_yT(pe, b, lambda: pe.wait_ge(a_vf, b + AHEAD_Q + 1))
                        else:
                            pe_yT(pe, b, lambda: pe.wait_ge(a_x3, 1 + b))
                        if more_s:
                            pe_mxT(pe, *at(g, k, AHEAD_S), lambda: pe.wait_ge(a_ya, b + 1))
                            pe_yo(pe, b, lambda: pe.wait_ge(a_nm, b + AHEAD_S + 1))
                        else:
                            pe_yo(pe, b, lambda: None)

                    with pe.Fori(0, NG - 1) as g:
                        for k in range(GB):
                            pe_batch(g, k, False)
                    for k in range(GB):
                        pe_batch(NG - 1, k, True)

                @block.vector
                def _(dve):
                    dve.memset(KA[:, :, :, :].rearrange("p s h t -> p (s h t)").bitcast(fp32), 0.0).then_inc(a_init, 2)
                    ch = Chain(dve, a_dve)
                    for b in range(AHEAD_Q):
                        dve_ln3(dve, ch, b)
                        dve.wait_ge(a_cx[b], 32)
                        dve_qk(dve, 0, b)
                        dve_vf(dve, b)
                    for b in range(AHEAD_S):
                        dve_reduce(dve, 0, b, range(HEADS), first=True)
                    before = ch.n
                    per_group = GB * (LN_STEPS(1) + Y_STEPS)

                    def dve_batch(ch, g, k, last):
                        b = GB * g + k
                        more_q = not last or k + AHEAD_Q < GB
                        more_s = not last or k + AHEAD_S < GB
                        if more_q:
                            gq, kq = at(g, k, AHEAD_Q)
                            dve_ln3(dve, ch, b + AHEAD_Q)
                            dve.wait_ge(a_cx[kq], 32 * (gq + 1))
                            dve_qk(dve, gq, kq)
                        for i in range(4):
                            if more_s:
                                dve_reduce(dve, *at(g, k, AHEAD_S), range(4 * i, 4 * i + 4))
                            if i == 1 and more_q:
                                dve_vf(dve, b + AHEAD_Q)
                        dve_y(dve, ch, b)
                        dve_x3(dve, b)

                    with dve.Fori(0, NG - 1) as g:
                        ch = Chain(dve, a_dve, before + per_group * g)
                        for k in range(GB):
                            dve_batch(ch, g, k, False)
                        assert ch.n == per_group, ch.n
                    ch = Chain(dve, a_dve, before + per_group * (NG - 1))
                    for k in range(GB):
                        dve_batch(ch, NG - 1, k, True)
        if stop_after == 2:
            store_x()
            return
        with ExitStack() as part:
            def sbp(name, shape, dt=fp32):
                return sb(name, shape, dt, part)

            def semp(name):
                return sem(name, part)

            at_one = []

            def primed(name):
                at_one.append(semp(name))
                return at_one[-1]

            Z4S = sbp("Z4S", [P, GB, C])
            Z4 = sbp("Z4", [P, B, C])
            ZT4 = sbp("ZT4", [P, 2, B * P])
            LT = sbp("LT", [NE, GT])
            L = sbp("L", [P, B, NE])
            LX = sbp("LX", [P, B, NE])
            mxl = sbp("mxl", [P, B])
            sml = sbp("sml", [P, B])
            gate = sbp("gate", [P, B])
            rev = sbp("rev", [P, B, NE], mybir.dt.int32)
            revf = sbp("revf", [P, B, NE])
            tok = sbp("tok", [P, B], mybir.dt.int32)
            tokf = sbp("tokf", [P, B])
            key = sbp("key", [P, B, NE])
            kmax = sbp("kmax", [P, B])
            OH = sbp("OH", [P, B, NE])
            OHB = sbp("OHB", [P, NE, B], bf16)
            tri = sbp("tri", [P, P], bf16)
            ones = sbp("ones", [P, P], bf16)
            carry = sbp("carry", [P, NE, B])
            INC = sbp("INC", [P, NE, B])
            TOT = sbp("TOT", [P, NE, B])
            POS = sbp("POS", [P, NE, B])
            pos = sbp("pos", [P, B])
            keepm = sbp("keepm", [P, B])
            flat = sbp("flat", [P, B])
            flat_u = sbp("flat_u", [P, B], u32)
            from_u = sbp("from_u", [P, B], u32)
            fromf = sbp("fromf", [P, B])
            TH = sbp("THs", [P, 2, GT])
            H1 = sbp("H1s", [P, 2, GT])
            HS = sbp("HS", [P, NH, GT])
            WE1 = sbp("WE1", [P, 2, 2, EH])
            WE3 = sbp("WE3", [P, 2, 2, EH])
            WE2 = sbp("WE2", [P, 2, NH, C])
            XD = sbp("XD", [P, 2, 2, C])
            XT = sbp("XT", [P, 2, 2, CAP])
            HE = sbp("HE", [P, NH, CAP])
            OE = sbp("OE", [P, 2, 2, C])
            GT_ = sbp("GT_", [P, B, C])

            m_pool = semp("m_pool")
            m_dve = semp("m_dve")
            m_var = semp("m_var")
            m_rstd = semp("m_rstd")
            m_z4 = semp("m_z4")
            m_z4T = primed("m_z4T")
            m_z4c = primed("m_z4c")
            m_zt = primed("m_zt")
            m_lg = semp("m_lg")
            m_lt = primed("m_lt")
            m_lb = semp("m_lb")
            m_l = primed("m_l")
            m_lx = semp("m_lx")
            m_ex = semp("m_ex")
            m_oh = semp("m_oh")
            m_cum = semp("m_cum")
            m_flat = semp("m_flat")
            m_scat = semp("m_scat")
            m_gu = semp("m_gu")
            m_th = semp("m_th")
            m_h = primed("m_h")
            m_dn = primed("m_dn")
            m_xs = primed("m_xs")
            e_w = [semp(f"e_w{s}") for s in range(2)]
            e_xd = [semp(f"e_xd{s}") for s in range(2)]
            e_xT = semp("e_xT")
            e_xt = primed("e_xt")
            e_gu = semp("e_gu")
            e_th = semp("e_th")
            e_h = primed("e_h")
            e_dn = primed("e_dn")
            e_oe = primed("e_oe")
            e_st = [primed(f"e_st{s}") for s in range(2)]
            m_gath = [semp(f"m_gath{g}") for g in range(NG)]
            m_out = semp("m_out")
            m_stored = semp("m_stored")

            ROUTE = LN_STEPS(GB)
            flat2 = lambda t: t[:, :, :].rearrange("p a b -> p (a b)")

            with nc.Block() as block:
                @block.sync
                def _(sp):
                    for primed_sem in at_one:
                        sp.sem_inc(primed_sem, 1)
                    def load_weights(e, s):
                        for dst, src in ((WE1[:, s, :, :], W1), (WE3[:, s, :, :], W3)):
                            sp.dma_start(dst, src[bass.ds(e, 1), :, :].rearrange("e (h p) i -> p (e h) i", p=P))\
                              .then_inc(e_w[s], 16)
                        sp.dma_start(WE2[:, s, 0:2, :], W2[bass.ds(e, 1), 0:2 * P, :]
                                     .rearrange("e (i p) c -> p (e i) c", p=P)).then_inc(e_w[s], 16)
                        sp.dma_start(WE2[0:EH - 2 * P, s, 2, :], W2[bass.ds(e, 1), 2 * P:EH, :]
                                     .rearrange("e p c -> (e p) c")).then_inc(e_w[s], 16)

                    def load_tokens(e, s):
                        sp.dma_start(XD[:, s, :, :], dispatched[bass.ds(CAP * e, CAP), :]
                                     .rearrange("(a p) c -> p a c", p=P)).then_inc(e_xd[s], 16)

                    for s in range(2):
                        load_weights(s, s)
                    sp.wait_ge(m_scat, 16 * B)
                    for s in range(2):
                        load_tokens(s, s)

                    def store(e2, s):
                        e = 2 * e2 + s
                        sp.wait_ge(e_oe, 1 + e + 1)
                        sp.dma_start(expert_out[bass.ds(CAP * e, CAP), :].rearrange("(a p) c -> p a c", p=P),
                                     OE[:, s, :, :]).then_inc(e_st[s], 16)

                    with sp.Fori(0, NE // 2 - 1) as e2:
                        for s in range(2):
                            sp.wait_ge(e_xT, 2 * e2 + s + 1)
                            load_tokens(2 * e2 + s + 2, s)
                            sp.wait_ge(e_dn, 1 + 2 * e2 + s + 1)
                            load_weights(2 * e2 + s + 2, s)
                            store(e2, s)
                    for s in range(2):
                        store(NE // 2 - 1, s)
                    for g in range(NG):
                        sp.wait_ge(m_out, GB * g + GB)
                        sp.dma_start(ot[:, GB * g:GB * (g + 1), :], X[:, GB * g:GB * (g + 1), :]).then_inc(m_stored, 16)
                    sp.wait_ge(m_stored, 16 * NG)

                @block.gpsimd
                def _(pool):
                    pool.memset(ones[:], 1.0).then_inc(m_pool, 1)
                    pool.memset(tri[:], 1.0).then_inc(m_pool, 1)
                    pool.memset(carry[:, :, 0:1], 0.0).then_inc(m_pool, 1)
                    pool.memset(carry[:, :, 1:B], 1.0).then_inc(m_pool, 1)
                    pool.iota(rev[:], pattern=[[0, B], [-1, NE]], base=NE, channel_multiplier=0).then_inc(m_pool, 1)
                    pool.iota(tok[:], pattern=[[P, B]], base=SLOTS, channel_multiplier=1).then_inc(m_pool, 1)
                    pool.wait_ge(m_pool, 6)
                    pool.tensor_copy(revf[:], rev[:]).then_inc(m_pool, 1)
                    pool.tensor_copy(tokf[:], tok[:]).then_inc(m_pool, 1)
                    pool.affine_select(out=tri[:], in_=tri[:], compare_op=ALU.is_gt, fill=0.0, base=0,
                                       pattern=[[1, P]], channel_multiplier=-1).then_inc(m_pool, 1)
                    with pool.Fori(0, NG) as g:
                        power_step(pool, GB, m_var, m_rstd, g + 1)
                    pool.wait_ge(m_flat, 1)
                    pool.wait_ge(m_z4c, 1 + NG)
                    for t in range(B):
                        pool.indirect_dma_start(out=dispatched, out_offset=bass.IndirectOffsetOnAxis(ap=flat_u[:, t:t + 1], axis=0),
                                                in_=Z4[:, t, :], in_offset=None).then_inc(m_scat, 16)
                    pool.wait_ge(m_flat, 3)
                    for s in range(2):
                        pool.wait_ge(e_st[s], 1 + 16 * (NE // 2))
                    for t in range(B):
                        pool.indirect_dma_start(out=GT_[:, t, :], out_offset=None, in_=expert_out,
                                                in_offset=bass.IndirectOffsetOnAxis(ap=from_u[:, t:t + 1], axis=0))\
                            .then_inc(m_gath[t // GB], 16)

                @block.scalar
                def _(act):
                    with act.Fori(0, NG) as g:
                        act.wait_ge(m_z4, g + 1)
                        act.activation(Z4[:, bass.ds(GB * g, GB), :], Z4S[:, :, :], ACT.Copy).then_inc(m_z4c, 1)
                        for h in range(2):
                            act.wait_ge(m_z4T, 1 + 2 * g + h + 1)
                            act.activation(ZT4[:, h, bass.ds(GT * g, GT)], bank[h], ACT.Copy).then_inc(m_zt, 1)
                        act.wait_ge(m_lg, g + 1)
                        act.activation(LT[:], bank[2][0:NE, :], ACT.Copy).then_inc(m_lt, 1)
                    act.wait_ge(m_lx, 1)
                    act.activation(flat2(LX), flat2(LX), ACT.Exp).then_inc(m_ex, 1)
                    with act.Fori(0, NG) as g:
                        for i in range(NH):
                            m = width(i, EH)
                            act.wait_ge(m_gu, NH * g + i + 1)
                            s = i % 2
                            if i < 2:
                                act.wait_ge(m_h, 1 + NH * g)
                            else:
                                act.wait_ge(m_h, 1 + NH * g + i - 1)
                            act.activation(TH[0:m, s, :], bank[2 * s][0:m, :], ACT.Tanh, scale=0.5).then_inc(m_th, 1)
                    with act.Fori(0, NE // 2) as e2:
                        for s in range(2):
                            e = 2 * e2 + s
                            act.wait_ge(e_xT, e + 1)
                            act.activation(XT[:, s, :, :].rearrange("p h t -> p (h t)"), bank[4], ACT.Copy).then_inc(e_xt, 1)
                            for i in range(NH):
                                m = width(i, EH)
                                act.wait_ge(e_gu, NH * e + i + 1)
                                if i == 2:
                                    act.wait_ge(e_h, 1 + NH * e + 1)
                                else:
                                    act.wait_ge(e_h, 1 + NH * e)
                                act.activation(TH[0:m, i % 2, 0:CAP], bank[i][0:m, 0:CAP], ACT.Tanh, scale=0.5).then_inc(e_th, 1)
                            act.wait_ge(e_dn, 1 + e + 1)
                            act.wait_ge(e_st[s], 1 + 16 * e2)
                            act.activation(OE[:, s, :, :].rearrange("p a c -> p (a c)"), bank[6], ACT.Copy).then_inc(e_oe, 1)

                @block.tensor
                def _(pe):
                    with pe.Fori(0, NG) as g:
                        pe.wait_ge(m_z4, g + 1)
                        pe.wait_ge(m_zt, 1 + 2 * g)
                        for h in range(2):
                            for b in range(GB):
                                last = pe.transpose(bank[h][:, b * P:(b + 1) * P], Z4S[:, b, h * P:(h + 1) * P], ident[:])
                            last.then_inc(m_z4T, 1)
                        pe.wait_ge(m_zt, 1 + 2 * g + 2)
                        pe.wait_ge(m_lt, 1 + g)
                        for h in range(2):
                            last = pe.matmul(bank[2][0:NE, :], wgt[:, h, :], ZT4[:, h, bass.ds(GT * g, GT)],
                                             start=(h == 0), stop=(h == 1))
                        last.then_inc(m_lg, 1)
                        pe.wait_ge(m_lt, 1 + g + 1)
                        pe.wait_ge(m_l, 1 + g)
                        alone(pe)
                        for b in range(GB):
                            last = pe.transpose(bank[3][:, b * NE:(b + 1) * NE], LT[:, b * P:(b + 1) * P], ident[0:NE, 0:NE])
                        last.then_inc(m_lb, 1)
                    pe.wait_ge(m_oh, 1)
                    pe.wait_ge(m_pool, 9)
                    pe.matmul(bank[4][:, 0:NE * B], tri[:], flat2(OHB), start=True, stop=True)
                    pe.matmul(bank[5][:, 0:NE * B], ones[:], flat2(OHB), start=True, stop=True).then_inc(m_cum, 1)
                    with pe.Fori(0, NG) as g:
                        for i in range(NH):
                            m = width(i, EH)
                            s = i % 2
                            if i == 0:
                                pe.wait_ge(m_l, 1 + NG)
                            if i < 2:
                                pe.wait_ge(m_h, 1 + NH * g)
                            else:
                                pe.wait_ge(m_h, 1 + NH * g + i - 1)
                            for w, bk in ((wsh1, bank[2 * s]), (wsh3, bank[2 * s + 1])):
                                for h in range(2):
                                    last = pe.matmul(bk[0:m, :], w[:, h, i * P:i * P + m], ZT4[:, h, bass.ds(GT * g, GT)],
                                                     start=(h == 0), stop=(h == 1))
                            last.then_inc(m_gu, 1)
                        pe.wait_ge(m_h, 1 + NH * g + NH)
                        pe.wait_ge(m_xs, 1 + 2 * g)
                        for k in range(2):
                            for b in range(2):
                                t = 2 * k + b
                                for i in range(NH):
                                    m = width(i, EH)
                                    last = pe.matmul(bank[6 + k][:, b * C:(b + 1) * C], HS[0:m, i, t * P:(t + 1) * P],
                                                     wsh2[0:m, i, :], start=(i == 0), stop=(i == NH - 1))
                            last.then_inc(m_dn, 1)
                    pe.wait_ge(m_xs, 1 + 2 * NG)
                    pe.wait_ge(m_flat, 1)
                    with pe.Fori(0, NE // 2) as e2:
                        for s in range(2):
                            e = 2 * e2 + s
                            pe.wait_ge(e_xd[s], 16 * (e2 + 1))
                            pe.wait_ge(e_xt, 1 + e)
                            for h in range(2):
                                for a in range(2):
                                    last = pe.transpose(bank[4][:, h * CAP + a * P:h * CAP + (a + 1) * P],
                                                        XD[:, s, a, h * P:(h + 1) * P], ident[:])
                            last.then_inc(e_xT, 1)
                            pe.wait_ge(e_xt, 1 + e + 1)
                            pe.wait_ge(e_w[s], 64 * (e2 + 1))
                            for i in range(NH):
                                m = width(i, EH)
                                if i == 0:
                                    pe.wait_ge(e_h, 1 + NH * e)
                                for w, lo in ((WE1, 0), (WE3, CAP)):
                                    for h in range(2):
                                        last = pe.matmul(bank[i][0:m, lo:lo + CAP], w[:, s, h, i * P:i * P + m],
                                                         XT[:, s, h, :], start=(h == 0), stop=(h == 1))
                                last.then_inc(e_gu, 1)
                            pe.wait_ge(e_h, 1 + NH * e + NH)
                            pe.wait_ge(e_oe, 1 + e)
                            for a in range(2):
                                for i in range(NH):
                                    m = width(i, EH)
                                    last = pe.matmul(bank[6][:, a * C:(a + 1) * C], HE[0:m, i, a * P:(a + 1) * P],
                                                     WE2[0:m, s, i, :], start=(i == 0), stop=(i == NH - 1))
                            last.then_inc(e_dn, 1)

                @block.vector
                def _(dve):
                    with dve.Fori(0, NG) as g:
                        ch = Chain(dve, m_dve, LN_STEPS(GB) * g)
                        dve.wait_ge(m_z4T, 1 + 2 * g)
                        dve.wait_ge(m_z4c, 1 + g)
                        layer_norm_steps(ch, lambda i: X[:, bass.ds(GB * g + i, 1), :].rearrange("p b c -> p (b c)"),
                                         lambda i: Z4S[:, i, :], GB, m_var, m_rstd, g + 1).then_inc(m_z4, 1)
                        dve.wait_ge(m_lb, g + 1)
                        dve.tensor_copy(L[:, bass.ds(GB * g, GB), :].rearrange("p b e -> p (b e)"),
                                        bank[3][:, 0:GB * NE]).then_inc(m_l, 1)
                    ch = Chain(dve, m_dve, LN_STEPS(GB) * NG)
                    over_e = lambda v: v[:, :].unsqueeze(2).broadcast_to([P, B, NE])
                    dve.wait_ge(m_l, 1 + NG)
                    ch.do(dve.tensor_reduce(mxl[:], L[:], axis=AX.X, op=ALU.max))
                    ch.wait()
                    dve.tensor_tensor(LX[:], L[:], over_e(mxl), ALU.subtract).then_inc(m_lx, 1)
                    ch.do(dve.tensor_tensor(key[:], L[:], over_e(mxl), ALU.is_equal))
                    ch.wait()
                    dve.wait_ge(m_pool, 9)
                    ch.do(dve.tensor_tensor(key[:], key[:], revf[:], ALU.mult))
                    ch.wait()
                    ch.do(dve.tensor_reduce(kmax[:], key[:], axis=AX.X, op=ALU.max))
                    ch.wait()
                    ch.do(dve.tensor_tensor(OH[:], key[:], over_e(kmax), ALU.is_equal))
                    ch.wait()
                    dve.tensor_copy(OHB[:].rearrange("p e b -> p b e"), OH[:]).then_inc(m_oh, 1)
                    dve.wait_ge(m_ex, 1)
                    ch.do(dve.tensor_reduce(sml[:], LX[:], axis=AX.X, op=ALU.add))
                    ch.wait()
                    ch.do(dve.reciprocal(gate[:], sml[:]))
                    dve.wait_ge(m_cum, 1)
                    ch.do(dve.tensor_copy(flat2(TOT), bank[5][:, 0:NE * B]))
                    ch.wait()
                    ch.do(dve.tensor_tensor_scan(out=flat2(INC), data0=flat2(carry), data1=flat2(TOT), initial=0.0,
                                                 op0=ALU.mult, op1=ALU.add))
                    ch.wait()
                    ch.do(dve.tensor_tensor(flat2(POS), flat2(INC), flat2(TOT), ALU.subtract))
                    ch.wait()
                    ch.do(dve.tensor_tensor(flat2(POS), flat2(POS), bank[4][:, 0:NE * B], ALU.add))
                    ch.wait()
                    ch.do(dve.tensor_tensor(key[:], OH[:], POS[:].rearrange("p e b -> p b e"), ALU.mult))
                    ch.wait()
                    ch.do(dve.tensor_reduce(pos[:], key[:], axis=AX.X, op=ALU.add))
                    ch.wait()
                    ch.do(dve.tensor_scalar(keepm[:], pos[:], float(CAP), None, ALU.is_lt))
                    ch.do(dve.tensor_scalar(flat[:], kmax[:], -float(CAP), float(SLOTS), ALU.mult, ALU.add))
                    ch.wait()
                    ch.do(dve.tensor_tensor(flat[:], flat[:], pos[:], ALU.add))
                    ch.wait()
                    ch.do(dve.tensor_tensor(flat[:], flat[:], tokf[:], ALU.subtract))
                    ch.wait()
                    ch.do(dve.tensor_tensor(flat[:], flat[:], keepm[:], ALU.mult))
                    ch.wait()
                    ch.do(dve.tensor_tensor(flat[:], flat[:], tokf[:], ALU.add))
                    ch.wait()
                    dve.tensor_copy(flat_u[:], flat[:]).then_inc(m_flat, 1)
                    ch.do(dve.tensor_scalar(fromf[:], flat[:], float(SLOTS - 1), None, ALU.min))
                    ch.wait()
                    dve.tensor_copy(from_u[:], fromf[:]).then_inc(m_flat, 1)
                    ch.do(dve.tensor_tensor(gate[:], gate[:], keepm[:], ALU.mult))
                    ch.wait()
                    dve.tensor_scalar(gate[:], gate[:], tg[:, 3:4], None, ALU.mult).then_inc(m_flat, 1)
                    before = LN_STEPS(GB) * NG + ch.n
                    with dve.Fori(0, NG) as g:
                        ch = Chain(dve, m_dve, before + NH * g)
                        for i in range(NH):
                            m = width(i, EH)
                            s = i % 2
                            dve.wait_ge(m_th, NH * g + i + 1)
                            ch.do(dve.scalar_tensor_tensor(out=H1[0:m, s, :], in0=TH[0:m, s, :], scalar=1.0,
                                                           in1=bank[2 * s][0:m, :], op0=ALU.add, op1=ALU.mult))
                            if i == 0:
                                dve.wait_ge(m_dn, 1 + 2 * g)
                            ch.wait()
                            dve.scalar_tensor_tensor(out=HS[0:m, i, :], in0=H1[0:m, s, :], scalar=0.5,
                                                     in1=bank[2 * s + 1][0:m, :], op0=ALU.mult, op1=ALU.mult).then_inc(m_h, 1)
                        for k in range(2):
                            dve.wait_ge(m_dn, 1 + 2 * g + k + 1)
                            xs = X[:, bass.ds(GB * g + 2 * k, 2), :].rearrange("p b c -> p (b c)")
                            dve.scalar_tensor_tensor(out=xs, in0=bank[6 + k], scalar=tg[:, 3:4], in1=xs,
                                                     op0=ALU.mult, op1=ALU.add).then_inc(m_xs, 1)
                    before += NH * NG
                    with dve.Fori(0, NE // 2) as e2:
                        ch = Chain(dve, m_dve, before + 2 * NH * e2)
                        for s in range(2):
                            e = 2 * e2 + s
                            for i in range(NH):
                                m = width(i, EH)
                                dve.wait_ge(e_th, NH * e + i + 1)
                                ch.do(dve.scalar_tensor_tensor(out=H1[0:m, i % 2, 0:CAP], in0=TH[0:m, i % 2, 0:CAP], scalar=1.0,
                                                               in1=bank[i][0:m, 0:CAP], op0=ALU.add, op1=ALU.mult))
                                if i == 0:
                                    dve.wait_ge(e_dn, 1 + e)
                                ch.wait()
                                dve.scalar_tensor_tensor(out=HE[0:m, i, :], in0=H1[0:m, i % 2, 0:CAP], scalar=0.5,
                                                         in1=bank[i][0:m, CAP:2 * CAP], op0=ALU.mult, op1=ALU.mult).then_inc(e_h, 1)
                    dve.wait_ge(m_xs, 1 + 2 * NG)
                    dve.wait_ge(m_flat, 3)
                    for t in range(B):
                        dve.wait_ge(m_gath[t // GB], 16 * GB)
                        dve.scalar_tensor_tensor(out=X[:, t, :], in0=GT_[:, t, :], scalar=gate[:, t:t + 1], in1=X[:, t, :],
                                                 op0=ALU.mult, op1=ALU.add).then_inc(m_out, 1)


def kernel(**inputs):
    import numpy as _np
    import concourse.bacc as _bacc
    from concourse import mybir as _mybir
    from concourse.bass_utils import run_bass_kernel_spmd as _run

    a = {k: _np.asarray(v) for k, v in inputs.items()}
    column = lambda v: v.reshape(-1, P).T
    laid = {
        "x": a["x"], "ctx": a["ctx_2048"], "mask": a["mask_Bx1x2048_fk1"].reshape(B, T),
        "g_xattn": a["g_xattn"], "g_ffn": a["g_ffn"],
        "time_decay": column(a["L0_xattn_time_decay"]), "time_first": column(a["L0_xattn_time_first"]),
        "gate_wT": a["L0_ffn_gate_w"].T, "up_wT": a["L0_ffn_up_w"].T, "down_wT": a["L0_ffn_down_w"].T,
        "gate_s": a["L0_ffn_gate_s"], "up_s": a["L0_ffn_up_s"], "down_s": a["L0_ffn_down_s"],
        "wqT": a["L1_xattn_Wq"].T, "bq": column(a["L1_xattn_bq"]),
        "wkT": a["L1_xattn_Wk"].T, "bk": column(a["L1_xattn_bk"]),
        "wvT": a["L1_xattn_Wv"].T, "bv": a["L1_xattn_bv"],
        "Wg": a["L1_ffn_Wg"], "W1": a["L1_ffn_W1"], "W3": a["L1_ffn_W3"], "W2": a["L1_ffn_W2"],
        "sw1": a["L1_ffn_sw1"], "sw3": a["L1_ffn_sw3"], "sw2": a["L1_ffn_sw2"],
    }
    nc = _bacc.Bacc("TRN2", target_bir_lowering=False, num_devices=1)
    arrays, args = {}, []
    for name, v in laid.items():
        arrays[f"in_{name}"] = _np.ascontiguousarray(v)
        args.append(nc.dram_tensor(f"in_{name}", v.shape, _mybir.dt.from_np(v.dtype), kind="ExternalInput").ap())
    args.append(nc.dram_tensor("out_x", (B, P, C), fp32, kind="ExternalOutput").ap())
    flamingo_kernel(nc, *args)
    r = _run(nc, [arrays], core_ids=[0])
    return r.results[0]["out_x"]
```

```python
from contextlib import ExitStack

import concourse.bass as bass
from concourse import mybir

fp32 = mybir.dt.float32
bf16 = mybir.dt.bfloat16
u32 = mybir.dt.uint32
ALU = mybir.AluOpType
ACT = mybir.ActivationFunctionType
AX = mybir.AxisListType

P = 128
B, C = 16, 256
NG, GB = 4, 4
GT = GB * P
INTER = 704
NI = -(-INTER // P)
HEADS, HD = 16, 8
T = 256
NE, EH = 8, 352
NH = -(-EH // P)
CAP = B * P // NE
SLOTS = NE * CAP
NEG = 1000000.0
EPS = 1e-5
MASK_Q, MASK_K, ONES = 48, 48, 54
STACK = 60
Q_PART = (0, 0, 0, 1, 1, 2)
K_PART = (0, 1, 2, 0, 1, 0)


def width(i, n):
    return min(P, n - i * P)


class Chain:

    def __init__(self, eng, sem, start=0):
        self.eng, self.sem, self.start, self.n = eng, sem, start, 0

    def do(self, ins):
        ins.then_inc(self.sem, 1)
        self.n += 1
        return self.n

    def wait(self, n=None):
        self.eng.wait_ge(self.sem, self.start + (self.n if n is None else n))


def flamingo_kernel(nc, x, ctx, mask, g_xattn, g_ffn, time_decay, time_first, gate_wT, up_wT, down_wT,
                    gate_s, up_s, down_s, wqT, bq, wkT, bk, wvT, bv, Wg, W1, W3, W2, sw1, sw3, sw2, out,
                    stop_after=9):
    stack_scr = nc.dram_tensor("stack_scr", [2, 6, P, T], bf16).ap()
    max_scr = nc.dram_tensor("max_scr", [2, 3, 2 * HEADS, P], bf16).ap()
    qrow_scr = nc.dram_tensor("qrow_scr", [B, 12, T], bf16).ap()
    krow_scr = nc.dram_tensor("krow_scr", [B, 12, T], bf16).ap()
    dispatched = nc.dram_tensor("dispatched", [SLOTS + B * P, C], fp32).ap()
    expert_out = nc.dram_tensor("expert_out", [SLOTS, C], fp32).ap()
    xt = x.rearrange("b p c -> p b c")
    ct = ctx.rearrange("b p c -> p b c")
    ot = out.rearrange("b p c -> p b c")

    with ExitStack() as keep:
        def sb(name, shape, dt=fp32, where=keep):
            return where.enter_context(nc.sbuf_tensor(name, shape, dt))

        def sem(name, where=keep):
            return where.enter_context(nc.semaphore(name))

        psum = keep.enter_context(nc.psum_tensor("psum", [P, 8 * 512], fp32))
        bank = [psum[:, i * 512:(i + 1) * 512] for i in range(8)]
        X = sb("X", [P, B, C])
        ident = sb("ident", [P, P])
        tg = sb("tg", [P, 4])
        neghalf = sb("neghalf", [P, GB])
        stats = sb("stats", [P, GB, 6])
        mv = sb("mv", [P, GB, 2])
        veps = sb("veps", [P, GB])
        rstd = sb("rstd", [P, GB])
        wsh1 = sb("wsh1", [P, 2, EH])
        wsh3 = sb("wsh3", [P, 2, EH])
        wsh2 = sb("wsh2", [P, NH, C])
        wgt = sb("wgt", [P, 2, NE])
        wq = sb("wq", [P, P])
        wk = sb("wk", [P, P])
        wv = sb("wv", [P, P])
        bqk = sb("bqk", [P, 2])
        bvb = sb("bvb", [P, P])
        maskT = sb("maskT", [P, 2, B])
        zeros = sb("zeros", [P, 2 * C])
        s_late = sem("s_late")
        s_alone = {e: sem(f"s_alone_{e}") for e in ("sp", "dve", "pe")}

        def alone(eng):
            eng.sem_inc(s_alone[{nc.sync: "sp", nc.vector: "dve", nc.tensor: "pe"}[eng]], 1)

        def layer_norm_stats(ch, src, n):
            for i in range(n):
                last = ch.do(ch.eng.bn_stats(stats[:, i, :], src(i)))
            ch.wait(last)
            alone(ch.eng)
            for i in range(n):
                last = ch.do(ch.eng.bn_aggr(mv[:, i, :], stats[:, i, :]))
            ch.wait()
            return ch.eng.tensor_scalar(veps[:, 0:n], mv[:, 0:n, 1], EPS, None, ALU.add)

        def layer_norm_steps(ch, src, dst, n, s_var, s_rstd, nth):
            layer_norm_stats(ch, src, n).then_inc(s_var, 1)
            ch.eng.wait_ge(s_rstd, nth)
            for i in range(n):
                last = ch.eng.tensor_scalar(dst(i), src(i), mv[:, i, 0:1], rstd[:, i:i + 1],
                                            ALU.subtract, ALU.mult)
                if i < n - 1:
                    ch.do(last)
            return last

        LN_STEPS = lambda n: n + n + n - 1

        def power_step(eng, n, s_var, s_rstd, nth):
            eng.wait_ge(s_var, nth)
            eng.tensor_tensor(rstd[:, 0:n], veps[:, 0:n], neghalf[:, 0:n], ALU.pow).then_inc(s_rstd, 1)

        def store_x():
            with nc.Block() as block:
                @block.sync
                def _(sp):
                    with ExitStack() as st:
                        s_o = sem("s_store", st)
                        sp.dma_start(ot, X[:, :, :]).then_inc(s_o, 16)
                        sp.wait_ge(s_o, 16)

        with ExitStack() as part:
            wkv = part.enter_context(ExitStack())

            def sbp(name, shape, dt=fp32):
                return sb(name, shape, dt, part)

            def sbw(name, shape, dt=fp32):
                return sb(name, shape, dt, wkv)

            def semp(name):
                return sem(name, part)

            at_one = []

            def primed(name):
                at_one.append(semp(name))
                return at_one[-1]

            gw = sbp("gw", [P, 2, INTER])
            uw = sbp("uw", [P, 2, INTER])
            dw = sbp("dw", [P, NI, C])
            hgs = sbp("hgs", [P, NI])
            hgu = sbp("hgu", [P, NI])
            Z2 = sbp("Z2", [P, GB, C])
            ZT = sbp("ZT", [P, 2, GT])
            TH = sbp("TH", [P, 2, GT])
            H1 = sbp("H1", [P, 2, GT])
            HP = sbp("HP", [P, 8, GT])
            H = HP
            CV = sbw("CV", [P, GB, C])
            dsb = sbw("dsb", [P, C])
            gs = sbw("gs", [P, NI])
            us = sbw("us", [P, NI])
            gates = sbw("gates", [P, 4])
            td = sbw("td", [P, 2])
            tf = sbw("tf", [P, 2])
            tdx = sbw("tdx", [P, 2])
            decay = sbw("decay", [P, 2])
            upos = sbw("upos", [P, 2])
            uneg = sbw("uneg", [P, 2])
            steps01 = sbw("steps01", [P, GB, P])
            DEC = sbw("DEC", [P, 2, GT])
            mrow = sbw("mrow", [B, T])
            mtmp = sbw("mtmp", [B, 3, T])
            mparts = sbw("mparts", [B, 3, 3, T], bf16)
            onesb = sbw("onesb", [6, T], bf16)
            Z1 = sbw("Z1", [P, GB, C])
            EA = sbw("EA", [P, 2, GB, P])
            EB = sbw("EB", [P, 2, GB, P])
            PA = sbw("PA", [P, 2, GB, P])
            PB = sbw("PB", [P, 2, GB, P])
            SA = sbw("SA", [P, 2, GT])
            SB = sbw("SB", [P, 2, GT])
            NUM = sbw("NUM", [P, 2, GT])
            DEN = sbw("DEN", [P, 2, GT])
            Y = sbw("Y", [P, 2, GT])

            s_ld = semp("s_ld")
            s_wts = semp("s_wts")
            s_x = semp("s_x")
            s_c = semp("s_c")
            s_pool0 = semp("s_pool0")
            s_id = semp("s_id")
            s_act0 = semp("s_act0")
            s_dv0 = semp("s_dv0")
            s_mT = semp("s_mT")
            s_mT2 = semp("s_mT2")
            s_mask = semp("s_mask")
            s_mp = semp("s_mp")
            s_zero = semp("s_zero")
            s_mst = semp("s_mst")
            s_dvech = semp("s_dvech")
            s_var1 = semp("s_var1")
            s_rstd1 = semp("s_rstd1")
            s_z1 = semp("s_z1")
            s_kT = semp("s_kT")
            s_vT = primed("s_vT")
            s_exp = semp("s_exp")
            s_pab = semp("s_pab")
            s_scan = semp("s_scan")
            s_den = semp("s_den")
            s_num = semp("s_num")
            s_rec = semp("s_rec")
            s_y = semp("s_y")
            s_yT = semp("s_yT")
            s_x1 = semp("s_x1")
            s_z2 = semp("s_z2")
            s_z2T = semp("s_z2T")
            s_zt = semp("s_zt")
            s_gu = semp("s_gu")
            s_th = semp("s_th")
            s_h = primed("s_h")
            s_dn = primed("s_dn")
            s_x2 = primed("s_x2")

            WB = [bank[4], bank[5]]
            DB = [bank[6], bank[7]]
            after_wkv = []

            def pe_wkv_in(pe, g, h):
                n = 2 * g + h
                if h == 0:
                    pe.wait_ge(s_z1, g + 1)
                    pe.wait_ge(s_c, 16 * (g + 1))
                    pe.wait_ge(s_x1, 2 * g)
                pe.wait_ge(s_exp, 2 * n)
                for b in range(GB):
                    last = pe.transpose(WB[0][:, b * P:(b + 1) * P], Z1[:, b, h * P:(h + 1) * P], ident[:])
                last.then_inc(s_kT, 1)
                pe.wait_ge(s_pab, 2 * n)
                for b in range(GB):
                    last = pe.transpose(WB[1][:, b * P:(b + 1) * P], CV[:, b, h * P:(h + 1) * P], ident[:])
                last.then_inc(s_vT, 1)

            def act_exps(act, g, h):
                act.wait_ge(s_kT, 2 * g + h + 1)
                act.wait_ge(s_y, 2 * g)
                kT = WB[0][:, :].rearrange("p (b t) -> p b t", b=GB)
                act.activation(EB[:, h, :, 1:P], kT[:, :, 1:P], ACT.Exp, bias=uneg[:, h:h + 1]).then_inc(s_exp, 1)
                act.activation(EA[:, h, :, 1:P], kT[:, :, 0:P - 1], ACT.Exp, bias=upos[:, h:h + 1]).then_inc(s_exp, 1)

            def dve_products(dve, g, h):
                n = 2 * g + h
                vT = WB[1][:, :].rearrange("p (b t) -> p b t", b=GB)
                dve.wait_ge(s_vT, 1 + n + 1)
                dve.wait_ge(s_exp, 2 * n + 2)
                dve.wait_ge(s_y, 2 * g)
                dve.tensor_tensor(PA[:, h, :, 1:P], EA[:, h, :, 1:P], vT[:, :, 0:P - 1], ALU.mult).then_inc(s_pab, 1)
                dve.tensor_tensor(PB[:, h, :, :], EB[:, h, :, :], vT, ALU.mult).then_inc(s_pab, 1)

            def dve_scans(dve, g, h):
                n = 2 * g + h
                flat = lambda t: t[:, h, :, :].rearrange("p b t -> p (b t)")
                dve.tensor_tensor_scan(out=SB[:, h, :], data0=DEC[:, h, :], data1=flat(EA), initial=0.0,
                                       op0=ALU.mult, op1=ALU.add).then_inc(s_scan, 1)
                dve.wait_ge(s_pab, 2 * n + 1)
                dve.tensor_tensor_scan(out=SA[:, h, :], data0=DEC[:, h, :], data1=flat(PA), initial=0.0,
                                       op0=ALU.mult, op1=ALU.add).then_inc(s_scan, 1)

            def pool_sums(pool, g, h):
                n = 2 * g + h
                flat = lambda t: t[:, h, :, :].rearrange("p b t -> p (b t)")
                pool.wait_ge(s_scan, 2 * n + 1)
                pool.tensor_tensor(DEN[:, h, :], SB[:, h, :], flat(EB), ALU.add).then_inc(s_den, 1)
                pool.wait_ge(s_scan, 2 * n + 2)
                pool.tensor_tensor(NUM[:, h, :], SA[:, h, :], flat(PB), ALU.add).then_inc(s_num, 1)

            def dve_recip(dve, g, h):
                dve.wait_ge(s_den, 2 * g + h + 1)
                dve.reciprocal(DEN[:, h, :], DEN[:, h, :]).then_inc(s_rec, 1)

            def pool_quot(pool, g, h):
                n = 2 * g + h
                pool.wait_ge(s_rec, n + 1)
                pool.wait_ge(s_num, n + 1)
                pool.wait_ge(s_yT, 2 * g)
                pool.tensor_tensor(Y[:, h, :], NUM[:, h, :], DEN[:, h, :], ALU.mult).then_inc(s_y, 1)

            def pe_wkv_out(pe, g):
                pe.wait_ge(s_y, 2 * g + 2)
                for k in range(2):
                    for b in range(2):
                        for h in range(2):
                            i = 2 * k + b
                            last = pe.transpose(WB[k][:, b * C + h * P:b * C + (h + 1) * P],
                                                Y[:, h, i * P:(i + 1) * P], ident[:])
                    last.then_inc(s_yT, 1)

            def dve_x1(dve, g):
                for k in range(2):
                    dve.wait_ge(s_yT, 2 * g + k + 1)
                    xs = X[:, bass.ds(GB * g + 2 * k, 2), :].rearrange("p b c -> p (b c)")
                    dve.scalar_tensor_tensor(out=xs, in0=WB[k][:, :], scalar=tg[:, 0:1], in1=xs,
                                             op0=ALU.mult, op1=ALU.add).then_inc(s_x1, 1)

            CH1 = 2 * LN_STEPS(GB) + NI
            xt_tile = lambda g: (lambda i: X[:, bass.ds(GB * g + i, 1), :].rearrange("p b c -> p (b c)"))

            def dve_ln1(dve, ch, g):
                dve.wait_ge(s_x, 16 * (g + 1))
                dve.wait_ge(s_kT, 2 * g)
                layer_norm_steps(ch, xt_tile(g), lambda i: Z1[:, i, :], GB, s_var1, s_rstd1, 2 * g + 1)\
                    .then_inc(s_z1, 1)

            def dve_ln2(dve, ch, g):
                dve.wait_ge(s_x1, 2 * g + 2)
                dve.wait_ge(s_z2T, 2 * g)
                alone(dve)
                layer_norm_steps(ch, xt_tile(g), lambda i: Z2[:, i, :], GB, s_var1, s_rstd1, 2 * g + 2)\
                    .then_inc(s_z2, 1)

            def pe_z2T(pe, g):
                pe.wait_ge(s_z2, g + 1)
                pe.wait_ge(s_h, 1 + NI * g)
                for h in range(2):
                    for b in range(GB):
                        last = pe.transpose(bank[h][:, b * P:(b + 1) * P], Z2[:, b, h * P:(h + 1) * P], ident[:])
                    last.then_inc(s_z2T, 1)

            def act_zt(act, g):
                for h in range(2):
                    act.wait_ge(s_z2T, 2 * g + h + 1)
                    act.activation(ZT[:, h, :], bank[h][:, :], ACT.Copy).then_inc(s_zt, 1)

            def pe_gu(pe, g, i, sides=(0, 1)):
                m = width(i, INTER)
                for side in sides:
                    if i == 0 and side == 0:
                        pe.wait_ge(s_zt, 2 * g + 2)
                    if i >= 2 and side == 0:
                        pe.wait_ge(s_h, 1 + NI * g + i - 1)
                    for h in range(2):
                        last = pe.matmul(bank[2 * (i % 2) + side][0:m, :], (gw, uw)[side][:, h, i * P:i * P + m],
                                         ZT[:, h, :], start=(h == 0), stop=(h == 1))
                    if side == 1:
                        last.then_inc(s_gu, 1)

            def act_tanh(act, g, i):
                m = width(i, INTER)
                act.wait_ge(s_gu, NI * g + i + 1)
                act.activation(TH[0:m, i % 2, :], bank[2 * (i % 2)][0:m, :], ACT.Tanh,
                               scale=hgs[0:m, i:i + 1]).then_inc(s_th, 1)

            def dve_h1(dve, ch, g, i):
                m = width(i, INTER)
                dve.wait_ge(s_th, NI * g + i + 1)
                ch.do(dve.scalar_tensor_tensor(out=H1[0:m, i % 2, :], in0=TH[0:m, i % 2, :], scalar=1.0,
                                               in1=bank[2 * (i % 2)][0:m, :], op0=ALU.add, op1=ALU.mult))

            def dve_h(dve, ch, g, i):
                m = width(i, INTER)
                if i == 0:
                    dve.wait_ge(s_dn, 1 + 2 * g)
                ch.wait()
                dve.scalar_tensor_tensor(out=H[0:m, i, :], in0=H1[0:m, i % 2, :], scalar=hgu[0:m, i:i + 1],
                                         in1=bank[2 * (i % 2) + 1][0:m, :], op0=ALU.mult,
                                         op1=ALU.mult).then_inc(s_h, 1)

            def pe_down(pe, g, t, DB, between=None):
                if t == 0:
                    pe.wait_ge(s_h, 1 + NI * g + NI)
                    pe.wait_ge(s_x2, 1 + 2 * g)
                for i in range(NI):
                    m = width(i, INTER)
                    last = pe.matmul(DB[t // 2][:, (t % 2) * C:(t % 2 + 1) * C], H[0:m, i, t * P:(t + 1) * P],
                                     dw[0:m, i, :], start=(i == 0), stop=(i == NI - 1))
                    if between and i % 2 == 0:
                        between()
                if t % 2 == 1:
                    last.then_inc(s_dn, 1)

            def dve_x2(dve, g, DB, ks=(0, 1)):
                for k in ks:
                    dve.wait_ge(s_dn, 1 + 2 * g + k + 1)
                    xs = X[:, bass.ds(GB * g + 2 * k, 2), :].rearrange("p b c -> p (b c)")
                    dve.scalar_tensor_tensor(out=xs, in0=DB[k][:, :], scalar=tg[:, 2:3], in1=xs,
                                             op0=ALU.mult, op1=ALU.add).then_inc(s_x2, 1)

            N_SMALL, N_ROWS, N_ZERO = 13, 9, SLOTS // P // 2
            with nc.Block() as block:
                @block.sync
                def _(sp):
                    for primed_sem in at_one:
                        sp.sem_inc(primed_sem, 1)

                    def load_x(g):
                        sp.dma_start(X[:, bass.ds(GB * g, GB), :], xt[:, bass.ds(GB * g, GB), :]).then_inc(s_x, 16)

                    def load_ctx(g):
                        sp.dma_start(CV[:, :, :], ct[:, bass.ds(GB * g, GB), :]).then_inc(s_c, 16)

                    small = [(gates[:, 0:2], g_xattn.partition_broadcast(P)), (gates[:, 2:4], g_ffn.partition_broadcast(P)),
                             (td[:], time_decay), (tf[:], time_first),
                             (gs[:, 0:NI - 1], gate_s[0:(NI - 1) * P].rearrange("(i p) -> p i", p=P)),
                             (us[:, 0:NI - 1], up_s[0:(NI - 1) * P].rearrange("(i p) -> p i", p=P)),
                             (gs[0:width(NI - 1, INTER), NI - 1:NI],
                              gate_s[(NI - 1) * P:INTER].rearrange("(p a) -> p a", a=1)),
                             (us[0:width(NI - 1, INTER), NI - 1:NI],
                              up_s[(NI - 1) * P:INTER].rearrange("(p a) -> p a", a=1)),
                             (dsb[:], down_s.partition_broadcast(P)), (bvb[:], bv.partition_broadcast(P)),
                             (bqk[:, 0:1], bq), (bqk[:, 1:2], bk), (wq[:], wqT)]
                    assert len(small) == N_SMALL
                    with nc.allow_non_contiguous_dma(reason="small vectors"):
                        sp.dma_start(mrow[:], mask).then_inc(s_mask, 16)
                        load_x(0)
                        for dst, src in small:
                            sp.dma_start(dst, src).then_inc(s_ld, 16)
                        load_ctx(0)
                    sp.dma_start(gw[:, :, :], gate_wT.rearrange("(h p) i -> p h i", p=P)).then_inc(s_wts, 16)
                    sp.dma_start(uw[:, :, :], up_wT.rearrange("(h p) i -> p h i", p=P)).then_inc(s_wts, 16)
                    n5 = (NI - 1) * P
                    sp.dma_start(dw[:, 0:NI - 1, :], down_wT[0:n5, :].rearrange("(i p) c -> p i c", p=P)).then_inc(s_wts, 16)
                    sp.dma_start(dw[0:INTER - n5, NI - 1, :], down_wT[n5:INTER, :]).then_inc(s_wts, 16)
                    for dst, src in ((wk[:], wkT), (wv[:], wvT),
                                     (wgt[:, :, :], Wg.rearrange("(h p) e -> p h e", p=P)),
                                     (wsh1[:, :, :], sw1.rearrange("(h p) e -> p h e", p=P)),
                                     (wsh3[:, :, :], sw3.rearrange("(h p) e -> p h e", p=P)),
                                     (wsh2[:, 0:2, :], sw2[0:2 * P, :].rearrange("(i p) c -> p i c", p=P)),
                                     (wsh2[0:EH - 2 * P, 2, :], sw2[2 * P:EH, :])):
                        sp.dma_start(dst, src).then_inc(s_late, 16)
                    with sp.Fori(1, NG) as g:
                        sp.wait_ge(s_vT, 1 + 2 * g)
                        load_x(g)
                        load_ctx(g)
                    sp.wait_ge(s_mp, 1)
                    every = lambda part, n: mparts[:, part[0], part[1], :].unsqueeze(1).broadcast_to([B, n, T])
                    rows = [(qrow_scr[:, 0:3, :], every((0, 0), 3)), (qrow_scr[:, 3:5, :], every((0, 1), 2)),
                            (qrow_scr[:, 5:6, :], every((0, 2), 1)), (qrow_scr[:, 6:9, :], mparts[:, 1, :, :]),
                            (qrow_scr[:, 9:12, :].rearrange("b r t -> b (r t)"), zeros[0:B, 0:3 * T // 2].bitcast(bf16)),
                            (krow_scr[:, 0:3, :], mparts[:, 2, :, :]), (krow_scr[:, 3:5, :], mparts[:, 2, 0:2, :]),
                            (krow_scr[:, 5:6, :], every((2, 0), 1)), (krow_scr[0, 6:12, :], onesb[:])]
                    assert len(rows) == N_ROWS
                    for dst, src in rows:
                        sp.dma_start(dst, src).then_inc(s_mst, 16)
                    dz = dispatched[0:SLOTS, :].rearrange("(p a b) c -> a p (b c)", p=P, b=2)
                    for a in range(N_ZERO):
                        sp.dma_start(dz[a], zeros[:, :]).then_inc(s_zero, 16)
                    sp.wait_ge(s_mst, 16 * N_ROWS)
                    sp.wait_ge(s_zero, 16 * N_ZERO)

                @block.scalar
                def _(act):
                    act.wait_ge(s_ld, 16 * N_SMALL)
                    act.activation(tg[:], gates[:], ACT.Tanh).then_inc(s_act0, 1)
                    act.activation(tdx[:], td[:], ACT.Exp).then_inc(s_act0, 1)
                    act.wait_ge(s_act0, 2)
                    act.activation(decay[:], tdx[:], ACT.Exp, scale=-1.0).then_inc(s_act0, 1)
                    act.wait_ge(s_dv0, 2)
                    act.wait_ge(s_pool0, 5)
                    act_exps(act, 0, 0)
                    act_exps(act, 0, 1)
                    act.wait_ge(s_dv0, 4)
                    with act.Fori(0, NG - 1) as g:
                        act_zt(act, g)
                        for i in range(NI):
                            act_tanh(act, g, i)
                            if i < 2:
                                act_exps(act, g + 1, i)
                    act.wait_ge(s_late, 16 * 7)

                @block.gpsimd
                def _(pool):
                    pool.memset(neghalf[:], -0.5).then_inc(s_pool0, 1)
                    pool.memset(ident[:], 0.0).then_inc(s_pool0, 1)
                    pool.memset(EA[:, :, :, 0:1], 0.0).then_inc(s_pool0, 1)
                    pool.memset(EB[:, :, :, 0:1], 1.0).then_inc(s_pool0, 1)
                    pool.memset(PA[:, :, :, 0:1], 0.0).then_inc(s_pool0, 1)
                    pool.memset(steps01[:, :, 0:1], 0.0).then_inc(s_pool0, 1)
                    pool.memset(steps01[:, :, 1:P], 1.0).then_inc(s_pool0, 1)
                    pool.memset(zeros[:], 0.0).then_inc(s_pool0, 1)
                    pool.memset(onesb[:], 1.0).then_inc(s_pool0, 1)
                    pool.wait_ge(s_pool0, 9)
                    pool.affine_select(out=ident[:], in_=ident[:], compare_op=ALU.not_equal, fill=1.0, base=0,
                                       pattern=[[-1, P]], channel_multiplier=1).then_inc(s_id, 1)
                    power_step(pool, GB, s_var1, s_rstd1, 1)
                    for h in range(2):
                        pool_sums(pool, 0, h)
                        pool_quot(pool, 0, h)
                    power_step(pool, GB, s_var1, s_rstd1, 2)
                    with pool.Fori(0, NG - 1) as g:
                        power_step(pool, GB, s_var1, s_rstd1, 2 * g + 3)
                        for h in range(2):
                            pool_sums(pool, g + 1, h)
                            pool_quot(pool, g + 1, h)
                        power_step(pool, GB, s_var1, s_rstd1, 2 * g + 4)

                @block.tensor
                def _(pe):
                    pe.wait_ge(s_id, 1)
                    pe.wait_ge(s_mask, 16)
                    for h in range(2):
                        last = pe.transpose(bank[7][:, h * B:(h + 1) * B], mrow[:, h * P:(h + 1) * P], ident[0:B, 0:B])
                    last.then_inc(s_mT, 1)
                    for h in range(2):
                        pe_wkv_in(pe, 0, h)
                    pe_wkv_out(pe, 0)
                    pe.wait_ge(s_wts, 64)
                    pe.wait_ge(s_dv0, 6)
                    pe.wait_ge(s_mT2, 1)
                    with pe.Fori(0, NG - 1) as g:
                        pe_z2T(pe, g)
                        for i in range(NI):
                            pe_gu(pe, g, i)
                            if i < 2:
                                pe_wkv_in(pe, g + 1, i)
                        for t in range(GB):
                            if t == 1:
                                pe_wkv_out(pe, g + 1)
                            pe_down(pe, g, t, DB)

                @block.vector
                def _(dve):
                    ch = Chain(dve, s_dvech)
                    dve.wait_ge(s_mask, 16)
                    for j, (mul, add) in enumerate(((-NEG, 0.0), (NEG, -NEG), (-1.0, 1.0))):
                        ch.do(dve.tensor_scalar(mtmp[:, j, :], mrow[:], mul, add, ALU.mult, ALU.add))

                    def mask_part(r):
                        ch.wait()
                        last = dve.tensor_copy(mparts[:, :, r, :], mtmp[:, :, :])
                        if r == 2:
                            last.then_inc(s_mp, 1)
                            return
                        ch.do(last)
                        ch.wait()
                        ch.do(dve.tensor_tensor(mtmp[:, :, :], mtmp[:, :, :], mparts[:, :, r, :], ALU.subtract))

                    mask_part(0)
                    dve_ln1(dve, ch, 0)
                    dve.wait_ge(s_ld, 16 * N_SMALL)
                    dve.tensor_scalar(upos[:], tf[:], 0.0, -1.0, ALU.max, ALU.mult).then_inc(s_dv0, 1)
                    dve.tensor_scalar(uneg[:], tf[:], 0.0, None, ALU.min).then_inc(s_dv0, 1)
                    m = width(NI - 1, INTER)
                    for lo, hi, q in ((0, NI - 1, P), (NI - 1, NI, m)):
                        dve.tensor_scalar(hgs[0:q, lo:hi], gs[0:q, lo:hi], 0.5, None, ALU.mult).then_inc(s_dv0, 1)
                    dve.wait_ge(s_dv0, 4)
                    for lo, hi, q in ((0, NI - 1, P), (NI - 1, NI, m)):
                        ch.do(dve.tensor_tensor(hgu[0:q, lo:hi], hgs[0:q, lo:hi], us[0:q, lo:hi], ALU.mult))
                    dve.wait_ge(s_act0, 3)
                    dve.wait_ge(s_pool0, 9)
                    for h in range(2):
                        ch.do(dve.tensor_scalar(DEC[:, h, :], steps01[:, :, :].rearrange("p b t -> p (b t)"),
                                                decay[:, h:h + 1], None, ALU.mult))
                    ch.wait()
                    for h in range(2):
                        dve_products(dve, 0, h)
                        dve_scans(dve, 0, h)
                    for h in range(2):
                        dve_recip(dve, 0, h)
                    mask_part(1)
                    dve_x1(dve, 0)
                    dve_ln2(dve, ch, 0)
                    mask_part(2)
                    dve.wait_ge(s_mT, 1)
                    dve.tensor_copy(maskT[:, :, :].rearrange("p h b -> p (h b)"), bank[7][:, 0:2 * B]).then_inc(s_mT2, 1)
                    dve.wait_ge(s_wts, 64)
                    dve.tensor_tensor(dw[:, 0:NI - 1, :], dw[:, 0:NI - 1, :],
                                      dsb[:, :].unsqueeze(1).broadcast_to([P, NI - 1, C]), ALU.mult).then_inc(s_dv0, 1)
                    dve.tensor_tensor(dw[0:m, NI - 1, :], dw[0:m, NI - 1, :], dsb[0:m, :], ALU.mult).then_inc(s_dv0, 1)
                    ch.do(dve.tensor_scalar(wq[:], wq[:], HD ** -0.5, None, ALU.mult))
                    ch.do(dve.tensor_scalar(bqk[:, 0:1], bqk[:, 0:1], HD ** -0.5, None, ALU.mult))
                    before = ch.n
                    with dve.Fori(0, NG - 1) as g:
                        ch = Chain(dve, s_dvech, before + CH1 * g)
                        dve_ln1(dve, ch, g + 1)
                        for i in range(NI):
                            dve_h1(dve, ch, g, i)
                            dve_h(dve, ch, g, i)
                            if i < 2:
                                dve_products(dve, g + 1, i)
                                dve_scans(dve, g + 1, i)
                            elif i < 4:
                                dve_recip(dve, g + 1, i - 2)
                        dve_x1(dve, g + 1)
                        dve_ln2(dve, ch, g + 1)
                        dve_x2(dve, g, DB)
                        assert ch.n == CH1
                    after_wkv.append(before + CH1 * (NG - 1))
                    dve.wait_ge(s_x2, 1 + 2 * (NG - 1))

            wkv.close()

            with ExitStack() as att:
                def sbp(name, shape, dt=fp32):
                    return sb(name, shape, dt, att)

                def semp(name):
                    return sem(name, att)

                NS = GB
                QA = sbp("QA", [P, NS, HEADS, T], bf16)
                KA = sbp("KA", [P, NS, HEADS, T], bf16)
                VP = sbp("VP", [P, NS, 2, HEADS, 32])
                CX = sbp("CX", [P, NS, T])
                MB = sbp("MB", [P, NS, T])
                Z3 = sbp("Z3", [P, T])
                QK = sbp("QK", [P, 2 * T])
                PARTS = sbp("PARTS", [P, 6, T], bf16)
                VF = sbp("VF", [P, 2, P])
                MX = sbp("MX", [P, 2, HEADS, 2])
                NM = sbp("NM", [2 * HEADS, P])
                NP = sbp("NP", [2 * HEADS, 3, P], bf16)
                AV = sbp("AV", [P, 2, T])
                RD = sbp("RD", [P, 2, 4, 4])
                YA = sbp("YA", [P, 2, P])

                a_init = semp("a_init")
                a_zero = semp("a_zero")
                a_ones = [semp(f"a_ones{k}") for k in range(NS)]
                a_cx = [semp(f"a_cx{k}") for k in range(NS)]
                a_qa = [semp(f"a_qa{k}") for k in range(NS)]
                a_mx = [semp(f"a_mx{k}") for k in range(NS)]
                a_dve = semp("a_dve")
                a_pool = semp("a_pool")
                a_var = semp("a_var")
                a_rstd = semp("a_rstd")
                a_z3 = semp("a_z3")
                a_proj = semp("a_proj")
                a_qk = semp("a_qk")
                a_part = semp("a_part")
                a_rest = semp("a_rest")
                a_scr = semp("a_scr")
                a_mscr = semp("a_mscr")
                a_vps = semp("a_vps")
                a_vf = semp("a_vf")
                a_vp = semp("a_vp")
                a_s = semp("a_s")
                a_red = semp("a_red")
                a_mxT = semp("a_mxT")
                a_nm = semp("a_nm")
                a_np = semp("a_np")
                a_st = semp("a_st")
                a_exp = semp("a_exp")
                a_pv = semp("a_pv")
                a_av = semp("a_av")
                a_yT = semp("a_yT")
                a_ya = semp("a_ya")
                a_yo = semp("a_yo")
                a_x3 = semp("a_x3")

                SBK = [bank[0], bank[1]]
                TBK = [psum[:, 2 * 512:4 * 512], psum[:, 4 * 512:6 * 512]]
                PVB, MISC = bank[6], bank[7]
                PT = HP[:, :, :].rearrange("p (a s q) (r t) -> p a s (q r) t", a=2, s=2, r=2)
                AHEAD_S, AHEAD_V, AHEAD_Q = 2, 3, 4
                TURN = 6

                def xb(b):
                    return X[:, bass.ds(b, 1), :].rearrange("p b c -> p (b c)")

                def at(g, k, ahead):
                    return g + (k + ahead) // GB, (k + ahead) % GB

                def later(count):
                    return not isinstance(count, int) or count > 0

                def pe_proj(pe, g, k):
                    pe.wait_ge(a_z3, GB * g + k + 1)
                    pe.wait_ge(a_cx[k], 32 * (g + 1))
                    pe.matmul(MISC[:, 0:T], wq[:], Z3[:], start=True, stop=True)
                    pe.matmul(MISC[:, T:2 * T], wk[:], CX[:, k, :], start=True, stop=True).then_inc(a_proj, 1)

                def pe_v(pe, k):
                    for st in range(2):
                        last = pe.matmul(MISC[:, st * P:(st + 1) * P], CX[:, k, st * P:(st + 1) * P], wv[:],
                                         start=True, stop=True)
                    last.then_inc(a_vps, 1)

                def pe_scores(pe, g, k, p, SBK=SBK):
                    b = GB * g + k
                    if p == 0:
                        pe.wait_ge(a_qa[k], 16 * N_FILL * (g + 1))
                    for h in (2 * p, 2 * p + 1):
                        if later(HEADS * b + h - 1):
                            pe.wait_ge(a_red, HEADS * b + h - 1)
                        for tt in range(2):
                            last = pe.matmul(SBK[h % 2][:, tt * T:(tt + 1) * T], QA[:, k, h, tt * P:(tt + 1) * P],
                                             KA[:, k, h, :], start=True, stop=True)
                        last.then_inc(a_s, 1)

                def pe_mxT(pe, g, k):
                    pe.wait_ge(a_red, HEADS * (GB * g + k + 1))
                    pe.transpose(MISC[0:2 * HEADS, 0:P], MX[:, k % 2, :, :].rearrange("p h t -> p (h t)"),
                                 ident[:]).then_inc(a_mxT, 1)

                def pe_scoresT(pe, g, k, i, st):
                    n = 8 * (GB * g + k) + 2 * i + st
                    if i == 0 and st == 0:
                        pe.wait_ge(a_mx[k], 16 * (g + 1))
                    if later(n - 1):
                        pe.wait_ge(a_exp, n - 1)
                    for j in range(4):
                        h = 4 * j + i
                        last = pe.matmul(TBK[st][:, j * T:(j + 1) * T],
                                         KA[:, k, h, st * P:(st + 1) * P], QA[:, k, h, :], start=True, stop=True)
                    last.then_inc(a_st, 1)

                def pe_pv(pe, g, k, i, st):
                    b = GB * g + k
                    if i == 0 and st == 0:
                        pe.wait_ge(a_vp, b + 1)
                        if later(b):
                            pe.wait_ge(a_av, b)
                    grp = 0 if i < 3 else 1
                    pe.wait_ge(a_exp, 8 * b + 2 * i + st + 1)
                    for j in range(4):
                        last = pe.matmul(PVB[32 * j:32 * j + 32, grp * T:(grp + 1) * T],
                                         VP[:, k, st, 4 * j + i, :], PT[:, i % 2, st, j, :],
                                         start=(i in (0, 3) and st == 0), stop=(i in (2, 3) and st == 1))
                    last.then_inc(a_pv, 1)

                def pe_yT(pe, b):
                    pe.wait_ge(a_av, b + 1)
                    for tt in range(2):
                        for grp in range(2):
                            last = pe.transpose(MISC[:, (2 * tt + grp) * P:(2 * tt + grp + 1) * P],
                                                AV[:, grp, tt * P:(tt + 1) * P], ident[:])
                    last.then_inc(a_yT, 1)

                def pe_yo(pe, b):
                    pe.wait_ge(a_ya, b + 1)
                    for tt in range(2):
                        last = pe.transpose(MISC[:, tt * P:(tt + 1) * P], YA[:, tt, :], ident[:])
                    last.then_inc(a_yo, 1)

                def dve_stats(dve, ch, b, step):
                    if step == 0:
                        ch.do(dve.bn_stats(stats[:, 0, :], xb(b)))
                    elif step == 1:
                        ch.wait()
                        alone(dve)
                        ch.do(dve.bn_aggr(mv[:, 0, :], stats[:, 0, :]))
                    else:
                        ch.wait()
                        dve.tensor_scalar(veps[:, 0:1], mv[:, 0:1, 1], EPS, None, ALU.add).then_inc(a_var, 1)

                LN_COUNT = lambda b: 1 if isinstance(b, int) and b < GB else b - 2

                def dve_z3(dve, b):
                    n = b if isinstance(b, int) and b < GB else 0
                    dve.wait_ge(a_rstd, LN_COUNT(b))
                    if later(b):
                        dve.wait_ge(a_proj, b)
                    dve.tensor_scalar(Z3[:], xb(b), mv[:, n, 0:1], rstd[:, n:n + 1], ALU.subtract, ALU.mult).then_inc(a_z3, 1)

                def dve_qk(dve, g, k):
                    b = GB * g + k
                    dve.wait_ge(a_proj, b + 1)
                    dve.wait_ge(a_cx[k], 32 * (g + 1))
                    if later(b):
                        dve.wait_ge(a_rest, 2 * b)
                    for c in range(2):
                        dve.scalar_tensor_tensor(out=QK[:, c * T:(c + 1) * T], in0=MISC[:, c * T:(c + 1) * T],
                                                 scalar=bqk[:, c:c + 1], in1=MB[:, k, :], op0=ALU.add,
                                                 op1=ALU.mult).then_inc(a_qk, 1)

                def dve_vf(dve, b):
                    dve.wait_ge(a_vps, b + 1)
                    if later(b):
                        dve.wait_ge(a_vp, b)
                    dve.tensor_tensor(VF[:, :, :], MISC[:, 0:T].rearrange("p (s c) -> p s c", s=2),
                                      bvb[:, :].unsqueeze(1).broadcast_to([P, 2, P]), ALU.add).then_inc(a_vf, 1)

                def dve_reduce(dve, g, k, h, SBK=SBK):
                    b, par = GB * g + k, k % 2
                    if h == 0 and later(b - 1):
                        dve.wait_ge(a_mxT, b - 1)
                    dve.wait_ge(a_s, HEADS * b + h + 1)
                    dve.tensor_reduce(MX[:, par, h, :], SBK[h % 2][:, :].rearrange("p (a s) -> p a s", a=2),
                                      axis=AX.X, op=ALU.max).then_inc(a_red, 1)

                yt = MISC[:, :].rearrange("p (t g c) -> p t g c", t=2, g=2)

                def dve_sums(dve, ch, b):
                    dve.wait_ge(a_yT, b + 1)
                    den_a = yt[:, :, 0, :].rearrange("p t (j r) -> p t j r", j=4)[:, :, :, 0:27]\
                        .rearrange("p t j (i r) -> p t j i r", r=9)[:, :, :, :, 8]
                    den_b = yt[:, :, 1, :].rearrange("p t (j r) -> p t j r", j=4)[:, :, :, 8]
                    ch.do(dve.reciprocal(RD[:, :, :, 3], den_b))
                    for tt in range(2):
                        ch.do(dve.reciprocal(RD[:, tt, :, 0:3], den_a[:, tt]))

                def dve_factors(dve, ch, b):
                    ch.wait()
                    for tt in range(2):
                        rd = RD[:, tt, :, :].rearrange("p j i -> p (j i)")
                        ch.do(dve.tensor_scalar(rd, rd, maskT[:, tt, bass.ds(b, 1)], tg[:, 1:2], ALU.mult, ALU.mult))

                def dve_y(dve, ch, b):
                    ch.wait()
                    for tt in range(2):
                        dst = YA[:, tt, :].rearrange("p (j i d) -> p j i d", j=4, i=4)
                        src = yt[:, tt, 0, :].rearrange("p (j r) -> p j r", j=4)[:, :, 0:27]\
                            .rearrange("p j (i r) -> p j i r", r=9)[:, :, :, 0:8]
                        ch.do(dve.tensor_tensor(dst[:, :, 0:3, :], src,
                                                RD[:, tt, :, 0:3].unsqueeze(3).broadcast_to([P, 4, 3, 8]), ALU.mult))
                    dst = YA[:, :, :].rearrange("p t (j i d) -> p t j i d", j=4, i=4)[:, :, :, 3, :]
                    src = yt[:, :, 1, :].rearrange("p t (j r) -> p t j r", j=4)[:, :, :, 0:8]
                    dve.tensor_tensor(dst, src, RD[:, :, :, 3].unsqueeze(3).broadcast_to([P, 2, 4, 8]), ALU.mult)\
                        .then_inc(a_ya, 1)

                def dve_x3(dve, b):
                    dve.wait_ge(a_yo, b + 1)
                    dve.tensor_tensor(xb(b), xb(b), MISC[:, 0:T], ALU.add).then_inc(a_x3, 1)

                def part_of(r):
                    return PARTS[:, r:6 - r:5 - 2 * r, :]

                QK2 = QK[:, :].rearrange("p (c t) -> p c t", c=2)

                def act_part(act, b, r):
                    if r == 0:
                        act.wait_ge(a_qk, 2 * b + 2)
                        if later(b):
                            act.wait_ge(a_scr, 16 * b)
                    else:
                        act.wait_ge(a_rest, 2 * b + 1)
                    act.activation(part_of(r), QK2, ACT.Copy).then_inc(a_part, 1)

                def act_nm(act, b):
                    act.wait_ge(a_mxT, b + 1)
                    if later(b):
                        act.wait_ge(a_np, b)
                    act.activation(NM[:], MISC[0:2 * HEADS, 0:P], ACT.Copy, scale=-1.0).then_inc(a_nm, 1)

                def act_exp(act, g, k, i, st):
                    n = 8 * (GB * g + k) + 2 * i + st
                    act.wait_ge(a_st, n + 1)
                    if later(n - 3):
                        act.wait_ge(a_pv, n - 3)
                    act.activation(PT[:, i % 2, st, :, :].rearrange("p j t -> p (j t)"), TBK[st], ACT.Exp)\
                        .then_inc(a_exp, 1)

                def act_av(act, b):
                    act.wait_ge(a_pv, 8 * b + 8)
                    act.activation(AV[:, :, :].rearrange("p a t -> p (a t)"), PVB[:, :], ACT.Copy).then_inc(a_av, 1)

                def pool_rest(pool, b, r):
                    pool.wait_ge(a_part, 2 * b + r + 1)
                    pool.tensor_tensor(QK2 if r == 0 else part_of(2), QK2, part_of(r), ALU.subtract).then_inc(a_rest, 1)

                def pool_vp(pool, g, k):
                    b = GB * g + k
                    pool.wait_ge(a_vf, b + 1)
                    if later(b - 3):
                        pool.wait_ge(a_pv, 8 * (b - 3))
                    for st in range(2):
                        for i in range(4):
                            lo = 9 * i if i < 3 else 0
                            dst = VP[:, k, st, :, :].rearrange("p (j i) c -> p j i c", i=4)[:, :, i, lo:lo + 8]
                            src = VF[:, st, :].rearrange("p (j i d) -> p j i d", j=4, i=4)[:, :, i, :]
                            last = pool.tensor_tensor(dst, src, maskT[:, st, bass.ds(b, 1)].unsqueeze(2)
                                                      .broadcast_to([P, 4, 8]), ALU.mult)
                    last.then_inc(a_vp, 1)

                def pool_np(pool, pch, b):
                    pool.wait_ge(a_nm, b + 1)
                    if later(b):
                        pool.wait_ge(a_mscr, 16 * b)
                    nil = zeros[0:2 * HEADS, 0:P]
                    for r in range(2):
                        if r > 0:
                            pch.wait()
                        pch.do(pool.tensor_tensor(NP[:, r, :], NM[:], nil, ALU.add))
                        pch.wait()
                        last = pool.tensor_tensor(NM[:] if r == 0 else NP[:, 2, :], NM[:], NP[:, r, :], ALU.subtract)
                        if r == 0:
                            pch.do(last)
                    last.then_inc(a_np, 1)

                NP_STEPS = 3

                N_FILL = 8

                def sp_ctx(sp, g, k):
                    sp.dma_start(CX[:, k, :], ctx[bass.ds(GB * g + k, 1), :, :].rearrange("b p c -> (b p) c")).then_inc(a_cx[k], 16)
                    sp.dma_start(MB[:, k, :], mask[bass.ds(GB * g + k, 1), :].broadcast_to([P, T])).then_inc(a_cx[k], 16)

                def sp_rows(sp, g, k):
                    b = GB * g + k
                    if later(b - 3):
                        sp.wait_ge(a_st, 8 * (b - 3))
                        alone(sp)
                    rows = lambda scr_, n: scr_[bass.ds(b, 1), 0:n, :].rearrange("b r t -> (b r) t").unsqueeze(1)\
                        .broadcast_to([n, HEADS, T])
                    sp.dma_start(QA[48:60, k, :, :], rows(qrow_scr, 12)).then_inc(a_qa[k], 16)
                    sp.dma_start(KA[48:54, k, :, :], rows(krow_scr, 6)).then_inc(a_qa[k], 16)

                def sp_store(sp, g, k):
                    b = GB * g + k
                    sp.wait_ge(a_rest, 2 * b + 2)
                    alone(sp)
                    if later(b - 1):
                        gg, kk = at(g, k, -2)
                        sp.wait_ge(a_qa[kk], 16 * N_FILL * (gg + 1))
                    sp.dma_start(stack_scr[k % 2].rearrange("r c t -> c r t"), PARTS[:, :, :]).then_inc(a_scr, 16)

                def sp_fill(sp, g, k):
                    sp.wait_ge(a_scr, 16 * (GB * g + k + 1))
                    alone(sp)
                    scr = stack_scr[k % 2]
                    for dst, parts, row in ((QA, (0, 3), 0), (KA, (3, 6), 0), (QA, (0, 2), 24), (KA, (4, 6), 24),
                                            (QA, (0, 1), 40), (KA, (5, 6), 40)):
                        lo, hi = parts
                        sp.dma_start(dst[row:row + HD * (hi - lo), k, :, :],
                                     scr[lo:hi, :, :].rearrange("r (d h) t -> (r d) h t", d=HD)).then_inc(a_qa[k], 16)

                def sp_max_store(sp, g, k):
                    b = GB * g + k
                    sp.wait_ge(a_np, b + 1)
                    alone(sp)
                    if later(b - 1):
                        gg, kk = at(g, k, -2)
                        sp.wait_ge(a_mx[kk], 16 * (gg + 1))
                    sp.dma_start(max_scr[k % 2].rearrange("r p c -> p r c"), NP[:, :, :]).then_inc(a_mscr, 16)

                def sp_max_fill(sp, g, k):
                    sp.wait_ge(a_mscr, 16 * (GB * g + k + 1))
                    alone(sp)
                    sp.dma_start(QA[57:60, k, :, :], max_scr[k % 2].rearrange("r (h t) c -> r h (t c)", t=2))\
                      .then_inc(a_mx[k], 16)

                def there(b, ahead=0):
                    return not isinstance(b, int) or 0 <= b + ahead < B

                def turns(eng, slot, start, group):
                    for p in range(TURN):
                        slot(start, 0, 0, p)

                    def turn(ch, g, k):
                        for p in range(TURN, 8):
                            slot(ch, g, k, p)
                        for p in range(TURN):
                            slot(ch, *at(g, k, 1), p)

                    with eng.Fori(0, NG - 1) as g:
                        ch = group(g)
                        for k in range(GB):
                            turn(ch, g, k)
                    ch = group(NG - 1)
                    for k in range(GB):
                        turn(ch, NG - 1, k)

                PRO = [bank[4], bank[5]]
                DB = [bank[2], bank[3]]
                G3 = NG - 1

                with nc.Block() as block:
                    @block.sync
                    def _(sp):
                        for k in range(GB):
                            sp_ctx(sp, 0, k)
                        for b in range(AHEAD_V):
                            sp.wait_ge(a_zero, 2 * b + 2)
                            sp.dma_start(KA[54:60, b, :, :], krow_scr[0, 6:12, :].unsqueeze(1).broadcast_to([6, HEADS, T]))\
                              .then_inc(a_ones[b], 16)
                            sp_rows(sp, 0, b)
                            sp_store(sp, 0, b)
                            sp_fill(sp, 0, b)
                        sp.wait_ge(a_zero, 2 * GB)
                        sp.dma_start(KA[54:60, GB - 1, :, :], krow_scr[0, 6:12, :].unsqueeze(1).broadcast_to([6, HEADS, T]))\
                          .then_inc(a_ones[GB - 1], 16)
                        sp_max_store(sp, 0, 0)
                        sp_max_fill(sp, 0, 0)

                        def sp_batch(g, k, last):
                            if not last:
                                sp.wait_ge(a_vps, GB * g + k + 1)
                                alone(sp)
                                sp_ctx(sp, g + 1, k)
                            if not last or k + AHEAD_V < GB:
                                sp_rows(sp, *at(g, k, AHEAD_V))
                                sp_store(sp, *at(g, k, AHEAD_V))
                            if not last or k + 1 < GB:
                                sp_max_store(sp, *at(g, k, 1))
                            if not last or k + AHEAD_V < GB:
                                sp_fill(sp, *at(g, k, AHEAD_V))
                            if not last or k + 1 < GB:
                                sp_max_fill(sp, *at(g, k, 1))

                        with sp.Fori(0, NG - 1) as g:
                            for k in range(GB):
                                sp_batch(g, k, False)
                        for k in range(GB):
                            sp_batch(NG - 1, k, True)

                    @block.scalar
                    def _(act):
                        act_zt(act, G3)
                        act_part(act, 0, 0)
                        for i in range(NI):
                            act_tanh(act, G3, i)
                            if i == 0:
                                act_part(act, 0, 1)
                            elif i > 1:
                                act_part(act, i // 2, i % 2)
                        act_nm(act, 0)
                        act.wait_ge(s_dn, 1 + 2 * NG)

                        def slot(_, g, k, p):
                            b = GB * g + k
                            if p < 2 and there(b, AHEAD_V):
                                act_part(act, b + AHEAD_V, p)
                            if p == 1 and there(b, -1):
                                act_av(act, b - 1)
                            if there(b):
                                act_exp(act, g, k, p // 2, p % 2)
                            if p == 0 and there(b, 1):
                                act_nm(act, b + 1)

                        turns(act, slot, None, lambda g: None)

                    @block.gpsimd
                    def _(pool):
                        pch = Chain(pool, a_pool)

                        def zero(k, both=(QA, KA)):
                            for stacked in both:
                                pool.memset(stacked[:, k, :, :].rearrange("p h t -> p (h t)").bitcast(fp32), 0.0)\
                                    .then_inc(a_zero, 1)

                        zero(0, (QA,))
                        power_step(pool, GB, a_var, a_rstd, 1)
                        zero(0, (KA,))
                        pch.do(pool.memset(VP[:, :, :, :, :], 0.0))
                        pch.wait()
                        for i in range(4):
                            c = 9 * i + 8 if i < 3 else 8
                            pch.do(pool.memset(VP[:, :, :, :, :].rearrange("p s a (j i) c -> p (s a) j i c", i=4)[:, :, :, i, c], 1.0))
                        pch.wait()
                        for b in range(AHEAD_V):
                            pool_rest(pool, b, 0)
                            pool_rest(pool, b, 1)
                            pool_vp(pool, 0, b)
                            zero(b + 1)
                        pool_np(pool, pch, 0)
                        before = pch.n

                        def slot(pch, g, k, p):
                            b = GB * g + k
                            if p < 2 and there(b, AHEAD_V):
                                pool_rest(pool, b + AHEAD_V, p)
                            if p == 1 and there(b, 1):
                                pool_np(pool, pch, b + 1)
                            if p == 5 and there(b, AHEAD_V):
                                pool_vp(pool, *at(g, k, AHEAD_V))
                            if p == 6 and there(b, AHEAD_Q):
                                power_step(pool, 1, a_var, a_rstd, LN_COUNT(b + AHEAD_Q))

                        turns(pool, slot, pch, lambda g: Chain(pool, a_pool, before + NP_STEPS * (1 + GB * g)))

                    @block.tensor
                    def _(pe):
                        def project(b):
                            if b > 0:
                                pe.wait_ge(a_vf, b)
                            pe_proj(pe, 0, b)

                        def values(b):
                            pe.wait_ge(a_qk, 2 * b + 2)
                            pe_v(pe, b)

                        pairs = [(b, p) for b in range(2) for p in range(8)]

                        def pair():
                            b, p = pairs.pop(0)
                            if p == 0:
                                pe.wait_ge(a_ones[b], 16)
                            pe_scores(pe, 0, b, p, PRO)
                            if (b, p) == (1, 0):
                                pe.wait_ge(a_vf, AHEAD_V)
                                pe_mxT(pe, 0, 0)
                            if (b, p) == (1, 3):
                                pe.wait_ge(a_nm, 1)
                                pe_proj(pe, 0, AHEAD_V)

                        pe_z2T(pe, G3)
                        for i in range(NI):
                            pe_gu(pe, G3, i, (0,))
                            if i == 0:
                                project(0)
                            if i == 5:
                                pair()
                            pe_gu(pe, G3, i, (1,))
                            if i == 5:
                                pair()
                            if i % 2 == 1:
                                values(i // 2)
                            elif i > 0:
                                project(i // 2)
                        for t in range(GB):
                            pe_down(pe, G3, t, DB, pair)
                        while pairs:
                            pair()
                        pe.wait_ge(a_ones[2], 16)
                        pe.wait_ge(a_ones[3], 16)
                        pe.wait_ge(s_x2, 1 + 2 * NG)
                        pe.wait_ge(a_red, 2 * HEADS)

                        def slot(_, g, k, p):
                            b = GB * g + k
                            i, st = p // 2, p % 2
                            if there(b, AHEAD_S):
                                pe_scores(pe, *at(g, k, AHEAD_S), p)
                            if p == 2 and there(b, -1):
                                if there(b, 1):
                                    pe.wait_ge(a_nm, b + 2)
                                else:
                                    pe.wait_ge(a_x3, b - 1)
                                pe_yT(pe, b - 1)
                            if p == 1 and there(b, -1):
                                pe_pv(pe, *at(g, k, -1), 3, st)
                            if there(b):
                                pe_scoresT(pe, g, k, i, st)
                            if p == 7 and there(b, AHEAD_Q):
                                pe.wait_ge(a_vf, b + AHEAD_V + 1)
                                pe_proj(pe, *at(g, k, AHEAD_Q))
                            if i > 0 and there(b):
                                pe_pv(pe, g, k, i - 1, st)
                            elif p == 0 and there(b, -1):
                                pe_pv(pe, *at(g, k, -1), 3, st)
                            if p == 0 and there(b, 1):
                                if there(b, AHEAD_V):
                                    pe.wait_ge(a_qk, 2 * (b + AHEAD_V) + 2)
                                pe_mxT(pe, *at(g, k, 1))
                            if p == 4 and there(b, -1):
                                pe_yo(pe, b - 1)
                            if p == 5 and there(b, AHEAD_V):
                                if there(b, -1):
                                    pe.wait_ge(a_x3, b)
                                else:
                                    pe.wait_ge(a_nm, 2)
                                pe_v(pe, at(g, k, AHEAD_V)[1])

                        turns(pe, slot, None, lambda g: None)

                    @block.vector
                    def _(dve):
                        fch = Chain(dve, s_dvech, after_wkv[0])
                        ch = Chain(dve, a_dve)
                        last_of = layer_norm_stats(ch, xt_tile(0), GB)
                        last_of.then_inc(a_var, 1)
                        dve_z3(dve, 0)
                        def reduces(b, lo, hi):
                            for h in range(lo, hi):
                                dve_reduce(dve, 0, b, h, PRO)

                        dve_qk(dve, 0, 0)
                        dve_z3(dve, 1)
                        for i in range(NI):
                            if i == NI - 1:
                                reduces(0, 0, 4)
                            dve_h1(dve, fch, G3, i)
                            dve_h(dve, fch, G3, i)
                            if i % 2 == 1:
                                dve_vf(dve, i // 2)
                            elif i > 0:
                                dve_qk(dve, 0, i // 2)
                                dve_z3(dve, i // 2 + 1)
                        reduces(0, 4, 16)
                        dve_x2(dve, G3, DB, (0,))
                        reduces(1, 0, 10)
                        dve_qk(dve, 0, AHEAD_V)
                        reduces(1, 10, 12)
                        dve_x2(dve, G3, DB, (1,))
                        reduces(1, 12, 16)
                        before = ch.n
                        per_batch = 2 + 3 + 2 + 2

                        def slot(ch, g, k, p):
                            b = GB * g + k
                            if p == 6 and there(b, AHEAD_Q):
                                dve_stats(dve, ch, b + AHEAD_Q, 0)
                            if p == 7 and there(b, AHEAD_Q):
                                dve_z3(dve, b + AHEAD_Q)
                            if there(b, AHEAD_S):
                                dve_reduce(dve, *at(g, k, AHEAD_S), 2 * p)
                            if p == 6 and there(b, AHEAD_Q):
                                dve_stats(dve, ch, b + AHEAD_Q, 1)
                            if p == 3 and there(b, -1):
                                dve_factors(dve, ch, b - 1)
                            if there(b, AHEAD_S):
                                dve_reduce(dve, *at(g, k, AHEAD_S), 2 * p + 1)
                            if p == 6 and there(b, AHEAD_Q):
                                dve_stats(dve, ch, b + AHEAD_Q, 2)
                            if p == 2 and there(b, -1):
                                dve_sums(dve, ch, b - 1)
                            if p == 3 and there(b, -1):
                                dve_y(dve, ch, b - 1)
                            if p == 4 and there(b, -1):
                                dve_x3(dve, b - 1)
                            if p == 5 and there(b, AHEAD_V):
                                dve_vf(dve, b + AHEAD_V)
                            if p == 7 and there(b, AHEAD_Q):
                                dve_qk(dve, *at(g, k, AHEAD_Q))

                        turns(dve, slot, ch, lambda g: Chain(dve, a_dve, before + per_batch * GB * g))
        if stop_after == 2:
            store_x()
            return
        with ExitStack() as part:
            def sbp(name, shape, dt=fp32):
                return sb(name, shape, dt, part)

            def semp(name):
                return sem(name, part)

            at_one = []

            def primed(name):
                at_one.append(semp(name))
                return at_one[-1]

            Z4 = sbp("Z4", [P, B, C])
            ZT4 = sbp("ZT4", [P, 2, B * P])
            stats4 = sbp("stats4", [P, B, 6])
            mv4 = sbp("mv4", [P, B, 2])
            veps4 = sbp("veps4", [P, B])
            rstd4 = sbp("rstd4", [P, B])
            L = sbp("L", [P, B, NE])
            LX = sbp("LX", [P, B, NE])
            mxl = sbp("mxl", [P, B])
            sml = sbp("sml", [P, B])
            gate = sbp("gate", [P, B])
            rev = sbp("rev", [P, B, NE], mybir.dt.int32)
            revf = sbp("revf", [P, B, NE])
            tok = sbp("tok", [P, B], mybir.dt.int32)
            tokf = sbp("tokf", [P, B])
            key = sbp("key", [P, B, NE])
            kmax = sbp("kmax", [P, B])
            OH = sbp("OH", [P, B, NE])
            OHB = sbp("OHB", [P, NE, B], bf16)
            tri = sbp("tri", [P, P], bf16)
            ones = sbp("ones", [P, P], bf16)
            carry = sbp("carry", [P, NE, B])
            INC = sbp("INC", [P, NE, B])
            TOT = sbp("TOT", [P, NE, B])
            POS = sbp("POS", [P, NE, B])
            pos = sbp("pos", [P, B])
            keepm = sbp("keepm", [P, B])
            flat = sbp("flat", [P, B])
            flat_u = sbp("flat_u", [P, B], u32)
            from_u = sbp("from_u", [P, B], u32)
            fromf = sbp("fromf", [P, B])
            TH = sbp("THs", [P, NH, GT])
            H1 = sbp("H1s", [P, NH, GT])
            HS = sbp("HS", [P, NH, GT])
            WE1 = sbp("WE1", [P, 2, 2, EH])
            WE3 = sbp("WE3", [P, 2, 2, EH])
            WE2 = sbp("WE2", [P, 2, NH, C])
            XD = sbp("XD", [P, 2, 2, C])
            XT = sbp("XT", [P, 2, 2, CAP])
            HE = sbp("HE", [P, NH, CAP])
            OE = sbp("OE", [P, 2, 2, C])
            GT_ = sbp("GT_", [P, B, C])

            m_pool = semp("m_pool")
            m_dve = semp("m_dve")
            m_var = semp("m_var")
            m_rstd = semp("m_rstd")
            m_z4 = semp("m_z4")
            m_z4T = semp("m_z4T")
            m_zt = semp("m_zt")
            m_lg = semp("m_lg")
            m_lx = semp("m_lx")
            m_ex = semp("m_ex")
            m_oh = semp("m_oh")
            m_cum = semp("m_cum")
            m_flat = semp("m_flat")
            m_scat = semp("m_scat")
            m_gu = semp("m_gu")
            m_th = semp("m_th")
            m_h = semp("m_h")
            m_dn = primed("m_dn")
            m_xs = primed("m_xs")
            e_w = [semp(f"e_w{s}") for s in range(2)]
            e_xd = [semp(f"e_xd{s}") for s in range(2)]
            e_xT = semp("e_xT")
            e_xt = semp("e_xt")
            e_gu = semp("e_gu")
            e_th = semp("e_th")
            e_h = semp("e_h")
            e_dn = primed("e_dn")
            e_oe = primed("e_oe")
            e_st = [primed(f"e_st{s}") for s in range(2)]
            m_gath = [semp(f"m_gath{g}") for g in range(NG)]
            m_out = semp("m_out")
            m_stored = semp("m_stored")

            flat2 = lambda t: t[:, :, :].rearrange("p a b -> p (a b)")

            with nc.Block() as block:
                @block.sync
                def _(sp):
                    for primed_sem in at_one:
                        sp.sem_inc(primed_sem, 1)
                    def load_w13(e, s):
                        for dst, src in ((WE1[:, s, :, :], W1), (WE3[:, s, :, :], W3)):
                            sp.dma_start(dst, src[bass.ds(e, 1), :, :].rearrange("e (h p) i -> p (e h) i", p=P))\
                              .then_inc(e_w[s], 16)

                    def load_w2(e, s):
                        sp.dma_start(WE2[:, s, 0:2, :], W2[bass.ds(e, 1), 0:2 * P, :]
                                     .rearrange("e (i p) c -> p (e i) c", p=P)).then_inc(e_w[s], 16)
                        sp.dma_start(WE2[0:EH - 2 * P, s, 2, :], W2[bass.ds(e, 1), 2 * P:EH, :]
                                     .rearrange("e p c -> (e p) c")).then_inc(e_w[s], 16)

                    def load_tokens(e, s):
                        sp.dma_start(XD[:, s, :, :], dispatched[bass.ds(CAP * e, CAP), :]
                                     .rearrange("(a p) c -> p a c", p=P)).then_inc(e_xd[s], 16)

                    for s in range(2):
                        load_w13(s, s)
                        load_w2(s, s)
                    sp.wait_ge(m_scat, 16 * B)
                    for s in range(2):
                        load_tokens(s, s)

                    def store(e2, s):
                        e = 2 * e2 + s
                        sp.wait_ge(e_oe, 1 + e + 1)
                        sp.dma_start(expert_out[bass.ds(CAP * e, CAP), :].rearrange("(a p) c -> p a c", p=P),
                                     OE[:, s, :, :]).then_inc(e_st[s], 16)

                    with sp.Fori(0, NE // 2 - 1) as e2:
                        for s in range(2):
                            e = 2 * e2 + s
                            sp.wait_ge(e_xT, e + 1)
                            load_tokens(e + 2, s)
                            sp.wait_ge(e_gu, NH * e + NH)
                            load_w13(e + 2, s)
                            sp.wait_ge(e_dn, 1 + e + 1)
                            load_w2(e + 2, s)
                            store(e2, s)
                    for s in range(2):
                        store(NE // 2 - 1, s)
                    for g in range(NG):
                        sp.wait_ge(m_out, GB * g + GB)
                        sp.dma_start(ot[:, GB * g:GB * (g + 1), :], X[:, GB * g:GB * (g + 1), :]).then_inc(m_stored, 16)
                    sp.wait_ge(m_stored, 16 * NG)

                @block.gpsimd
                def _(pool):
                    pool.memset(ones[:], 1.0).then_inc(m_pool, 1)
                    pool.memset(tri[:], 1.0).then_inc(m_pool, 1)
                    pool.memset(carry[:, :, 0:1], 0.0).then_inc(m_pool, 1)
                    pool.memset(carry[:, :, 1:B], 1.0).then_inc(m_pool, 1)
                    pool.iota(rev[:], pattern=[[0, B], [-1, NE]], base=NE, channel_multiplier=0).then_inc(m_pool, 1)
                    pool.iota(tok[:], pattern=[[P, B]], base=SLOTS, channel_multiplier=1).then_inc(m_pool, 1)
                    pool.wait_ge(m_pool, 6)
                    pool.tensor_copy(revf[:], rev[:]).then_inc(m_pool, 1)
                    pool.tensor_copy(tokf[:], tok[:]).then_inc(m_pool, 1)
                    pool.affine_select(out=tri[:], in_=tri[:], compare_op=ALU.is_gt, fill=0.0, base=0,
                                       pattern=[[1, P]], channel_multiplier=-1).then_inc(m_pool, 1)
                    for g in range(NG):
                        pool.wait_ge(m_var, g + 1)
                        pool.tensor_tensor(rstd4[:, GB * g:GB * (g + 1)], veps4[:, GB * g:GB * (g + 1)], neghalf[:, :],
                                           ALU.pow).then_inc(m_rstd, 1)
                    pool.wait_ge(m_flat, 1)
                    for t in range(B):
                        pool.indirect_dma_start(out=dispatched, out_offset=bass.IndirectOffsetOnAxis(ap=flat_u[:, t:t + 1], axis=0),
                                                in_=Z4[:, t, :], in_offset=None).then_inc(m_scat, 16)
                    pool.wait_ge(m_flat, 3)
                    for s in range(2):
                        pool.wait_ge(e_st[s], 1 + 16 * (NE // 2))
                    for t in range(B):
                        pool.indirect_dma_start(out=GT_[:, t, :], out_offset=None, in_=expert_out,
                                                in_offset=bass.IndirectOffsetOnAxis(ap=from_u[:, t:t + 1], axis=0))\
                            .then_inc(m_gath[t // GB], 16)

                @block.scalar
                def _(act):
                    for g in range(NG):
                        for h in range(2):
                            act.wait_ge(m_z4T, 2 * g + h + 1)
                            act.activation(ZT4[:, h, GT * g:GT * (g + 1)], bank[2 * (g % 2) + h], ACT.Copy).then_inc(m_zt, 1)
                    act.wait_ge(m_lx, 1)
                    act.activation(flat2(LX), flat2(LX), ACT.Exp).then_inc(m_ex, 1)

                    def tanh_shared(g, i, first=False):
                        m = width(i, EH)
                        act.wait_ge(m_gu, NH * g + i + 1)
                        if not first:
                            act.wait_ge(m_h, NH * (g - 1) + i + 1)
                        act.activation(TH[0:m, i, :], bank[2 * i][0:m, :], ACT.Tanh, scale=0.5).then_inc(m_th, 1)

                    for i in range(NH):
                        tanh_shared(0, i, first=True)
                    with act.Fori(1, NG) as g:
                        for i in range(NH):
                            tanh_shared(g, i)

                    def turn_tokens(e, s):
                        act.wait_ge(e_xT, e + 1)
                        act.activation(XT[:, s, :, :].rearrange("p h t -> p (h t)"), bank[4], ACT.Copy).then_inc(e_xt, 1)

                    def tanh_expert(e, i, first=False):
                        m = width(i, EH)
                        act.wait_ge(e_gu, NH * e + i + 1)
                        if not first:
                            act.wait_ge(e_h, NH * (e - 1) + i + 1)
                        act.activation(TH[0:m, i, 0:CAP], bank[i][0:m, 0:CAP], ACT.Tanh, scale=0.5).then_inc(e_th, 1)

                    def result(e2, s):
                        e = 2 * e2 + s
                        act.wait_ge(e_dn, 1 + e + 1)
                        act.wait_ge(e_st[s], 1 + 16 * e2)
                        act.activation(OE[:, s, :, :].rearrange("p a c -> p (a c)"), bank[6], ACT.Copy).then_inc(e_oe, 1)

                    act.wait_ge(m_h, NH * NG)
                    turn_tokens(0, 0)
                    for i in range(NH):
                        tanh_expert(0, i, first=True)

                    def step(e2, s):
                        e = 2 * e2 + s
                        turn_tokens(e + 1, 1 - s)
                        tanh_expert(e + 1, 0)
                        result(e2, s)
                        for i in range(1, NH):
                            tanh_expert(e + 1, i)

                    with act.Fori(0, NE // 2 - 1) as e2:
                        for s in range(2):
                            step(e2, s)
                    step(NE // 2 - 1, 0)
                    result(NE // 2 - 1, 1)

                @block.tensor
                def _(pe):
                    def turn(g):
                        pe.wait_ge(m_z4, g + 1)
                        if g >= 2:
                            pe.wait_ge(m_zt, 2 * (g - 1))
                        for h in range(2):
                            for b in range(GB):
                                last = pe.transpose(bank[2 * (g % 2) + h][:, b * P:(b + 1) * P],
                                                    Z4[:, GB * g + b, h * P:(h + 1) * P], ident[:])
                            last.then_inc(m_z4T, 1)

                    def route(g):
                        pe.wait_ge(m_zt, 2 * g + 2)
                        for t in range(GB * g, GB * (g + 1)):
                            for h in range(2):
                                last = pe.matmul(bank[7][:, t * NE:(t + 1) * NE], ZT4[:, h, t * P:(t + 1) * P], wgt[:, h, :],
                                                 start=(h == 0), stop=(h == 1))
                        last.then_inc(m_lg, 1)

                    turn(0)
                    for g in range(1, NG):
                        turn(g)
                        route(g - 1)
                    route(NG - 1)

                    def gu_shared(g, i, side, first=False):
                        m = width(i, EH)
                        if not first and side == 0:
                            pe.wait_ge(m_h, NH * (g - 1) + i + 1)
                        for h in range(2):
                            last = pe.matmul(bank[2 * i + side][0:m, :], (wsh1, wsh3)[side][:, h, i * P:i * P + m],
                                             ZT4[:, h, bass.ds(GT * g, GT)], start=(h == 0), stop=(h == 1))
                        if side == 1:
                            last.then_inc(m_gu, 1)

                    def down_shared(g):
                        pe.wait_ge(m_h, NH * g + NH)
                        pe.wait_ge(m_xs, 1 + 2 * g)
                        for k in range(2):
                            for b in range(2):
                                t = 2 * k + b
                                for i in range(NH):
                                    m = width(i, EH)
                                    last = pe.matmul(bank[6 + k][:, b * C:(b + 1) * C], HS[0:m, i, t * P:(t + 1) * P],
                                                     wsh2[0:m, i, :], start=(i == 0), stop=(i == NH - 1))
                            last.then_inc(m_dn, 1)

                    gu_shared(0, 0, 0, first=True)
                    pe.wait_ge(m_oh, 1)
                    pe.wait_ge(m_pool, 9)
                    pe.matmul(bank[6][:, 0:NE * B], tri[:], flat2(OHB), start=True, stop=True)
                    pe.matmul(bank[6][:, NE * B:2 * NE * B], ones[:], flat2(OHB), start=True, stop=True).then_inc(m_cum, 1)
                    gu_shared(0, 0, 1, first=True)
                    for i in range(1, NH):
                        for side in range(2):
                            gu_shared(0, i, side, first=True)
                    pe.wait_ge(m_flat, 1)
                    with pe.Fori(0, NG - 1) as g:
                        for side in range(2):
                            gu_shared(g + 1, 0, side)
                        down_shared(g)
                        for i in range(1, NH):
                            for side in range(2):
                                gu_shared(g + 1, i, side)
                    down_shared(NG - 1)

                    def turn_tokens(e2, s):
                        e = 2 * e2 + s
                        pe.wait_ge(e_xd[s], 16 * (e2 + 1))
                        if not isinstance(e, int) or e > 0:
                            pe.wait_ge(e_xt, e)
                        for h in range(2):
                            for a in range(2):
                                last = pe.transpose(bank[4][:, h * CAP + a * P:h * CAP + (a + 1) * P],
                                                    XD[:, s, a, h * P:(h + 1) * P], ident[:])
                        last.then_inc(e_xT, 1)

                    def gu_expert(e2, s, i, first=False):
                        e = 2 * e2 + s
                        m = width(i, EH)
                        if i == 0:
                            pe.wait_ge(e_xt, e + 1)
                            pe.wait_ge(e_w[s], 64 * (e2 + 1))
                        if not first:
                            pe.wait_ge(e_h, NH * (e - 1) + i + 1)
                        for w, lo in ((WE1, 0), (WE3, CAP)):
                            for h in range(2):
                                last = pe.matmul(bank[i][0:m, lo:lo + CAP], w[:, s, h, i * P:i * P + m],
                                                 XT[:, s, h, :], start=(h == 0), stop=(h == 1))
                        last.then_inc(e_gu, 1)

                    def down_expert(e, s):
                        pe.wait_ge(e_h, NH * e + NH)
                        pe.wait_ge(e_oe, 1 + e)
                        for a in range(2):
                            for i in range(NH):
                                m = width(i, EH)
                                last = pe.matmul(bank[6][:, a * C:(a + 1) * C], HE[0:m, i, a * P:(a + 1) * P],
                                                 WE2[0:m, s, i, :], start=(i == 0), stop=(i == NH - 1))
                        last.then_inc(e_dn, 1)

                    turn_tokens(0, 0)
                    for i in range(NH):
                        gu_expert(0, 0, i, first=True)
                    pe.wait_ge(m_xs, 1 + 2 * NG)

                    def step(e2, s):
                        e = 2 * e2 + s
                        ahead = (e2 + (s + 1) // 2, (s + 1) % 2)
                        turn_tokens(*ahead)
                        gu_expert(*ahead, 0)
                        down_expert(e, s)
                        for i in range(1, NH):
                            gu_expert(*ahead, i)

                    with pe.Fori(0, NE // 2 - 1) as e2:
                        for s in range(2):
                            step(e2, s)
                    step(NE // 2 - 1, 0)
                    down_expert(NE - 1, 1)

                @block.vector
                def _(dve):
                    ch = Chain(dve, m_dve)
                    token = lambda t: X[:, t, :]

                    def statistics(g):
                        tiles = range(GB * g, GB * (g + 1))
                        for t in tiles:
                            ch.do(dve.bn_stats(stats4[:, t, :], token(t)))
                        ch.wait()
                        for t in tiles:
                            ch.do(dve.bn_aggr(mv4[:, t, :], stats4[:, t, :]))
                        ch.wait()
                        dve.tensor_scalar(veps4[:, GB * g:GB * (g + 1)], mv4[:, GB * g:GB * (g + 1), 1], EPS, None, ALU.add)\
                            .then_inc(m_var, 1)

                    def normalise(g):
                        dve.wait_ge(m_rstd, g + 1)
                        for t in range(GB * g, GB * (g + 1)):
                            last = dve.tensor_scalar(Z4[:, t, :], token(t), mv4[:, t, 0:1], rstd4[:, t:t + 1],
                                                     ALU.subtract, ALU.mult)
                        last.then_inc(m_z4, 1)

                    statistics(0)
                    for g in range(1, NG):
                        statistics(g)
                        normalise(g - 1)
                    normalise(NG - 1)
                    over_e = lambda v: v[:, :].unsqueeze(2).broadcast_to([P, B, NE])
                    dve.wait_ge(m_lg, NG)
                    ch.do(dve.tensor_copy(flat2(L), bank[7][:, 0:B * NE]))
                    ch.wait()
                    ch.do(dve.tensor_reduce(mxl[:], L[:], axis=AX.X, op=ALU.max))
                    ch.wait()
                    dve.tensor_tensor(LX[:], L[:], over_e(mxl), ALU.subtract).then_inc(m_lx, 1)
                    ch.do(dve.tensor_tensor(key[:], L[:], over_e(mxl), ALU.is_equal))
                    ch.wait()
                    dve.wait_ge(m_pool, 9)
                    ch.do(dve.tensor_tensor(key[:], key[:], revf[:], ALU.mult))
                    ch.wait()
                    ch.do(dve.tensor_reduce(kmax[:], key[:], axis=AX.X, op=ALU.max))
                    ch.wait()
                    ch.do(dve.tensor_tensor(OH[:], key[:], over_e(kmax), ALU.is_equal))
                    ch.wait()
                    dve.tensor_copy(OHB[:].rearrange("p e b -> p b e"), OH[:]).then_inc(m_oh, 1)
                    dve.wait_ge(m_ex, 1)
                    ch.do(dve.tensor_reduce(sml[:], LX[:], axis=AX.X, op=ALU.add))
                    ch.wait()
                    ch.do(dve.reciprocal(gate[:], sml[:]))
                    dve.wait_ge(m_cum, 1)
                    ch.do(dve.tensor_copy(flat2(TOT), bank[6][:, NE * B:2 * NE * B]))
                    ch.wait()
                    ch.do(dve.tensor_tensor_scan(out=flat2(INC), data0=flat2(carry), data1=flat2(TOT), initial=0.0,
                                                 op0=ALU.mult, op1=ALU.add))
                    ch.wait()
                    ch.do(dve.tensor_tensor(flat2(POS), flat2(INC), flat2(TOT), ALU.subtract))
                    ch.wait()
                    ch.do(dve.tensor_tensor(flat2(POS), flat2(POS), bank[6][:, 0:NE * B], ALU.add))
                    ch.wait()
                    ch.do(dve.tensor_tensor(key[:], OH[:], POS[:].rearrange("p e b -> p b e"), ALU.mult))
                    ch.wait()
                    ch.do(dve.tensor_reduce(pos[:], key[:], axis=AX.X, op=ALU.add))
                    ch.wait()
                    ch.do(dve.tensor_scalar(keepm[:], pos[:], float(CAP), None, ALU.is_lt))
                    ch.do(dve.tensor_scalar(flat[:], kmax[:], -float(CAP), float(SLOTS), ALU.mult, ALU.add))
                    ch.wait()
                    ch.do(dve.tensor_tensor(flat[:], flat[:], pos[:], ALU.add))
                    ch.wait()
                    ch.do(dve.tensor_tensor(flat[:], flat[:], tokf[:], ALU.subtract))
                    ch.wait()
                    ch.do(dve.tensor_tensor(flat[:], flat[:], keepm[:], ALU.mult))
                    ch.wait()
                    ch.do(dve.tensor_tensor(flat[:], flat[:], tokf[:], ALU.add))
                    ch.wait()
                    dve.tensor_copy(flat_u[:], flat[:]).then_inc(m_flat, 1)
                    ch.do(dve.tensor_scalar(fromf[:], flat[:], float(SLOTS - 1), None, ALU.min))
                    ch.wait()
                    dve.tensor_copy(from_u[:], fromf[:]).then_inc(m_flat, 1)
                    ch.do(dve.tensor_tensor(gate[:], gate[:], keepm[:], ALU.mult))
                    ch.wait()
                    dve.tensor_scalar(gate[:], gate[:], tg[:, 3:4], None, ALU.mult).then_inc(m_flat, 1)
                    before = ch.n

                    def hidden_shared(ch, g, i):
                        m = width(i, EH)
                        dve.wait_ge(m_th, NH * g + i + 1)
                        ch.do(dve.scalar_tensor_tensor(out=H1[0:m, i, :], in0=TH[0:m, i, :], scalar=1.0,
                                                       in1=bank[2 * i][0:m, :], op0=ALU.add, op1=ALU.mult))
                        ch.wait()
                        dve.scalar_tensor_tensor(out=HS[0:m, i, :], in0=H1[0:m, i, :], scalar=0.5,
                                                 in1=bank[2 * i + 1][0:m, :], op0=ALU.mult, op1=ALU.mult).then_inc(m_h, 1)

                    def add_shared(g):
                        for k in range(2):
                            dve.wait_ge(m_dn, 1 + 2 * g + k + 1)
                            xs = X[:, bass.ds(GB * g + 2 * k, 2), :].rearrange("p b c -> p (b c)")
                            dve.scalar_tensor_tensor(out=xs, in0=bank[6 + k], scalar=tg[:, 3:4], in1=xs,
                                                     op0=ALU.mult, op1=ALU.add).then_inc(m_xs, 1)

                    for i in range(NH):
                        hidden_shared(ch, 0, i)
                    before = ch.n
                    with dve.Fori(0, NG - 1) as g:
                        ch = Chain(dve, m_dve, before + NH * g)
                        add_shared(g)
                        for i in range(NH):
                            hidden_shared(ch, g + 1, i)
                    add_shared(NG - 1)
                    before += NH * (NG - 1)

                    def hidden_expert(ch, e, i):
                        m = width(i, EH)
                        dve.wait_ge(e_th, NH * e + i + 1)
                        ch.do(dve.scalar_tensor_tensor(out=H1[0:m, i, 0:CAP], in0=TH[0:m, i, 0:CAP], scalar=1.0,
                                                       in1=bank[i][0:m, 0:CAP], op0=ALU.add, op1=ALU.mult))
                        if i == 0:
                            dve.wait_ge(e_dn, 1 + e)
                        ch.wait()
                        dve.scalar_tensor_tensor(out=HE[0:m, i, :], in0=H1[0:m, i, 0:CAP], scalar=0.5,
                                                 in1=bank[i][0:m, CAP:2 * CAP], op0=ALU.mult, op1=ALU.mult).then_inc(e_h, 1)

                    with dve.Fori(0, NE // 2) as e2:
                        ch = Chain(dve, m_dve, before + 2 * NH * e2)
                        for s in range(2):
                            for i in range(NH):
                                hidden_expert(ch, 2 * e2 + s, i)
                    dve.wait_ge(m_xs, 1 + 2 * NG)
                    dve.wait_ge(m_flat, 3)
                    for t in range(B):
                        dve.wait_ge(m_gath[t // GB], 16 * GB)
                        dve.scalar_tensor_tensor(out=X[:, t, :], in0=GT_[:, t, :], scalar=gate[:, t:t + 1], in1=X[:, t, :],
                                                 op0=ALU.mult, op1=ALU.add).then_inc(m_out, 1)


def kernel(**inputs):
    import numpy as _np
    import concourse.bacc as _bacc
    from concourse import mybir as _mybir
    from concourse.bass_utils import run_bass_kernel_spmd as _run

    a = {k: _np.asarray(v) for k, v in inputs.items()}
    column = lambda v: v.reshape(-1, P).T
    by_dim = _np.arange(P).reshape(HEADS, HD).T.reshape(-1)
    laid = {
        "x": a["x"], "ctx": a["ctx_2048"], "mask": a["mask_Bx1x2048_fk1"].reshape(B, T),
        "g_xattn": a["g_xattn"], "g_ffn": a["g_ffn"],
        "time_decay": column(a["L0_xattn_time_decay"]), "time_first": column(a["L0_xattn_time_first"]),
        "gate_wT": a["L0_ffn_gate_w"].T, "up_wT": a["L0_ffn_up_w"].T, "down_wT": a["L0_ffn_down_w"].T,
        "gate_s": a["L0_ffn_gate_s"], "up_s": a["L0_ffn_up_s"], "down_s": a["L0_ffn_down_s"],
        "wqT": a["L1_xattn_Wq"][by_dim].T, "bq": column(a["L1_xattn_bq"][by_dim]),
        "wkT": a["L1_xattn_Wk"][by_dim].T, "bk": column(a["L1_xattn_bk"][by_dim]),
        "wvT": a["L1_xattn_Wv"].T, "bv": a["L1_xattn_bv"],
        "Wg": a["L1_ffn_Wg"], "W1": a["L1_ffn_W1"], "W3": a["L1_ffn_W3"], "W2": a["L1_ffn_W2"],
        "sw1": a["L1_ffn_sw1"], "sw3": a["L1_ffn_sw3"], "sw2": a["L1_ffn_sw2"],
    }
    nc = _bacc.Bacc("TRN2", target_bir_lowering=False, num_devices=1)
    arrays, args = {}, []
    for name, v in laid.items():
        arrays[f"in_{name}"] = _np.ascontiguousarray(v)
        args.append(nc.dram_tensor(f"in_{name}", v.shape, _mybir.dt.from_np(v.dtype), kind="ExternalInput").ap())
    args.append(nc.dram_tensor("out_x", (B, P, C), fp32, kind="ExternalOutput").ap())
    flamingo_kernel(nc, *args)
    r = _run(nc, [arrays], core_ids=[0])
    return r.results[0]["out_x"]
```

```python
from contextlib import ExitStack

import concourse.bass as bass
from concourse import mybir

fp32 = mybir.dt.float32
bf16 = mybir.dt.bfloat16
u32 = mybir.dt.uint32
ALU = mybir.AluOpType
ACT = mybir.ActivationFunctionType
AX = mybir.AxisListType

P = 128
B, C = 16, 256
NG, GB = 4, 4
GT = GB * P
INTER = 704
NI = -(-INTER // P)
HEADS, HD = 16, 8
T = 256
NE, EH = 8, 352
NH = -(-EH // P)
CAP = B * P // NE
SLOTS = NE * CAP
NEG = 1000000.0
EPS = 1e-5
STACK = 60


def width(i, n):
    return min(P, n - i * P)


class Chain:

    def __init__(self, eng, sem, start=0):
        self.eng, self.sem, self.start, self.n = eng, sem, start, 0

    def do(self, ins):
        ins.then_inc(self.sem, 1)
        self.n += 1
        return self.n

    def wait(self, n=None):
        self.eng.wait_ge(self.sem, self.start + (self.n if n is None else n))


def flamingo_kernel(nc, x, ctx, mask, g_xattn, g_ffn, time_decay, time_first, gate_wT, up_wT, down_wT,
                    gate_s, up_s, down_s, wqT, bq, wkT, bk, wvT, bv, Wg, W1, W3, W2, sw1, sw3, sw2, out):
    stack_scr = nc.dram_tensor("stack_scr", [2, 6, P, T], bf16).ap()
    max_scr = nc.dram_tensor("max_scr", [2, 3, 2 * HEADS, P], bf16).ap()
    qrow_scr = nc.dram_tensor("qrow_scr", [B, 12, T], bf16).ap()
    krow_scr = nc.dram_tensor("krow_scr", [B, 12, T], bf16).ap()
    dispatched = nc.dram_tensor("dispatched", [SLOTS + B * P, C + 1], fp32).ap()
    combined = nc.dram_tensor("combined", [1 + B * P, C], fp32).ap()
    xt = x.rearrange("b p c -> p b c")
    ct = ctx.rearrange("b p c -> p b c")
    ot = out.rearrange("b p c -> p b c")

    with ExitStack() as keep:
        def sb(name, shape, dt=fp32, where=keep):
            return where.enter_context(nc.sbuf_tensor(name, shape, dt))

        def sem(name, where=keep):
            return where.enter_context(nc.semaphore(name))

        psum = keep.enter_context(nc.psum_tensor("psum", [P, 8 * 512], fp32))
        bank = [psum[:, i * 512:(i + 1) * 512] for i in range(8)]
        X = sb("X", [P, B, C])
        ident = sb("ident", [P, P])
        tg = sb("tg", [P, 4])
        neghalf = sb("neghalf", [P, GB])
        stats = sb("stats", [P, GB, 6])
        mv = sb("mv", [P, GB, 2])
        veps = sb("veps", [P, GB])
        rstd = sb("rstd", [P, GB])
        wsh1 = sb("wsh1", [P, 2, EH])
        wsh3 = sb("wsh3", [P, 2, EH])
        wsh2 = sb("wsh2", [P, NH, C])
        wgt = sb("wgt", [P, 2, 32])
        wq = sb("wq", [P, P])
        wk = sb("wk", [P, P])
        wv = sb("wv", [P, P])
        bqk = sb("bqk", [P, 2])
        bvb = sb("bvb", [P, P])
        maskT = sb("maskT", [P, 2, B])
        zeros = sb("zeros", [P, 2 * (C + 1)])
        space_w = sb("space_w", [P, 4 * INTER + NI * C])
        space_a = sb("space_a", [P, 4, 2 * GT])
        gw = space_w[:, 0:2 * INTER].rearrange("p (h i) -> p h i", h=2)
        uw = space_w[:, 2 * INTER:4 * INTER].rearrange("p (h i) -> p h i", h=2)
        dw = space_w[:, 4 * INTER:].rearrange("p (i c) -> p i c", c=C)
        Z4 = space_w[:, 0:B * (C + 1)].rearrange("p (b c) -> p b c", c=C + 1)
        Z2 = space_a[:, 0, :].rearrange("p (b c) -> p b c", b=GB)
        ZT, TH, H1 = (space_a[:, i, :].rearrange("p (h t) -> p h t", h=2) for i in (1, 2, 3))
        ZT4 = space_a[:, :, :].rearrange("p a t -> p (a t)").rearrange("p (h t) -> p h t", h=2)
        stats4 = sb("stats4", [P, B, 6])
        mv4 = sb("mv4", [P, B, 2])
        veps4 = sb("veps4", [P, B])
        rstd4 = sb("rstd4", [P, B])
        m_ln = sem("m_ln")
        m_var = sem("m_var")
        m_rstd = sem("m_rstd")
        m_z4 = sem("m_z4")
        m_z4T = sem("m_z4T")
        m_zt = sem("m_zt")
        s_late = sem("s_late")
        s_alone = {e: sem(f"s_alone_{e}") for e in ("sp", "dve", "pe", "pool")}

        def alone(eng):
            eng.sem_inc(s_alone[{nc.sync: "sp", nc.vector: "dve", nc.tensor: "pe", nc.gpsimd: "pool"}[eng]], 1)

        def layer_norm_stats(ch, src, n):
            for i in range(n):
                last = ch.do(ch.eng.bn_stats(stats[:, i, :], src(i)))
            ch.wait(last)
            alone(ch.eng)
            for i in range(n):
                last = ch.do(ch.eng.bn_aggr(mv[:, i, :], stats[:, i, :]))
            ch.wait()
            return ch.eng.tensor_scalar(veps[:, 0:n], mv[:, 0:n, 1], EPS, None, ALU.add)

        def layer_norm_steps(ch, src, dst, n, s_var, s_rstd, nth):
            layer_norm_stats(ch, src, n).then_inc(s_var, 1)
            ch.eng.wait_ge(s_rstd, nth)
            for i in range(n):
                last = ch.eng.tensor_scalar(dst(i), src(i), mv[:, i, 0:1], rstd[:, i:i + 1],
                                            ALU.subtract, ALU.mult)
                if i < n - 1:
                    ch.do(last)
            return last

        LN_STEPS = lambda n: n + n + n - 1

        def power_step(eng, n, s_var, s_rstd, nth):
            eng.wait_ge(s_var, nth)
            eng.tensor_tensor(rstd[:, 0:n], veps[:, 0:n], neghalf[:, 0:n], ALU.pow).then_inc(s_rstd, 1)

        def dve_statistics(ch, g):
            tiles = range(GB * g, GB * (g + 1))
            for t in tiles:
                ch.do(ch.eng.bn_stats(stats4[:, t, :], X[:, t, :]))
            ch.wait()
            for t in tiles:
                ch.do(ch.eng.bn_aggr(mv4[:, t, :], stats4[:, t, :]))
            ch.wait()
            ch.eng.tensor_scalar(veps4[:, GB * g:GB * (g + 1)], mv4[:, GB * g:GB * (g + 1), 1], EPS, None, ALU.add)\
                .then_inc(m_var, 1)

        def dve_normalise(dve, g):
            dve.wait_ge(m_rstd, g + 1)
            for t in range(GB * g, GB * (g + 1)):
                last = dve.tensor_scalar(Z4[:, t, 0:C], X[:, t, :], mv4[:, t, 0:1], rstd4[:, t:t + 1],
                                         ALU.subtract, ALU.mult)
            last.then_inc(m_z4, 1)

        def pool_power4(pool, g):
            pool.wait_ge(m_var, g + 1)
            pool.tensor_tensor(rstd4[:, GB * g:GB * (g + 1)], veps4[:, GB * g:GB * (g + 1)], neghalf[:, :],
                               ALU.pow).then_inc(m_rstd, 1)

        def pe_turn4(pe, g, h, to):
            pe.wait_ge(m_z4, g + 1)
            if g > 0:
                pe.wait_ge(m_zt, 2 * g + h - 1)
            for b in range(GB):
                last = pe.transpose(to[:, b * P:(b + 1) * P], Z4[:, GB * g + b, h * P:(h + 1) * P], ident[:])
            last.then_inc(m_z4T, 1)

        def dve_turn4(dve, g, h, to):
            dve.wait_ge(m_z4T, 2 * g + h + 1)
            dve.tensor_copy(ZT4[:, h, GT * g:GT * (g + 1)], to).then_inc(m_zt, 1)

        with ExitStack() as part:
            wkv = part.enter_context(ExitStack())

            def sbp(name, shape, dt=fp32):
                return sb(name, shape, dt, part)

            def sbw(name, shape, dt=fp32):
                return sb(name, shape, dt, wkv)

            def semp(name):
                return sem(name, part)

            at_one = []

            def primed(name):
                at_one.append(semp(name))
                return at_one[-1]

            hgs = sbp("hgs", [P, NI])
            hgu = sbp("hgu", [P, NI])
            HP = sbp("HP", [P, 8, GT])
            CV = sbw("CV", [P, GB, C])
            dsb = sbw("dsb", [P, C])
            gs = sbw("gs", [P, NI])
            us = sbw("us", [P, NI])
            gates = sbw("gates", [P, 4])
            td = sbw("td", [P, 2])
            tf = sbw("tf", [P, 2])
            tdx = sbw("tdx", [P, 2])
            decay = sbw("decay", [P, 2])
            upos = sbw("upos", [P, 2])
            uneg = sbw("uneg", [P, 2])
            steps01 = sbw("steps01", [P, GB, P])
            DEC = sbw("DEC", [P, 2, GT])
            mrow = sbw("mrow", [B, T])
            mtmp = sbw("mtmp", [B, 3, T])
            mparts = sbw("mparts", [B, 3, 3, T], bf16)
            onesb = sbw("onesb", [6, T], bf16)
            Z1 = sbw("Z1", [P, GB, C])
            EA = sbw("EA", [P, 2, GB, P])
            EB = sbw("EB", [P, 2, GB, P])
            PA = sbw("PA", [P, 2, GB, P])
            PB = sbw("PB", [P, 2, GB, P])
            SA = sbw("SA", [P, 2, GT])
            SB = sbw("SB", [P, 2, GT])
            NUM = sbw("NUM", [P, 2, GT])
            DEN = sbw("DEN", [P, 2, GT])
            Y = sbw("Y", [P, 2, GT])

            s_ld = semp("s_ld")
            s_wts = semp("s_wts")
            s_x = semp("s_x")
            s_c = semp("s_c")
            s_pool0 = semp("s_pool0")
            s_id = semp("s_id")
            s_act0 = semp("s_act0")
            s_dv0 = semp("s_dv0")
            s_mT = semp("s_mT")
            s_mT2 = semp("s_mT2")
            s_mask = semp("s_mask")
            s_mp = semp("s_mp")
            s_zero = semp("s_zero")
            s_mst = semp("s_mst")
            s_dvech = semp("s_dvech")
            s_var1 = semp("s_var1")
            s_rstd1 = semp("s_rstd1")
            s_z1 = semp("s_z1")
            s_kT = semp("s_kT")
            s_vT = primed("s_vT")
            s_exp = semp("s_exp")
            s_pab = semp("s_pab")
            s_scan = semp("s_scan")
            s_den = semp("s_den")
            s_num = semp("s_num")
            s_rec = semp("s_rec")
            s_y = semp("s_y")
            s_yT = semp("s_yT")
            s_x1 = semp("s_x1")
            s_z2 = semp("s_z2")
            s_z2T = semp("s_z2T")
            s_zt = semp("s_zt")
            s_gu = semp("s_gu")
            s_th = semp("s_th")
            s_h = primed("s_h")
            s_dn = primed("s_dn")
            s_x2 = primed("s_x2")

            WB = [bank[4], bank[5]]
            DB = [bank[6], bank[7]]
            after_wkv = []

            def pe_wkv_in(pe, g, h):
                n = 2 * g + h
                if h == 0:
                    pe.wait_ge(s_z1, g + 1)
                    pe.wait_ge(s_x1, 2 * g)
                pe.wait_ge(s_exp, 2 * n)
                for b in range(GB):
                    last = pe.transpose(WB[0][:, b * P:(b + 1) * P], Z1[:, b, h * P:(h + 1) * P], ident[:])
                last.then_inc(s_kT, 1)
                if h == 0:
                    pe.wait_ge(s_c, 16 * (g + 1))
                pe.wait_ge(s_pab, 2 * n)
                for b in range(GB):
                    last = pe.transpose(WB[1][:, b * P:(b + 1) * P], CV[:, b, h * P:(h + 1) * P], ident[:])
                last.then_inc(s_vT, 1)

            def act_exps(act, g, h):
                act.wait_ge(s_kT, 2 * g + h + 1)
                act.wait_ge(s_y, 2 * g)
                kT = WB[0][:, :].rearrange("p (b t) -> p b t", b=GB)
                act.activation(EB[:, h, :, 1:P], kT[:, :, 1:P], ACT.Exp, bias=uneg[:, h:h + 1]).then_inc(s_exp, 1)
                act.activation(EA[:, h, :, 1:P], kT[:, :, 0:P - 1], ACT.Exp, bias=upos[:, h:h + 1]).then_inc(s_exp, 1)

            def dve_products(dve, g, h):
                n = 2 * g + h
                vT = WB[1][:, :].rearrange("p (b t) -> p b t", b=GB)
                dve.wait_ge(s_vT, 1 + n + 1)
                dve.wait_ge(s_exp, 2 * n + 2)
                dve.wait_ge(s_y, 2 * g)
                dve.tensor_tensor(PA[:, h, :, 1:P], EA[:, h, :, 1:P], vT[:, :, 0:P - 1], ALU.mult).then_inc(s_pab, 1)
                dve.tensor_tensor(PB[:, h, :, :], EB[:, h, :, :], vT, ALU.mult).then_inc(s_pab, 1)

            def dve_scans(dve, g, h):
                n = 2 * g + h
                flat = lambda t: t[:, h, :, :].rearrange("p b t -> p (b t)")
                dve.tensor_tensor_scan(out=SB[:, h, :], data0=DEC[:, h, :], data1=flat(EA), initial=0.0,
                                       op0=ALU.mult, op1=ALU.add).then_inc(s_scan, 1)
                dve.wait_ge(s_pab, 2 * n + 1)
                dve.tensor_tensor_scan(out=SA[:, h, :], data0=DEC[:, h, :], data1=flat(PA), initial=0.0,
                                       op0=ALU.mult, op1=ALU.add).then_inc(s_scan, 1)

            def pool_sums(pool, g, h):
                n = 2 * g + h
                flat = lambda t: t[:, h, :, :].rearrange("p b t -> p (b t)")
                pool.wait_ge(s_scan, 2 * n + 1)
                pool.tensor_tensor(DEN[:, h, :], SB[:, h, :], flat(EB), ALU.add).then_inc(s_den, 1)
                pool.wait_ge(s_scan, 2 * n + 2)
                pool.tensor_tensor(NUM[:, h, :], SA[:, h, :], flat(PB), ALU.add).then_inc(s_num, 1)

            def dve_recip(dve, g, h):
                dve.wait_ge(s_den, 2 * g + h + 1)
                dve.reciprocal(DEN[:, h, :], DEN[:, h, :]).then_inc(s_rec, 1)

            def pool_quot(pool, g, h):
                n = 2 * g + h
                pool.wait_ge(s_rec, n + 1)
                pool.wait_ge(s_num, n + 1)
                pool.wait_ge(s_yT, 2 * g)
                pool.tensor_tensor(Y[:, h, :], NUM[:, h, :], DEN[:, h, :], ALU.mult).then_inc(s_y, 1)

            def pe_wkv_out(pe, g):
                pe.wait_ge(s_y, 2 * g + 2)
                for k in range(2):
                    for b in range(2):
                        for h in range(2):
                            i = 2 * k + b
                            last = pe.transpose(WB[k][:, b * C + h * P:b * C + (h + 1) * P],
                                                Y[:, h, i * P:(i + 1) * P], ident[:])
                    last.then_inc(s_yT, 1)

            def dve_x1(dve, g):
                for k in range(2):
                    dve.wait_ge(s_yT, 2 * g + k + 1)
                    xs = X[:, bass.ds(GB * g + 2 * k, 2), :].rearrange("p b c -> p (b c)")
                    dve.scalar_tensor_tensor(out=xs, in0=WB[k][:, :], scalar=tg[:, 0:1], in1=xs,
                                             op0=ALU.mult, op1=ALU.add).then_inc(s_x1, 1)

            CH1 = 2 * LN_STEPS(GB) + NI
            xt_tile = lambda g: (lambda i: X[:, bass.ds(GB * g + i, 1), :].rearrange("p b c -> p (b c)"))

            def dve_ln1(dve, ch, g):
                dve.wait_ge(s_x, 16 * (g + 1))
                dve.wait_ge(s_kT, 2 * g)
                layer_norm_steps(ch, xt_tile(g), lambda i: Z1[:, i, :], GB, s_var1, s_rstd1, 2 * g + 1)\
                    .then_inc(s_z1, 1)

            def dve_ln2(dve, ch, g):
                dve.wait_ge(s_x1, 2 * g + 2)
                dve.wait_ge(s_z2T, 2 * g)
                alone(dve)
                layer_norm_steps(ch, xt_tile(g), lambda i: Z2[:, i, :], GB, s_var1, s_rstd1, 2 * g + 2)\
                    .then_inc(s_z2, 1)

            def pe_z2T(pe, g):
                pe.wait_ge(s_z2, g + 1)
                pe.wait_ge(s_h, 1 + NI * g)
                for h in range(2):
                    for b in range(GB):
                        last = pe.transpose(bank[h][:, b * P:(b + 1) * P], Z2[:, b, h * P:(h + 1) * P], ident[:])
                    last.then_inc(s_z2T, 1)

            def act_zt(act, g):
                for h in range(2):
                    act.wait_ge(s_z2T, 2 * g + h + 1)
                    act.activation(ZT[:, h, :], bank[h][:, :], ACT.Copy).then_inc(s_zt, 1)

            def pe_gu(pe, g, i, sides=(0, 1)):
                m = width(i, INTER)
                for side in sides:
                    if i == 0 and side == 0:
                        pe.wait_ge(s_zt, 2 * g + 2)
                    if i >= 2 and side == 0:
                        pe.wait_ge(s_h, 1 + NI * g + i - 1)
                    for h in range(2):
                        last = pe.matmul(bank[2 * (i % 2) + side][0:m, :], (gw, uw)[side][:, h, i * P:i * P + m],
                                         ZT[:, h, :], start=(h == 0), stop=(h == 1))
                    if side == 1:
                        last.then_inc(s_gu, 1)

            def act_tanh(act, g, i):
                m = width(i, INTER)
                act.wait_ge(s_gu, NI * g + i + 1)
                act.activation(TH[0:m, i % 2, :], bank[2 * (i % 2)][0:m, :], ACT.Tanh,
                               scale=hgs[0:m, i:i + 1]).then_inc(s_th, 1)

            def dve_h1(dve, ch, g, i):
                m = width(i, INTER)
                dve.wait_ge(s_th, NI * g + i + 1)
                ch.do(dve.scalar_tensor_tensor(out=H1[0:m, i % 2, :], in0=TH[0:m, i % 2, :], scalar=1.0,
                                               in1=bank[2 * (i % 2)][0:m, :], op0=ALU.add, op1=ALU.mult))

            def dve_h(dve, ch, g, i):
                m = width(i, INTER)
                if i == 0:
                    dve.wait_ge(s_dn, 1 + 2 * g)
                ch.wait()
                dve.scalar_tensor_tensor(out=HP[0:m, i, :], in0=H1[0:m, i % 2, :], scalar=hgu[0:m, i:i + 1],
                                         in1=bank[2 * (i % 2) + 1][0:m, :], op0=ALU.mult,
                                         op1=ALU.mult).then_inc(s_h, 1)

            def pe_down(pe, g, t, DB, between=None):
                ahead = 0 if between else 1
                if t == 0:
                    pe.wait_ge(s_x2, 1 + 2 * g)
                for i in range(NI):
                    if t == 0 and i in (0, NI - 1):
                        pe.wait_ge(s_h, 1 + NI * g + (NI - ahead if i == 0 else NI))
                    m = width(i, INTER)
                    last = pe.matmul(DB[t // 2][:, (t % 2) * C:(t % 2 + 1) * C], HP[0:m, i, t * P:(t + 1) * P],
                                     dw[0:m, i, :], start=(i == 0), stop=(i == NI - 1))
                    if between and i % 2 == 0:
                        between()
                if t % 2 == 1:
                    last.then_inc(s_dn, 1)

            def dve_x2(dve, g, DB, ks=(0, 1)):
                for k in ks:
                    dve.wait_ge(s_dn, 1 + 2 * g + k + 1)
                    xs = X[:, bass.ds(GB * g + 2 * k, 2), :].rearrange("p b c -> p (b c)")
                    dve.scalar_tensor_tensor(out=xs, in0=DB[k][:, :], scalar=tg[:, 2:3], in1=xs,
                                             op0=ALU.mult, op1=ALU.add).then_inc(s_x2, 1)

            N_SMALL, N_ROWS, N_ZERO = 13, 9, SLOTS // P // 2
            with nc.Block() as block:
                @block.sync
                def _(sp):
                    for primed_sem in at_one:
                        sp.sem_inc(primed_sem, 1)

                    def load_x(g):
                        sp.dma_start(X[:, bass.ds(GB * g, GB), :], xt[:, bass.ds(GB * g, GB), :]).then_inc(s_x, 16)

                    def load_ctx(g):
                        sp.dma_start(CV[:, :, :], ct[:, bass.ds(GB * g, GB), :]).then_inc(s_c, 16)

                    small = [(gates[:, 0:2], g_xattn.partition_broadcast(P)), (gates[:, 2:4], g_ffn.partition_broadcast(P)),
                             (td[:], time_decay), (tf[:], time_first),
                             (gs[:, 0:NI - 1], gate_s[0:(NI - 1) * P].rearrange("(i p) -> p i", p=P)),
                             (us[:, 0:NI - 1], up_s[0:(NI - 1) * P].rearrange("(i p) -> p i", p=P)),
                             (gs[0:width(NI - 1, INTER), NI - 1:NI],
                              gate_s[(NI - 1) * P:INTER].rearrange("(p a) -> p a", a=1)),
                             (us[0:width(NI - 1, INTER), NI - 1:NI],
                              up_s[(NI - 1) * P:INTER].rearrange("(p a) -> p a", a=1)),
                             (dsb[:], down_s.partition_broadcast(P)), (bvb[:], bv.partition_broadcast(P)),
                             (bqk[:, 0:1], bq), (bqk[:, 1:2], bk), (wq[:], wqT)]
                    assert len(small) == N_SMALL
                    with nc.allow_non_contiguous_dma(reason="small vectors"):
                        load_x(0)
                        sp.dma_start(mrow[:], mask).then_inc(s_mask, 16)
                        load_ctx(0)
                        for dst, src in small:
                            sp.dma_start(dst, src).then_inc(s_ld, 16)
                    sp.dma_start(gw[:, :, :], gate_wT.rearrange("(h p) i -> p h i", p=P)).then_inc(s_wts, 16)
                    sp.dma_start(uw[:, :, :], up_wT.rearrange("(h p) i -> p h i", p=P)).then_inc(s_wts, 16)
                    n5 = (NI - 1) * P
                    sp.dma_start(dw[:, 0:NI - 1, :], down_wT[0:n5, :].rearrange("(i p) c -> p i c", p=P)).then_inc(s_wts, 16)
                    sp.dma_start(dw[0:INTER - n5, NI - 1, :], down_wT[n5:INTER, :]).then_inc(s_wts, 16)
                    sp.wait_ge(s_pool0, 10)
                    for dst, src in ((wk[:], wkT), (wv[:], wvT),
                                     (wgt[:, :, 0:NE], Wg.rearrange("(h p) e -> p h e", p=P)),
                                     (wsh1[:, :, :], sw1.rearrange("(h p) e -> p h e", p=P)),
                                     (wsh3[:, :, :], sw3.rearrange("(h p) e -> p h e", p=P)),
                                     (wsh2[:, 0:2, :], sw2[0:2 * P, :].rearrange("(i p) c -> p i c", p=P)),
                                     (wsh2[0:EH - 2 * P, 2, :], sw2[2 * P:EH, :])):
                        sp.dma_start(dst, src).then_inc(s_late, 16)
                    with sp.Fori(1, NG) as g:
                        sp.wait_ge(s_vT, 1 + 2 * g)
                        load_x(g)
                        load_ctx(g)
                    sp.wait_ge(s_mp, 1)
                    every = lambda part, n: mparts[:, part[0], part[1], :].unsqueeze(1).broadcast_to([B, n, T])
                    rows = [(qrow_scr[:, 0:3, :], every((0, 0), 3)), (qrow_scr[:, 3:5, :], every((0, 1), 2)),
                            (qrow_scr[:, 5:6, :], every((0, 2), 1)), (qrow_scr[:, 6:9, :], mparts[:, 1, :, :]),
                            (qrow_scr[:, 9:12, :].rearrange("b r t -> b (r t)"), zeros[0:B, 0:3 * T // 2].bitcast(bf16)),
                            (krow_scr[:, 0:3, :], mparts[:, 2, :, :]), (krow_scr[:, 3:5, :], mparts[:, 2, 0:2, :]),
                            (krow_scr[:, 5:6, :], every((2, 0), 1)), (krow_scr[0, 6:12, :], onesb[:])]
                    assert len(rows) == N_ROWS
                    for dst, src in rows:
                        sp.dma_start(dst, src).then_inc(s_mst, 16)
                    dz = dispatched[0:SLOTS, :].rearrange("(p a b) c -> a p (b c)", p=P, b=2)
                    for a in range(N_ZERO):
                        sp.dma_start(dz[a], zeros[:, :]).then_inc(s_zero, 16)
                    cz = combined[1:, :].rearrange("(p a b) c -> a p (b c)", p=P, b=2)
                    for a in range(N_ZERO):
                        sp.dma_start(cz[a], zeros[:, 0:2 * C]).then_inc(s_zero, 16)
                    sp.wait_ge(s_mst, 16 * N_ROWS)
                    sp.wait_ge(s_zero, 2 * 16 * N_ZERO)

                @block.scalar
                def _(act):
                    act.wait_ge(s_ld, 16 * N_SMALL)
                    act.activation(tg[:], gates[:], ACT.Tanh).then_inc(s_act0, 1)
                    act.activation(tdx[:], td[:], ACT.Exp).then_inc(s_act0, 1)
                    act.wait_ge(s_act0, 2)
                    act.activation(decay[:], tdx[:], ACT.Exp, scale=-1.0).then_inc(s_act0, 1)
                    act.wait_ge(s_dv0, 2)
                    act.wait_ge(s_pool0, 5)
                    act_exps(act, 0, 0)
                    act_exps(act, 0, 1)
                    act.wait_ge(s_dv0, 4)
                    with act.Fori(0, NG - 1) as g:
                        act_zt(act, g)
                        for i in range(NI):
                            act_tanh(act, g, i)
                            if i < 2:
                                act_exps(act, g + 1, i)
                    act.wait_ge(s_late, 16 * 7)

                @block.gpsimd
                def _(pool):
                    pool.memset(neghalf[:], -0.5).then_inc(s_pool0, 1)
                    pool.memset(ident[:], 0.0).then_inc(s_pool0, 1)
                    pool.memset(EA[:, :, :, 0:1], 0.0).then_inc(s_pool0, 1)
                    pool.memset(EB[:, :, :, 0:1], 1.0).then_inc(s_pool0, 1)
                    pool.memset(PA[:, :, :, 0:1], 0.0).then_inc(s_pool0, 1)
                    pool.memset(steps01[:, :, 0:1], 0.0).then_inc(s_pool0, 1)
                    pool.memset(steps01[:, :, 1:P], 1.0).then_inc(s_pool0, 1)
                    pool.memset(zeros[:], 0.0).then_inc(s_pool0, 1)
                    pool.memset(onesb[:], 1.0).then_inc(s_pool0, 1)
                    pool.memset(wgt[:, :, :], 0.0).then_inc(s_pool0, 1)
                    pool.wait_ge(s_pool0, 10)
                    pool.affine_select(out=ident[:], in_=ident[:], compare_op=ALU.not_equal, fill=1.0, base=0,
                                       pattern=[[-1, P]], channel_multiplier=1).then_inc(s_id, 1)
                    power_step(pool, GB, s_var1, s_rstd1, 1)
                    for h in range(2):
                        pool_sums(pool, 0, h)
                    for h in range(2):
                        pool_quot(pool, 0, h)
                    power_step(pool, GB, s_var1, s_rstd1, 2)
                    with pool.Fori(0, NG - 1) as g:
                        power_step(pool, GB, s_var1, s_rstd1, 2 * g + 3)
                        for h in range(2):
                            pool_sums(pool, g + 1, h)
                        for h in range(2):
                            pool_quot(pool, g + 1, h)
                        power_step(pool, GB, s_var1, s_rstd1, 2 * g + 4)

                @block.tensor
                def _(pe):
                    pe.wait_ge(s_id, 1)
                    pe.wait_ge(s_mask, 16)
                    for h in range(2):
                        last = pe.transpose(bank[7][:, h * B:(h + 1) * B], mrow[:, h * P:(h + 1) * P], ident[0:B, 0:B])
                    last.then_inc(s_mT, 1)
                    for h in range(2):
                        pe_wkv_in(pe, 0, h)
                    pe_wkv_out(pe, 0)
                    pe.wait_ge(s_wts, 64)
                    with pe.Fori(0, NG - 1) as g:
                        pe_z2T(pe, g)
                        for i in range(NI):
                            pe_gu(pe, g, i)
                            if i < 2:
                                pe_wkv_in(pe, g + 1, i)
                        pe.wait_ge(s_dv0, 6)
                        pe.wait_ge(s_mT2, 1)
                        for t in range(GB):
                            if t == 2:
                                pe_wkv_out(pe, g + 1)
                            pe_down(pe, g, t, DB)

                @block.vector
                def _(dve):
                    ch = Chain(dve, s_dvech)
                    dve_ln1(dve, ch, 0)
                    dve.wait_ge(s_mask, 16)
                    for j, (mul, add) in enumerate(((-NEG, 0.0), (NEG, -NEG), (-1.0, 1.0))):
                        ch.do(dve.tensor_scalar(mtmp[:, j, :], mrow[:], mul, add, ALU.mult, ALU.add))

                    def mask_part(r):
                        ch.wait()
                        last = dve.tensor_copy(mparts[:, :, r, :], mtmp[:, :, :])
                        if r == 2:
                            last.then_inc(s_mp, 1)
                            return
                        ch.do(last)
                        ch.wait()
                        ch.do(dve.tensor_tensor(mtmp[:, :, :], mtmp[:, :, :], mparts[:, :, r, :], ALU.subtract))

                    mask_part(0)
                    dve.wait_ge(s_ld, 16 * N_SMALL)
                    dve.tensor_scalar(upos[:], tf[:], 0.0, -1.0, ALU.max, ALU.mult).then_inc(s_dv0, 1)
                    dve.tensor_scalar(uneg[:], tf[:], 0.0, None, ALU.min).then_inc(s_dv0, 1)
                    m = width(NI - 1, INTER)
                    for lo, hi, q in ((0, NI - 1, P), (NI - 1, NI, m)):
                        dve.tensor_scalar(hgs[0:q, lo:hi], gs[0:q, lo:hi], 0.5, None, ALU.mult).then_inc(s_dv0, 1)
                    dve.wait_ge(s_dv0, 4)
                    for lo, hi, q in ((0, NI - 1, P), (NI - 1, NI, m)):
                        ch.do(dve.tensor_tensor(hgu[0:q, lo:hi], hgs[0:q, lo:hi], us[0:q, lo:hi], ALU.mult))
                    dve.wait_ge(s_act0, 3)
                    dve.wait_ge(s_pool0, 10)
                    for h in range(2):
                        ch.do(dve.tensor_scalar(DEC[:, h, :], steps01[:, :, :].rearrange("p b t -> p (b t)"),
                                                decay[:, h:h + 1], None, ALU.mult))
                    ch.wait()
                    for h in range(2):
                        dve_products(dve, 0, h)
                        dve_scans(dve, 0, h)
                    for h in range(2):
                        dve_recip(dve, 0, h)
                    mask_part(1)
                    dve_x1(dve, 0)
                    dve_ln2(dve, ch, 0)
                    mask_part(2)
                    dve.wait_ge(s_mT, 1)
                    dve.tensor_copy(maskT[:, :, :].rearrange("p h b -> p (h b)"), bank[7][:, 0:2 * B]).then_inc(s_mT2, 1)
                    dve.wait_ge(s_wts, 64)
                    dve.tensor_tensor(dw[:, 0:NI - 1, :], dw[:, 0:NI - 1, :],
                                      dsb[:, :].unsqueeze(1).broadcast_to([P, NI - 1, C]), ALU.mult).then_inc(s_dv0, 1)
                    dve.tensor_tensor(dw[0:m, NI - 1, :], dw[0:m, NI - 1, :], dsb[0:m, :], ALU.mult).then_inc(s_dv0, 1)
                    ch.do(dve.tensor_scalar(wq[:], wq[:], HD ** -0.5, None, ALU.mult))
                    ch.do(dve.tensor_scalar(bqk[:, 0:1], bqk[:, 0:1], HD ** -0.5, None, ALU.mult))
                    before = ch.n
                    with dve.Fori(0, NG - 1) as g:
                        ch = Chain(dve, s_dvech, before + CH1 * g)
                        dve_ln1(dve, ch, g + 1)
                        for i in range(NI):
                            dve_h1(dve, ch, g, i)
                            dve_h(dve, ch, g, i)
                            if i < 2:
                                dve_products(dve, g + 1, i)
                                dve_scans(dve, g + 1, i)
                            elif i in (2, NI - 1):
                                dve_recip(dve, g + 1, i // 3)
                        dve_x1(dve, g + 1)
                        dve_ln2(dve, ch, g + 1)
                        dve_x2(dve, g, DB)
                        assert ch.n == CH1
                    after_wkv.append(before + CH1 * (NG - 1))
                    dve.wait_ge(s_x2, 1 + 2 * (NG - 1))

            wkv.close()

            with ExitStack() as att:
                def sbp(name, shape, dt=fp32):
                    return sb(name, shape, dt, att)

                def semp(name):
                    return sem(name, att)

                NS = GB
                QA = sbp("QA", [P, NS, HEADS, T], bf16)
                KA = sbp("KA", [P, NS, HEADS, T], bf16)
                VP = sbp("VP", [P, NS, 2, HEADS, 32])
                CX = sbp("CX", [P, NS, T])
                MB = sbp("MB", [P, NS, T])
                Z3 = sbp("Z3", [P, T])
                QK = sbp("QK", [P, 2 * T])
                PARTS = sbp("PARTS", [P, 6, T], bf16)
                VF = sbp("VF", [P, 2, P])
                MX = sbp("MX", [P, 2, HEADS, 2])
                NM = sbp("NM", [2 * HEADS, P])
                NP = sbp("NP", [2 * HEADS, 3, P], bf16)
                AV = sbp("AV", [P, 2, T])
                RD = sbp("RD", [P, 2, 4, 4])
                YA = sbp("YA", [P, 2, P])

                a_zero = [semp(f"a_zero{k}") for k in range(NS)]
                a_ones = [semp(f"a_ones{k}") for k in range(NS)]
                a_cx = [semp(f"a_cx{k}") for k in range(NS)]
                a_qa = [semp(f"a_qa{k}") for k in range(NS)]
                a_mx = [semp(f"a_mx{k}") for k in range(NS)]
                a_dve = semp("a_dve")
                a_pool = semp("a_pool")
                a_var = semp("a_var")
                a_rstd = semp("a_rstd")
                a_z3 = semp("a_z3")
                a_proj = semp("a_proj")
                a_qk = semp("a_qk")
                a_masked = semp("a_masked")
                a_part = semp("a_part")
                a_rest = semp("a_rest")
                a_scr = semp("a_scr")
                a_mscr = semp("a_mscr")
                a_vps = semp("a_vps")
                a_vf = semp("a_vf")
                a_vp = semp("a_vp")
                a_s = semp("a_s")
                a_red = semp("a_red")
                a_mxT = semp("a_mxT")
                a_nm = semp("a_nm")
                a_np = semp("a_np")
                a_st = semp("a_st")
                a_exp = semp("a_exp")
                a_pv = semp("a_pv")
                a_av = semp("a_av")
                a_yT = semp("a_yT")
                a_ya = semp("a_ya")
                a_yo = semp("a_yo")
                a_x3 = semp("a_x3")

                SBK = [bank[0], bank[1]]
                TBK = [psum[:, 2 * 512:4 * 512], psum[:, 4 * 512:6 * 512]]
                PVB, MISC = bank[6], bank[7]
                PT = HP[:, :, :].rearrange("p (a s q) (r t) -> p a s (q r) t", a=2, s=2, r=2)
                AHEAD_S, AHEAD_V, AHEAD_Q = 2, 3, 4
                TURN = 6

                def xb(b):
                    return X[:, bass.ds(b, 1), :].rearrange("p b c -> p (b c)")

                def at(g, k, ahead):
                    return g + (k + ahead) // GB, (k + ahead) % GB

                def later(count):
                    return not isinstance(count, int) or count > 0

                def pe_proj_k(pe, g, k):
                    pe.wait_ge(a_cx[k], 32 * (g + 1))
                    pe.matmul(MISC[:, T:2 * T], wk[:], CX[:, k, :], start=True, stop=True)

                def pe_proj_q(pe, g, k):
                    pe.wait_ge(a_z3, GB * g + k + 1)
                    pe.matmul(MISC[:, 0:T], wq[:], Z3[:], start=True, stop=True).then_inc(a_proj, 1)

                def pe_v(pe, k):
                    for st in range(2):
                        last = pe.matmul(MISC[:, st * P:(st + 1) * P], CX[:, k, st * P:(st + 1) * P], wv[:],
                                         start=True, stop=True)
                    last.then_inc(a_vps, 1)

                def pe_scores(pe, g, k, p, SBK=SBK):
                    b = GB * g + k
                    if p == 0:
                        pe.wait_ge(a_qa[k], 16 * N_FILL * (g + 1))
                    for h in (2 * p, 2 * p + 1):
                        if later(HEADS * b + h - 1):
                            pe.wait_ge(a_red, HEADS * b + h - 1)
                        for tt in range(2):
                            last = pe.matmul(SBK[h % 2][:, tt * T:(tt + 1) * T], QA[:, k, h, tt * P:(tt + 1) * P],
                                             KA[:, k, h, :], start=True, stop=True)
                        last.then_inc(a_s, 1)

                def pe_mxT(pe, g, k):
                    pe.wait_ge(a_red, HEADS * (GB * g + k + 1))
                    pe.transpose(MISC[0:2 * HEADS, 0:P], MX[:, k % 2, :, :].rearrange("p h t -> p (h t)"),
                                 ident[:]).then_inc(a_mxT, 1)

                def pe_scoresT(pe, g, k, i, st):
                    n = 8 * (GB * g + k) + 2 * i + st
                    if i == 0 and st == 0:
                        pe.wait_ge(a_mx[k], 16 * (g + 1))
                    if later(n - 1):
                        pe.wait_ge(a_exp, n - 1)
                    for j in range(4):
                        h = 4 * j + i
                        last = pe.matmul(TBK[st][:, j * T:(j + 1) * T],
                                         KA[:, k, h, st * P:(st + 1) * P], QA[:, k, h, :], start=True, stop=True)
                    last.then_inc(a_st, 1)

                def pe_pv(pe, g, k, i, st):
                    b = GB * g + k
                    if i == 0 and st == 0:
                        pe.wait_ge(a_vp, b + 1)
                        if later(b):
                            pe.wait_ge(a_av, b)
                    grp = 0 if i < 3 else 1
                    pe.wait_ge(a_exp, 8 * b + 2 * i + st + 1)
                    for j in range(4):
                        last = pe.matmul(PVB[32 * j:32 * j + 32, grp * T:(grp + 1) * T],
                                         VP[:, k, st, 4 * j + i, :], PT[:, i % 2, st, j, :],
                                         start=(i in (0, 3) and st == 0), stop=(i in (2, 3) and st == 1))
                    last.then_inc(a_pv, 1)

                def pe_yT(pe, b):
                    pe.wait_ge(a_av, b + 1)
                    for tt in range(2):
                        for grp in range(2):
                            last = pe.transpose(MISC[:, (2 * tt + grp) * P:(2 * tt + grp + 1) * P],
                                                AV[:, grp, tt * P:(tt + 1) * P], ident[:])
                    last.then_inc(a_yT, 1)

                def pe_yo(pe, b):
                    pe.wait_ge(a_ya, b + 1)
                    for tt in range(2):
                        last = pe.transpose(MISC[:, tt * P:(tt + 1) * P], YA[:, tt, :], ident[:])
                    last.then_inc(a_yo, 1)

                def dve_stats(dve, ch, b, step):
                    if step == 0:
                        ch.do(dve.bn_stats(stats[:, 0, :], xb(b)))
                    elif step == 1:
                        ch.wait()
                        alone(dve)
                        ch.do(dve.bn_aggr(mv[:, 0, :], stats[:, 0, :]))
                    else:
                        ch.wait()
                        dve.tensor_scalar(veps[:, 0:1], mv[:, 0:1, 1], EPS, None, ALU.add).then_inc(a_var, 1)

                LN_COUNT = lambda b: 1 if isinstance(b, int) and b < GB else b - 2

                def dve_z3(dve, b):
                    n = b if isinstance(b, int) and b < GB else 0
                    dve.wait_ge(a_rstd, LN_COUNT(b))
                    if later(b):
                        dve.wait_ge(a_proj, b)
                    dve.tensor_scalar(Z3[:], xb(b), mv[:, n, 0:1], rstd[:, n:n + 1], ALU.subtract, ALU.mult).then_inc(a_z3, 1)

                def dve_vf(dve, b):
                    dve.wait_ge(a_vps, b + 1)
                    if later(b):
                        dve.wait_ge(a_vp, b)
                    dve.tensor_tensor(VF[:, :, :], MISC[:, 0:T].rearrange("p (s c) -> p s c", s=2),
                                      bvb[:, :].unsqueeze(1).broadcast_to([P, 2, P]), ALU.add).then_inc(a_vf, 1)

                def dve_reduce(dve, g, k, h, SBK=SBK):
                    b, par = GB * g + k, k % 2
                    if h == 0 and later(b - 1):
                        dve.wait_ge(a_mxT, b - 1)
                    dve.wait_ge(a_s, HEADS * b + h + 1)
                    dve.tensor_reduce(MX[:, par, h, :], SBK[h % 2][:, :].rearrange("p (a s) -> p a s", a=2),
                                      axis=AX.X, op=ALU.max).then_inc(a_red, 1)

                yt = MISC[:, :].rearrange("p (t g c) -> p t g c", t=2, g=2)

                def dve_sums(dve, ch, b):
                    dve.wait_ge(a_yT, b + 1)
                    den_a = yt[:, :, 0, :].rearrange("p t (j r) -> p t j r", j=4)[:, :, :, 0:27]\
                        .rearrange("p t j (i r) -> p t j i r", r=9)[:, :, :, :, 8]
                    den_b = yt[:, :, 1, :].rearrange("p t (j r) -> p t j r", j=4)[:, :, :, 8]
                    ch.do(dve.reciprocal(RD[:, :, :, 3], den_b))
                    for tt in range(2):
                        ch.do(dve.reciprocal(RD[:, tt, :, 0:3], den_a[:, tt]))

                def dve_factors(dve, ch, b):
                    ch.wait()
                    for tt in range(2):
                        rd = RD[:, tt, :, :].rearrange("p j i -> p (j i)")
                        ch.do(dve.tensor_scalar(rd, rd, maskT[:, tt, bass.ds(b, 1)], tg[:, 1:2], ALU.mult, ALU.mult))

                def dve_y(dve, ch, b):
                    ch.wait()
                    for tt in range(2):
                        dst = YA[:, tt, :].rearrange("p (j i d) -> p j i d", j=4, i=4)
                        src = yt[:, tt, 0, :].rearrange("p (j r) -> p j r", j=4)[:, :, 0:27]\
                            .rearrange("p j (i r) -> p j i r", r=9)[:, :, :, 0:8]
                        ch.do(dve.tensor_tensor(dst[:, :, 0:3, :], src,
                                                RD[:, tt, :, 0:3].unsqueeze(3).broadcast_to([P, 4, 3, 8]), ALU.mult))
                    dst = YA[:, :, :].rearrange("p t (j i d) -> p t j i d", j=4, i=4)[:, :, :, 3, :]
                    src = yt[:, :, 1, :].rearrange("p t (j r) -> p t j r", j=4)[:, :, :, 0:8]
                    dve.tensor_tensor(dst, src, RD[:, :, :, 3].unsqueeze(3).broadcast_to([P, 2, 4, 8]), ALU.mult)\
                        .then_inc(a_ya, 1)

                def dve_x3(dve, b):
                    dve.wait_ge(a_yo, b + 1)
                    dve.tensor_tensor(xb(b), xb(b), MISC[:, 0:T], ALU.add).then_inc(a_x3, 1)

                def part_of(r):
                    return PARTS[:, r:6 - r:5 - 2 * r, :]

                QK2 = QK[:, :].rearrange("p (c t) -> p c t", c=2)

                def act_qk(act, b):
                    act.wait_ge(a_proj, b + 1)
                    if later(b):
                        act.wait_ge(a_rest, 2 * b)
                    for c in range(2):
                        act.activation(QK[:, c * T:(c + 1) * T], MISC[:, c * T:(c + 1) * T], ACT.Identity,
                                       bias=bqk[:, c:c + 1]).then_inc(a_qk, 1)

                def act_part(act, b, r):
                    if r == 0:
                        act.wait_ge(a_masked, b + 1)
                        if later(b):
                            act.wait_ge(a_scr, 16 * b)
                    else:
                        act.wait_ge(a_rest, 2 * b + 1)
                    act.activation(part_of(r), QK2, ACT.Copy).then_inc(a_part, 1)

                def act_nm(act, b):
                    act.wait_ge(a_mxT, b + 1)
                    if later(b):
                        act.wait_ge(a_np, b)
                    act.activation(NM[:], MISC[0:2 * HEADS, 0:P], ACT.Copy, scale=-1.0).then_inc(a_nm, 1)

                def act_exp(act, g, k, i, st):
                    n = 8 * (GB * g + k) + 2 * i + st
                    act.wait_ge(a_st, n + 1)
                    if later(n - 3):
                        act.wait_ge(a_pv, n - 3)
                    act.activation(PT[:, i % 2, st, :, :].rearrange("p j t -> p (j t)"), TBK[st], ACT.Exp)\
                        .then_inc(a_exp, 1)

                def act_av(act, b):
                    act.wait_ge(a_pv, 8 * b + 8)
                    act.activation(AV[:, :, :].rearrange("p a t -> p (a t)"), PVB[:, :], ACT.Copy).then_inc(a_av, 1)

                def pool_masked(pool, g, k):
                    pool.wait_ge(a_qk, 2 * (GB * g + k) + 2)
                    pool.wait_ge(a_cx[k], 32 * (g + 1))
                    pool.tensor_tensor(QK2, QK2, MB[:, k, :].unsqueeze(1).broadcast_to([P, 2, T]), ALU.mult).then_inc(a_masked, 1)

                def pool_rest(pool, b, r):
                    pool.wait_ge(a_part, 2 * b + r + 1)
                    pool.tensor_tensor(QK2 if r == 0 else part_of(2), QK2, part_of(r), ALU.subtract).then_inc(a_rest, 1)

                def pool_vp(pool, g, k):
                    b = GB * g + k
                    pool.wait_ge(a_vf, b + 1)
                    if later(b - 2):
                        pool.wait_ge(a_s, HEADS * (b - 1) + 5)
                    for st in range(2):
                        for i in range(4):
                            lo = 9 * i if i < 3 else 0
                            dst = VP[:, k, st, :, :].rearrange("p (j i) c -> p j i c", i=4)[:, :, i, lo:lo + 8]
                            src = VF[:, st, :].rearrange("p (j i d) -> p j i d", j=4, i=4)[:, :, i, :]
                            last = pool.tensor_tensor(dst, src, maskT[:, st, bass.ds(b, 1)].unsqueeze(2)
                                                      .broadcast_to([P, 4, 8]), ALU.mult)
                    last.then_inc(a_vp, 1)

                def pool_np(pool, pch, b):
                    pool.wait_ge(a_nm, b + 1)
                    if later(b):
                        pool.wait_ge(a_mscr, 16 * b)
                    nil = zeros[0:2 * HEADS, 0:P]
                    for r in range(2):
                        if r > 0:
                            pch.wait()
                        pch.do(pool.tensor_tensor(NP[:, r, :], NM[:], nil, ALU.add))
                        pch.wait()
                        last = pool.tensor_tensor(NM[:] if r == 0 else NP[:, 2, :], NM[:], NP[:, r, :], ALU.subtract)
                        if r == 0:
                            pch.do(last)
                    last.then_inc(a_np, 1)

                NP_STEPS = 3

                N_FILL = 8

                def sp_ctx(sp, g, k):
                    sp.dma_start(CX[:, k, :], ctx[bass.ds(GB * g + k, 1), :, :].rearrange("b p c -> (b p) c")).then_inc(a_cx[k], 16)
                    sp.dma_start(MB[:, k, :], mask[bass.ds(GB * g + k, 1), :].broadcast_to([P, T])).then_inc(a_cx[k], 16)

                def sp_rows(sp, g, k):
                    b = GB * g + k
                    if later(b - 2):
                        sp.wait_ge(a_s, HEADS * (b - 1) + 1)
                        alone(sp)
                    rows = lambda scr_, n: scr_[bass.ds(b, 1), 0:n, :].rearrange("b r t -> (b r) t").unsqueeze(1)\
                        .broadcast_to([n, HEADS, T])
                    sp.dma_start(QA[48:60, k, :, :], rows(qrow_scr, 12)).then_inc(a_qa[k], 16)
                    sp.dma_start(KA[48:54, k, :, :], rows(krow_scr, 6)).then_inc(a_qa[k], 16)

                def sp_store(sp, g, k):
                    b = GB * g + k
                    sp.wait_ge(a_rest, 2 * b + 2)
                    alone(sp)
                    if later(b - 1):
                        gg, kk = at(g, k, -2)
                        sp.wait_ge(a_qa[kk], 16 * N_FILL * (gg + 1))
                    sp.dma_start(stack_scr[k % 2].rearrange("r c t -> c r t"), PARTS[:, :, :]).then_inc(a_scr, 16)

                def sp_fill(sp, g, k):
                    sp.wait_ge(a_scr, 16 * (GB * g + k + 1))
                    alone(sp)
                    scr = stack_scr[k % 2]
                    for dst, parts, row in ((QA, (0, 3), 0), (KA, (3, 6), 0), (QA, (0, 2), 24), (KA, (4, 6), 24),
                                            (QA, (0, 1), 40), (KA, (5, 6), 40)):
                        lo, hi = parts
                        sp.dma_start(dst[row:row + HD * (hi - lo), k, :, :],
                                     scr[lo:hi, :, :].rearrange("r (d h) t -> (r d) h t", d=HD)).then_inc(a_qa[k], 16)

                def sp_max_store(sp, g, k):
                    b = GB * g + k
                    sp.wait_ge(a_np, b + 1)
                    alone(sp)
                    sp.dma_start(max_scr[k % 2].rearrange("r p c -> p r c"), NP[:, :, :]).then_inc(a_mscr, 16)

                def sp_max_fill(sp, g, k):
                    sp.wait_ge(a_mscr, 16 * (GB * g + k + 1))
                    alone(sp)
                    sp.dma_start(QA[57:60, k, :, :], max_scr[k % 2].rearrange("r (h t) c -> r h (t c)", t=2))\
                      .then_inc(a_mx[k], 16)

                def tail(b, p):
                    return 8 * (b - (B - 2)) + p if isinstance(b, int) and b >= B - 2 else None

                def there(b, ahead=0):
                    return not isinstance(b, int) or 0 <= b + ahead < B

                def turns(eng, slot, start, group):
                    for p in range(TURN):
                        slot(start, 0, 0, p)

                    def turn(ch, g, k):
                        for p in range(TURN, 8):
                            slot(ch, g, k, p)
                        for p in range(TURN):
                            slot(ch, *at(g, k, 1), p)

                    with eng.Fori(0, NG - 1) as g:
                        ch = group(g)
                        for k in range(GB):
                            turn(ch, g, k)
                    ch = group(NG - 1)
                    for k in range(GB):
                        turn(ch, NG - 1, k)

                PRO = [bank[4], bank[5]]
                DB = [bank[2], bank[3]]
                G3 = NG - 1
                LN4, TURN4 = 3, 9

                def zero(eng, stacked, k):
                    eng.memset(stacked[:, k, :, :].rearrange("p h t -> p (h t)").bitcast(fp32), 0.0).then_inc(a_zero[k], 1)

                with nc.Block() as block:
                    @block.sync
                    def _(sp):
                        for k in range(GB):
                            sp_ctx(sp, 0, k)
                        for b in range(AHEAD_V):
                            sp.wait_ge(a_zero[b], 2)
                            sp.dma_start(KA[54:60, b, :, :], krow_scr[0, 6:12, :].unsqueeze(1).broadcast_to([6, HEADS, T]))\
                              .then_inc(a_ones[b], 16)
                            sp_rows(sp, 0, b)
                            sp_store(sp, 0, b)
                            sp_fill(sp, 0, b)
                        sp.wait_ge(a_zero[GB - 1], 2)
                        sp.dma_start(KA[54:60, GB - 1, :, :], krow_scr[0, 6:12, :].unsqueeze(1).broadcast_to([6, HEADS, T]))\
                          .then_inc(a_ones[GB - 1], 16)
                        sp_max_store(sp, 0, 0)
                        sp_max_fill(sp, 0, 0)

                        def sp_batch(g, k, last):
                            if not last:
                                sp.wait_ge(a_vps, GB * g + k + 1)
                                alone(sp)
                                sp_ctx(sp, g + 1, k)
                            if not last or k + AHEAD_V < GB:
                                sp_rows(sp, *at(g, k, AHEAD_V))
                                sp_store(sp, *at(g, k, AHEAD_V))
                            if not last or k + 1 < GB:
                                sp_max_store(sp, *at(g, k, 1))
                            if not last or k + AHEAD_V < GB:
                                sp_fill(sp, *at(g, k, AHEAD_V))
                            if not last or k + 1 < GB:
                                sp_max_fill(sp, *at(g, k, 1))

                        with sp.Fori(0, NG - 1) as g:
                            for k in range(GB):
                                sp_batch(g, k, False)
                        for k in range(GB):
                            sp_batch(NG - 1, k, True)

                    @block.scalar
                    def _(act):
                        act_zt(act, G3)
                        act_qk(act, 0)
                        act_part(act, 0, 0)
                        for i in range(NI):
                            act_tanh(act, G3, i)
                            if i == 0:
                                act_part(act, 0, 1)
                            elif i > 1:
                                act_part(act, i // 2, i % 2)
                            if i in (1, 3):
                                act_qk(act, i // 2 + 1)
                        act_nm(act, 0)
                        act_qk(act, AHEAD_V)
                        act.wait_ge(s_dn, 1 + 2 * NG)

                        def slot(_, g, k, p):
                            b = GB * g + k
                            if p == 1 and there(b, -1):
                                act_av(act, b - 1)
                            if there(b):
                                act_exp(act, g, k, p // 2, p % 2)
                            if p < 2 and there(b, AHEAD_V):
                                act_part(act, b + AHEAD_V, p)
                            if p == 7 and there(b, AHEAD_Q):
                                act_qk(act, b + AHEAD_Q)
                            if p == 0 and there(b, 1):
                                act_nm(act, b + 1)

                        turns(act, slot, None, lambda g: None)

                    @block.gpsimd
                    def _(pool):
                        pch = Chain(pool, a_pool)

                        zero(pool, QA, 0)
                        power_step(pool, GB, a_var, a_rstd, 1)
                        for b in range(AHEAD_V):
                            pool_masked(pool, 0, b)
                            pool_rest(pool, b, 0)
                            pool_rest(pool, b, 1)
                            if b == 0:
                                pch.do(pool.memset(VP[:, :, :, :, :], 0.0))
                                pch.wait()
                                for i in range(4):
                                    c = 9 * i + 8 if i < 3 else 8
                                    pch.do(pool.memset(VP[:, :, :, :, :].rearrange("p s a (j i) c -> p (s a) j i c", i=4)[:, :, :, i, c],
                                                       1.0))
                                pch.wait()
                            pool_vp(pool, 0, b)
                            zero(pool, QA, b + 1)
                        zero(pool, KA, GB - 1)
                        pool_np(pool, pch, 0)
                        pool_masked(pool, 0, AHEAD_V)
                        before = pch.n

                        def slot(pch, g, k, p):
                            b = GB * g + k
                            if tail(b, p) in range(LN4, LN4 + G3):
                                pool_power4(pool, tail(b, p) - LN4)
                            if p < 2 and there(b, AHEAD_V):
                                pool_rest(pool, b + AHEAD_V, p)
                            if p == 1 and there(b, 1):
                                pool_np(pool, pch, b + 1)
                            if p == 7 and there(b, AHEAD_Q):
                                pool_masked(pool, *at(g, k, AHEAD_Q))
                            if p == 6 and there(b, AHEAD_Q):
                                power_step(pool, 1, a_var, a_rstd, LN_COUNT(b + AHEAD_Q))
                            if p == 6 and there(b, AHEAD_V):
                                pool_vp(pool, *at(g, k, AHEAD_V))

                        turns(pool, slot, pch, lambda g: Chain(pool, a_pool, before + NP_STEPS * (1 + GB * g)))

                    @block.tensor
                    def _(pe):
                        def project(b):
                            if b > 0:
                                pe.wait_ge(a_vf, b)
                            pe_proj_k(pe, 0, b)
                            pe_proj_q(pe, 0, b)

                        def values(b):
                            pe.wait_ge(a_qk, 2 * b + 2)
                            pe_v(pe, b)

                        pairs = [(b, p) for b in range(2) for p in range(8)]

                        def pair():
                            b, p = pairs.pop(0)
                            if p == 0:
                                pe.wait_ge(a_ones[b], 16)
                            pe_scores(pe, 0, b, p, PRO)
                            if (b, p) == (1, 0):
                                pe.wait_ge(a_vf, AHEAD_V)
                                pe_mxT(pe, 0, 0)
                            if (b, p) == (1, 3):
                                pe.wait_ge(a_nm, 1)
                                pe_proj_k(pe, 0, AHEAD_V)
                                pe_proj_q(pe, 0, AHEAD_V)

                        pe_z2T(pe, G3)
                        for i in range(NI):
                            pe_gu(pe, G3, i, (0,))
                            if i == 0:
                                project(0)
                            if i == 5:
                                pair()
                            pe_gu(pe, G3, i, (1,))
                            if i == 5:
                                pair()
                            if i % 2 == 1:
                                values(i // 2)
                            elif i > 0:
                                project(i // 2)
                        for t in range(GB):
                            pe_down(pe, G3, t, DB, pair)
                        while pairs:
                            pair()
                        pe.wait_ge(a_ones[2], 16)
                        pe.wait_ge(a_ones[3], 16)
                        pe.wait_ge(s_x2, 1 + 2 * NG)
                        pe.wait_ge(a_red, 2 * HEADS)

                        def slot(_, g, k, p):
                            b = GB * g + k
                            i, st = p // 2, p % 2
                            if there(b, AHEAD_S):
                                pe_scores(pe, *at(g, k, AHEAD_S), p)
                            if p == 2 and there(b, -1):
                                if there(b, 1):
                                    pe.wait_ge(a_nm, b + 2)
                                else:
                                    pe.wait_ge(a_x3, b - 1)
                                pe_yT(pe, b - 1)
                            if p == 1 and there(b, -1):
                                pe_pv(pe, *at(g, k, -1), 3, st)
                            if there(b):
                                pe_scoresT(pe, g, k, i, st)
                            if p == 7 and there(b, AHEAD_Q):
                                pe_proj_q(pe, *at(g, k, AHEAD_Q))
                            if i > 0 and there(b):
                                pe_pv(pe, g, k, i - 1, st)
                            elif p == 0 and there(b, -1):
                                pe_pv(pe, *at(g, k, -1), 3, st)
                            if p == 0 and there(b, 1):
                                if there(b, AHEAD_V):
                                    pe.wait_ge(a_qk, 2 * (b + AHEAD_V) + 2)
                                pe_mxT(pe, *at(g, k, 1))
                            if p == 4 and there(b, -1):
                                pe_yo(pe, b - 1)
                            if tail(b, p) in range(TURN4, TURN4 + 2 * G3):
                                pe_turn4(pe, *divmod(tail(b, p) - TURN4, 2), SBK[(tail(b, p) - TURN4) % 2])
                            if p == 6 and there(b, AHEAD_Q):
                                pe.wait_ge(a_vf, b + AHEAD_V + 1)
                                pe_proj_k(pe, *at(g, k, AHEAD_Q))
                            if p == 5 and there(b, AHEAD_V):
                                if there(b, -1):
                                    pe.wait_ge(a_x3, b)
                                else:
                                    pe.wait_ge(a_nm, 2)
                                pe_v(pe, at(g, k, AHEAD_V)[1])

                        turns(pe, slot, None, lambda g: None)

                    @block.vector
                    def _(dve):
                        fch = Chain(dve, s_dvech, after_wkv[0])
                        ln4 = Chain(dve, m_ln)
                        ch = Chain(dve, a_dve)
                        last_of = layer_norm_stats(ch, xt_tile(0), GB)
                        last_of.then_inc(a_var, 1)
                        dve_z3(dve, 0)
                        zero(dve, KA, 0)
                        zero(dve, KA, 1)
                        def reduces(b, lo, hi):
                            for h in range(lo, hi):
                                dve_reduce(dve, 0, b, h, PRO)

                        dve_z3(dve, 1)
                        zero(dve, KA, 2)
                        for i in range(NI):
                            if i == NI - 1:
                                reduces(0, 0, 4)
                            dve_h1(dve, fch, G3, i)
                            dve_h(dve, fch, G3, i)
                            if i % 2 == 1:
                                dve_vf(dve, i // 2)
                            elif i > 0:
                                dve_z3(dve, i // 2 + 1)
                        reduces(0, 4, 16)
                        dve_x2(dve, G3, DB, (0,))
                        reduces(1, 0, 12)
                        dve_x2(dve, G3, DB, (1,))
                        reduces(1, 12, 16)
                        before = ch.n
                        per_batch = 2 + 3 + 2 + 2

                        def slot(ch, g, k, p):
                            b = GB * g + k
                            if p == 6 and there(b, AHEAD_Q):
                                dve_stats(dve, ch, b + AHEAD_Q, 0)
                            if p == 7 and there(b, AHEAD_Q):
                                dve_z3(dve, b + AHEAD_Q)
                            if there(b, AHEAD_S):
                                dve_reduce(dve, *at(g, k, AHEAD_S), 2 * p)
                            if p == 6 and there(b, AHEAD_Q):
                                dve_stats(dve, ch, b + AHEAD_Q, 1)
                            if p == 3 and there(b, -1):
                                dve_factors(dve, ch, b - 1)
                            if there(b, AHEAD_S):
                                dve_reduce(dve, *at(g, k, AHEAD_S), 2 * p + 1)
                            if p == 6 and there(b, AHEAD_Q):
                                dve_stats(dve, ch, b + AHEAD_Q, 2)
                            if p == 2 and there(b, -1):
                                dve_sums(dve, ch, b - 1)
                            if p == 3 and there(b, -1):
                                dve_y(dve, ch, b - 1)
                            if p == 4 and there(b, -1):
                                dve_x3(dve, b - 1)
                            if tail(b, p) in range(LN4, LN4 + G3):
                                dve_statistics(ln4, tail(b, p) - LN4)
                            if tail(b, p) in range(LN4 + 1, LN4 + 1 + G3):
                                dve_normalise(dve, tail(b, p) - LN4 - 1)
                            if tail(b, p) in range(TURN4, TURN4 + 2 * G3):
                                dve_turn4(dve, *divmod(tail(b, p) - TURN4, 2), SBK[(tail(b, p) - TURN4) % 2])
                            if p == 5 and there(b, AHEAD_V):
                                dve_vf(dve, b + AHEAD_V)
                        turns(dve, slot, ch, lambda g: Chain(dve, a_dve, before + per_batch * GB * g))
        with ExitStack() as part:
            def sbp(name, shape, dt=fp32):
                return sb(name, shape, dt, part)

            def semp(name):
                return sem(name, part)

            at_one = []

            def primed(name):
                at_one.append(semp(name))
                return at_one[-1]

            LT = sbp("LT", [P, GT])
            L = sbp("L", [P, B, NE])
            LX = sbp("LX", [P, B, NE])
            mxl = sbp("mxl", [P, B])
            sml = sbp("sml", [P, B])
            gate = sbp("gate", [P, B])
            rev = sbp("rev", [P, B, NE], mybir.dt.int32)
            revf = sbp("revf", [P, B, NE])
            tok = sbp("tok", [P, B], mybir.dt.int32)
            tokf = sbp("tokf", [P, B])
            key = sbp("key", [P, B, NE])
            kmax = sbp("kmax", [P, B])
            OH = sbp("OH", [P, B, NE])
            OHB = sbp("OHB", [P, NE, B], bf16)
            tri = sbp("tri", [P, P], bf16)
            ones = sbp("ones", [P, P], bf16)
            carry = sbp("carry", [P, NE, B])
            INC = sbp("INC", [P, NE, B])
            TOT = sbp("TOT", [P, NE, B])
            POS = sbp("POS", [P, NE, B])
            pos = sbp("pos", [P, B])
            keepm = sbp("keepm", [P, B])
            flat = sbp("flat", [P, B])
            flat_u = sbp("flat_u", [P, B], u32)
            TH = sbp("THs", [P, NH, GT])
            H1 = sbp("H1s", [P, NH, GT])
            HS = sbp("HS", [P, NH, GT])
            WE1 = sbp("WE1", [P, 2, 2, EH])
            WE3 = sbp("WE3", [P, 2, 2, EH])
            WE2 = sbp("WE2", [P, 2, NH, C])
            XD = sbp("XD", [P, 2, 2, C + 1])
            to_u = sbp("to_u", [P, 2, 2], u32)
            XT = sbp("XT", [P, 2, 2, CAP])
            HE = sbp("HE", [P, NH, CAP])
            OE = sbp("OE", [P, 2, 2, C])
            GT_ = sbp("GT_", [P, B, C])

            m_pool = semp("m_pool")
            m_dve = semp("m_dve")
            m_lg = semp("m_lg")
            m_lt = semp("m_lt")
            m_lb = semp("m_lb")
            m_lx = semp("m_lx")
            m_ex = semp("m_ex")
            m_oh = semp("m_oh")
            m_cum = semp("m_cum")
            m_flat = semp("m_flat")
            m_scat = semp("m_scat")
            m_gu = semp("m_gu")
            m_th = semp("m_th")
            m_h = semp("m_h")
            m_dn = primed("m_dn")
            m_xs = primed("m_xs")
            e_w = [semp(f"e_w{s}") for s in range(2)]
            e_xd = [semp(f"e_xd{s}") for s in range(2)]
            e_xT = semp("e_xT")
            e_xt = semp("e_xt")
            e_gu = semp("e_gu")
            e_th = semp("e_th")
            e_h = semp("e_h")
            e_dn = primed("e_dn")
            e_oe = primed("e_oe")
            e_sc = [semp(f"e_sc{s}") for s in range(2)]
            e_done = semp("e_done")
            m_id = semp("m_id")
            m_gath = [semp(f"m_gath{g}") for g in range(NG)]
            m_out = semp("m_out")
            m_stored = semp("m_stored")

            flat2 = lambda t: t[:, :, :].rearrange("p a b -> p (a b)")

            with nc.Block() as block:
                @block.sync
                def _(sp):
                    for primed_sem in at_one:
                        sp.sem_inc(primed_sem, 1)
                    def load_w13(e, s):
                        for dst, src in ((WE1[:, s, :, :], W1), (WE3[:, s, :, :], W3)):
                            sp.dma_start(dst, src[bass.ds(e, 1), :, :].rearrange("e (h p) i -> p (e h) i", p=P))\
                              .then_inc(e_w[s], 16)

                    def load_w2(e, s):
                        sp.dma_start(WE2[:, s, 0:2, :], W2[bass.ds(e, 1), 0:2 * P, :]
                                     .rearrange("e (i p) c -> p (e i) c", p=P)).then_inc(e_w[s], 16)
                        sp.dma_start(WE2[0:EH - 2 * P, s, 2, :], W2[bass.ds(e, 1), 2 * P:EH, :]
                                     .rearrange("e p c -> (e p) c")).then_inc(e_w[s], 16)

                    def load_tokens(e, s):
                        sp.dma_start(XD[:, s, :, :], dispatched[bass.ds(CAP * e, CAP), :]
                                     .rearrange("(a p) c -> p a c", p=P)).then_inc(e_xd[s], 16)

                    for s in range(2):
                        load_w13(s, s)
                        load_w2(s, s)
                    sp.wait_ge(m_scat, 16 * B)
                    for s in range(2):
                        load_tokens(s, s)

                    with sp.Fori(0, NE // 2 - 1) as e2:
                        for s in range(2):
                            e = 2 * e2 + s
                            sp.wait_ge(e_xT, e + 1)
                            alone(sp)
                            sp.wait_ge(m_id, 1 + e + 1)
                            alone(sp)
                            load_tokens(e + 2, s)
                            sp.wait_ge(e_gu, NH * e + NH)
                            alone(sp)
                            load_w13(e + 2, s)
                            sp.wait_ge(e_dn, 1 + e + 1)
                            alone(sp)
                            load_w2(e + 2, s)
                    for s in range(2):
                        sp.wait_ge(e_sc[s], 2 * 16 * (NE // 2))
                    for g in range(NG):
                        sp.dma_start(GT_[:, GB * g:GB * (g + 1), :],
                                     combined[1 + GT * g:1 + GT * (g + 1), :].rearrange("(b p) c -> p b c", p=P))\
                          .then_inc(m_gath[g], 16)
                    for g in range(NG):
                        sp.wait_ge(m_out, GB * g + GB)
                        sp.dma_start(ot[:, GB * g:GB * (g + 1), :], X[:, GB * g:GB * (g + 1), :]).then_inc(m_stored, 16)
                    sp.wait_ge(m_stored, 16 * NG)

                @block.gpsimd
                def _(pool):
                    pool.sem_inc(e_done, 2)
                    pool.memset(ones[:], 1.0).then_inc(m_pool, 1)
                    pool.memset(tri[:], 1.0).then_inc(m_pool, 1)
                    pool.memset(carry[:, :, 0:1], 0.0).then_inc(m_pool, 1)
                    pool.memset(carry[:, :, 1:B], 1.0).then_inc(m_pool, 1)
                    pool.iota(rev[:], pattern=[[0, B], [-1, NE]], base=NE, channel_multiplier=0).then_inc(m_pool, 1)
                    pool.iota(tok[:], pattern=[[P, B]], base=SLOTS, channel_multiplier=1).then_inc(m_pool, 1)
                    pool.wait_ge(m_pool, 6)
                    pool.tensor_copy(revf[:], rev[:]).then_inc(m_pool, 1)
                    pool.tensor_copy(tokf[:], tok[:]).then_inc(m_pool, 1)
                    pool.affine_select(out=tri[:], in_=tri[:], compare_op=ALU.is_gt, fill=0.0, base=0,
                                       pattern=[[1, P]], channel_multiplier=-1).then_inc(m_pool, 1)
                    pool_power4(pool, NG - 1)
                    pool.wait_ge(m_flat, 1)
                    pool.wait_ge(m_id, 1)
                    for t in range(B):
                        pool.indirect_dma_start(out=dispatched, out_offset=bass.IndirectOffsetOnAxis(ap=flat_u[:, t:t + 1], axis=0),
                                                in_=Z4[:, t, :], in_offset=None).then_inc(m_scat, 16)
                    with pool.Fori(0, NE // 2) as e2:
                        for s in range(2):
                            pool.wait_ge(e_oe, 1 + 2 * e2 + s + 1)
                            alone(pool)
                            for a in range(2):
                                pool.indirect_dma_start(out=combined, out_offset=bass.IndirectOffsetOnAxis(ap=to_u[:, s, a:a + 1], axis=0),
                                                        in_=OE[:, s, a, :], in_offset=None).then_inc(e_sc[s], 16)
                            pool.wait_ge(e_sc[s], 2 * 16 * (e2 + 1))
                            pool.sem_inc(e_done, 1)

                @block.scalar
                def _(act):
                    def tanh_shared(g, i, first=False):
                        m = width(i, EH)
                        act.wait_ge(m_gu, NH * g + i + 1)
                        if not first:
                            act.wait_ge(m_h, NH * (g - 1) + i + 1)
                        act.activation(TH[0:m, i, :], bank[2 * i][0:m, :], ACT.Tanh, scale=0.5).then_inc(m_th, 1)

                    tanh_shared(0, 0, first=True)
                    tanh_shared(0, 1, first=True)
                    act.wait_ge(m_lg, 1)
                    act.activation(LT[:], bank[6], ACT.Copy).then_inc(m_lt, 1)
                    act.wait_ge(m_lx, 1)
                    act.activation(flat2(LX), flat2(LX), ACT.Exp).then_inc(m_ex, 1)
                    tanh_shared(0, 2, first=True)
                    with act.Fori(1, NG) as g:
                        for i in range(NH):
                            tanh_shared(g, i)

                    def turn_tokens(e, s):
                        act.wait_ge(e_xT, e + 1)
                        act.activation(XT[:, s, :, :].rearrange("p h t -> p (h t)"), bank[4], ACT.Copy).then_inc(e_xt, 1)

                    def tanh_expert(e, i, first=False):
                        m = width(i, EH)
                        act.wait_ge(e_gu, NH * e + i + 1)
                        if not first:
                            act.wait_ge(e_h, NH * (e - 1) + i + 1)
                        act.activation(TH[0:m, i, 0:CAP], bank[i][0:m, 0:CAP], ACT.Tanh, scale=0.5).then_inc(e_th, 1)

                    def result(e2, s):
                        e = 2 * e2 + s
                        act.wait_ge(e_dn, 1 + e + 1)
                        act.wait_ge(e_done, e + 1)
                        act.activation(OE[:, s, :, :].rearrange("p a c -> p (a c)"), bank[6], ACT.Copy).then_inc(e_oe, 1)

                    act.wait_ge(m_h, NH * NG)
                    turn_tokens(0, 0)
                    for i in range(NH):
                        tanh_expert(0, i, first=True)

                    turn_tokens(1, 1)

                    def step(e2, s, last=False):
                        e = 2 * e2 + s
                        tanh_expert(e + 1, 0)
                        result(e2, s)
                        tanh_expert(e + 1, 1)
                        if not last:
                            turn_tokens(e + 2, s)
                        tanh_expert(e + 1, 2)

                    with act.Fori(0, NE // 2 - 1) as e2:
                        for s in range(2):
                            step(e2, s)
                    step(NE // 2 - 1, 0, last=True)
                    result(NE // 2 - 1, 1)

                @block.tensor
                def _(pe):
                    def gu_shared(g, i, side, first=False):
                        m = width(i, EH)
                        if not first and side == 0:
                            pe.wait_ge(m_h, NH * (g - 1) + i + 1)
                        for h in range(2):
                            last = pe.matmul(bank[2 * i + side][0:m, :], (wsh1, wsh3)[side][:, h, i * P:i * P + m],
                                             ZT4[:, h, bass.ds(GT * g, GT)], start=(h == 0), stop=(h == 1))
                        if side == 1:
                            last.then_inc(m_gu, 1)

                    def down_shared(g):
                        pe.wait_ge(m_xs, 1 + 2 * g)
                        for k in range(2):
                            for b in range(2):
                                t = 2 * k + b
                                for i in range(NH):
                                    if t == 0 and i in (0, NH - 1):
                                        pe.wait_ge(m_h, NH * g + (NH - 1 if i == 0 else NH))
                                    m = width(i, EH)
                                    last = pe.matmul(bank[6 + k][:, b * C:(b + 1) * C], HS[0:m, i, t * P:(t + 1) * P],
                                                     wsh2[0:m, i, :], start=(i == 0), stop=(i == NH - 1))
                            last.then_inc(m_dn, 1)

                    for side in range(2):
                        gu_shared(0, 0, side, first=True)
                    for h in range(2):
                        pe_turn4(pe, NG - 1, h, bank[6 + h])
                    for side in range(2):
                        gu_shared(0, 1, side, first=True)
                    pe.wait_ge(m_zt, 2 * NG)
                    for h in range(2):
                        for g in range(NG):
                            last = pe.matmul(bank[6][32 * g:32 * g + 32, :], wgt[:, h, :], ZT4[:, h, GT * g:GT * (g + 1)],
                                             start=(h == 0), stop=(h == 1))
                    last.then_inc(m_lg, 1)
                    gu_shared(0, 2, 0, first=True)
                    pe.wait_ge(m_lt, 1)
                    for b in range(GB):
                        last = pe.transpose(bank[7][:, b * P:(b + 1) * P], LT[:, b * P:(b + 1) * P], ident[:])
                    last.then_inc(m_lb, 1)
                    gu_shared(0, 2, 1, first=True)
                    pe.wait_ge(m_oh, 1)
                    pe.wait_ge(m_pool, 9)
                    pe.matmul(bank[6][:, 0:NE * B], tri[:], flat2(OHB), start=True, stop=True)
                    pe.matmul(bank[6][:, NE * B:2 * NE * B], ones[:], flat2(OHB), start=True, stop=True).then_inc(m_cum, 1)
                    with pe.Fori(0, NG - 1) as g:
                        for side in range(2):
                            gu_shared(g + 1, 0, side)
                        pe.wait_ge(m_flat, 1)
                        down_shared(g)
                        for i in range(1, NH):
                            for side in range(2):
                                gu_shared(g + 1, i, side)
                    down_shared(NG - 1)

                    def turn_tokens(e2, s):
                        e = 2 * e2 + s
                        pe.wait_ge(e_xd[s], 16 * (e2 + 1))
                        if not isinstance(e, int) or e > 0:
                            pe.wait_ge(e_xt, e)
                        for h in range(2):
                            for a in range(2):
                                last = pe.transpose(bank[4][:, h * CAP + a * P:h * CAP + (a + 1) * P],
                                                    XD[:, s, a, h * P:(h + 1) * P], ident[:])
                        last.then_inc(e_xT, 1)

                    def gu_expert(e2, s, i, first=False):
                        e = 2 * e2 + s
                        m = width(i, EH)
                        if i == 0:
                            pe.wait_ge(e_xt, e + 1)
                            pe.wait_ge(e_w[s], 64 * (e2 + 1))
                        if not first:
                            pe.wait_ge(e_h, NH * (e - 1) + i + 1)
                        for w, lo in ((WE1, 0), (WE3, CAP)):
                            for h in range(2):
                                last = pe.matmul(bank[i][0:m, lo:lo + CAP], w[:, s, h, i * P:i * P + m],
                                                 XT[:, s, h, :], start=(h == 0), stop=(h == 1))
                        last.then_inc(e_gu, 1)

                    def down_expert(e, s):
                        pe.wait_ge(e_oe, 1 + e)
                        for a in range(2):
                            for i in range(NH):
                                if a == 0 and i in (0, NH - 1):
                                    pe.wait_ge(e_h, NH * e + (NH - 1 if i == 0 else NH))
                                m = width(i, EH)
                                last = pe.matmul(bank[6][:, a * C:(a + 1) * C], HE[0:m, i, a * P:(a + 1) * P],
                                                 WE2[0:m, s, i, :], start=(i == 0), stop=(i == NH - 1))
                        last.then_inc(e_dn, 1)

                    turn_tokens(0, 0)
                    for i in range(NH):
                        gu_expert(0, 0, i, first=True)
                    turn_tokens(0, 1)
                    pe.wait_ge(m_xs, 1 + 2 * NG)

                    def step(e2, s, last=False):
                        e = 2 * e2 + s
                        ahead = (e2 + (s + 1) // 2, (s + 1) % 2)
                        gu_expert(*ahead, 0)
                        down_expert(e, s)
                        gu_expert(*ahead, 1)
                        if not last:
                            turn_tokens(e2 + 1, s)
                        gu_expert(*ahead, 2)

                    with pe.Fori(0, NE // 2 - 1) as e2:
                        for s in range(2):
                            step(e2, s)
                    step(NE // 2 - 1, 0, last=True)
                    down_expert(NE - 1, 1)

                @block.vector
                def _(dve):
                    ch = Chain(dve, m_dve)

                    def hidden_shared(ch, g, i):
                        m = width(i, EH)
                        dve.wait_ge(m_th, NH * g + i + 1)
                        ch.do(dve.scalar_tensor_tensor(out=H1[0:m, i, :], in0=TH[0:m, i, :], scalar=1.0,
                                                       in1=bank[2 * i][0:m, :], op0=ALU.add, op1=ALU.mult))
                        ch.wait()
                        dve.scalar_tensor_tensor(out=HS[0:m, i, :], in0=H1[0:m, i, :], scalar=0.5,
                                                 in1=bank[2 * i + 1][0:m, :], op0=ALU.mult, op1=ALU.mult).then_inc(m_h, 1)

                    dve_statistics(Chain(dve, m_ln, (NG - 1) * 2 * GB), NG - 1)
                    dve_normalise(dve, NG - 1)
                    hidden_shared(ch, 0, 0)
                    for h in range(2):
                        dve_turn4(dve, NG - 1, h, bank[6 + h])
                    hidden_shared(ch, 0, 1)
                    dve.wait_ge(m_pool, 9)
                    dve.tensor_scalar(Z4[:, :, C], tokf[:], float(1 - SLOTS), None, ALU.add).then_inc(m_id, 1)
                    over_e = lambda v: v[:, :].unsqueeze(2).broadcast_to([P, B, NE])
                    dve.wait_ge(m_lb, 1)
                    ch.do(dve.tensor_copy(L[:, :, :].rearrange("p (g b) e -> p b g e", g=NG),
                                          bank[7].rearrange("p (b g c) -> p b g c", b=GB, g=NG)[:, :, :, 0:NE]))
                    ch.wait()
                    ch.do(dve.tensor_reduce(mxl[:], L[:], axis=AX.X, op=ALU.max))
                    ch.wait()
                    dve.tensor_tensor(LX[:], L[:], over_e(mxl), ALU.subtract).then_inc(m_lx, 1)
                    ch.do(dve.tensor_tensor(key[:], L[:], over_e(mxl), ALU.is_equal))
                    ch.wait()
                    dve.wait_ge(m_pool, 9)
                    ch.do(dve.tensor_tensor(key[:], key[:], revf[:], ALU.mult))
                    ch.wait()
                    ch.do(dve.tensor_reduce(kmax[:], key[:], axis=AX.X, op=ALU.max))
                    ch.wait()
                    ch.do(dve.tensor_tensor(OH[:], key[:], over_e(kmax), ALU.is_equal))
                    ch.wait()
                    dve.tensor_copy(OHB[:].rearrange("p e b -> p b e"), OH[:]).then_inc(m_oh, 1)
                    dve.wait_ge(m_ex, 1)
                    ch.do(dve.tensor_reduce(sml[:], LX[:], axis=AX.X, op=ALU.add))
                    ch.wait()
                    ch.do(dve.reciprocal(gate[:], sml[:]))
                    dve.wait_ge(m_cum, 1)
                    ch.do(dve.tensor_copy(flat2(TOT), bank[6][:, NE * B:2 * NE * B]))
                    ch.wait()
                    ch.do(dve.tensor_tensor_scan(out=flat2(INC), data0=flat2(carry), data1=flat2(TOT), initial=0.0,
                                                 op0=ALU.mult, op1=ALU.add))
                    ch.wait()
                    ch.do(dve.tensor_tensor(flat2(POS), flat2(INC), flat2(TOT), ALU.subtract))
                    ch.wait()
                    ch.do(dve.tensor_tensor(flat2(POS), flat2(POS), bank[6][:, 0:NE * B], ALU.add))
                    ch.wait()
                    ch.do(dve.tensor_tensor(key[:], OH[:], POS[:].rearrange("p e b -> p b e"), ALU.mult))
                    ch.wait()
                    ch.do(dve.tensor_reduce(pos[:], key[:], axis=AX.X, op=ALU.add))
                    ch.wait()
                    ch.do(dve.tensor_scalar(keepm[:], pos[:], float(CAP), None, ALU.is_lt))
                    ch.do(dve.tensor_scalar(flat[:], kmax[:], -float(CAP), float(SLOTS), ALU.mult, ALU.add))
                    ch.wait()
                    ch.do(dve.tensor_tensor(flat[:], flat[:], pos[:], ALU.add))
                    ch.wait()
                    ch.do(dve.tensor_tensor(flat[:], flat[:], tokf[:], ALU.subtract))
                    ch.wait()
                    ch.do(dve.tensor_tensor(flat[:], flat[:], keepm[:], ALU.mult))
                    ch.wait()
                    ch.do(dve.tensor_tensor(flat[:], flat[:], tokf[:], ALU.add))
                    ch.wait()
                    dve.tensor_copy(flat_u[:], flat[:]).then_inc(m_flat, 1)
                    ch.do(dve.tensor_tensor(gate[:], gate[:], keepm[:], ALU.mult))
                    ch.wait()
                    dve.tensor_scalar(gate[:], gate[:], tg[:, 3:4], None, ALU.mult).then_inc(m_flat, 1)
                    def add_shared(g):
                        for k in range(2):
                            dve.wait_ge(m_dn, 1 + 2 * g + k + 1)
                            xs = X[:, bass.ds(GB * g + 2 * k, 2), :].rearrange("p b c -> p (b c)")
                            dve.scalar_tensor_tensor(out=xs, in0=bank[6 + k], scalar=tg[:, 3:4], in1=xs,
                                                     op0=ALU.mult, op1=ALU.add).then_inc(m_xs, 1)

                    hidden_shared(ch, 0, 2)
                    before = ch.n
                    with dve.Fori(0, NG - 1) as g:
                        ch = Chain(dve, m_dve, before + NH * g)
                        add_shared(g)
                        for i in range(NH):
                            hidden_shared(ch, g + 1, i)
                    add_shared(NG - 1)
                    before += NH * (NG - 1)

                    def hidden_expert(ch, e, i):
                        m = width(i, EH)
                        dve.wait_ge(e_th, NH * e + i + 1)
                        ch.do(dve.scalar_tensor_tensor(out=H1[0:m, i, 0:CAP], in0=TH[0:m, i, 0:CAP], scalar=1.0,
                                                       in1=bank[i][0:m, 0:CAP], op0=ALU.add, op1=ALU.mult))
                        if i == 0:
                            dve.wait_ge(e_dn, 1 + e)
                        ch.wait()
                        dve.scalar_tensor_tensor(out=HE[0:m, i, :], in0=H1[0:m, i, 0:CAP], scalar=0.5,
                                                 in1=bank[i][0:m, CAP:2 * CAP], op0=ALU.mult, op1=ALU.mult).then_inc(e_h, 1)

                    with dve.Fori(0, NE // 2) as e2:
                        ch = Chain(dve, m_dve, before + 2 * NH * e2)
                        for s in range(2):
                            dve.wait_ge(e_xd[s], 16 * (e2 + 1))
                            dve.wait_ge(e_done, 2 * e2 + s + 1)
                            dve.tensor_copy(to_u[:, s, :], XD[:, s, :, C]).then_inc(m_id, 1)
                            for i in range(NH):
                                hidden_expert(ch, 2 * e2 + s, i)
                    dve.wait_ge(m_xs, 1 + 2 * NG)
                    dve.wait_ge(m_flat, 2)
                    for t in range(B):
                        dve.wait_ge(m_gath[t // GB], 16)
                        dve.scalar_tensor_tensor(out=X[:, t, :], in0=GT_[:, t, :], scalar=gate[:, t:t + 1], in1=X[:, t, :],
                                                 op0=ALU.mult, op1=ALU.add).then_inc(m_out, 1)


def kernel(**inputs):
    import numpy as _np
    import concourse.bacc as _bacc
    from concourse import mybir as _mybir
    from concourse.bass_utils import run_bass_kernel_spmd as _run

    a = {k: _np.asarray(v) for k, v in inputs.items()}
    column = lambda v: v.reshape(-1, P).T
    by_dim = _np.arange(P).reshape(HEADS, HD).T.reshape(-1)
    laid = {
        "x": a["x"], "ctx": a["ctx_2048"], "mask": a["mask_Bx1x2048_fk1"].reshape(B, T),
        "g_xattn": a["g_xattn"], "g_ffn": a["g_ffn"],
        "time_decay": column(a["L0_xattn_time_decay"]), "time_first": column(a["L0_xattn_time_first"]),
        "gate_wT": a["L0_ffn_gate_w"].T, "up_wT": a["L0_ffn_up_w"].T, "down_wT": a["L0_ffn_down_w"].T,
        "gate_s": a["L0_ffn_gate_s"], "up_s": a["L0_ffn_up_s"], "down_s": a["L0_ffn_down_s"],
        "wqT": a["L1_xattn_Wq"][by_dim].T, "bq": column(a["L1_xattn_bq"][by_dim]),
        "wkT": a["L1_xattn_Wk"][by_dim].T, "bk": column(a["L1_xattn_bk"][by_dim]),
        "wvT": a["L1_xattn_Wv"].T, "bv": a["L1_xattn_bv"],
        "Wg": a["L1_ffn_Wg"], "W1": a["L1_ffn_W1"], "W3": a["L1_ffn_W3"], "W2": a["L1_ffn_W2"],
        "sw1": a["L1_ffn_sw1"], "sw3": a["L1_ffn_sw3"], "sw2": a["L1_ffn_sw2"],
    }
    nc = _bacc.Bacc("TRN2", target_bir_lowering=False, num_devices=1)
    arrays, args = {}, []
    for name, v in laid.items():
        arrays[f"in_{name}"] = _np.ascontiguousarray(v)
        args.append(nc.dram_tensor(f"in_{name}", v.shape, _mybir.dt.from_np(v.dtype), kind="ExternalInput").ap())
    args.append(nc.dram_tensor("out_x", (B, P, C), fp32, kind="ExternalOutput").ap())
    flamingo_kernel(nc, *args)
    r = _run(nc, [arrays], core_ids=[0])
    return r.results[0]["out_x"]
```
